# Optimizing a Trainium2 kernel written in Bass

```python
import numpy as np
import jax
import jax.numpy as jnp

def _softmax(x, axis=-1):
    return jax.nn.softmax(x, axis=axis)

def _gelu(x):
    return jax.nn.gelu(x, approximate=True)

def _silu(x):
    return jax.nn.silu(x)

def _sigmoid(x):
    return jax.nn.sigmoid(x)

def _layernorm(x, axis=-1, eps=1e-05):
    m = jnp.mean(x, axis=axis, keepdims=True)
    v = jnp.var(x, axis=axis, keepdims=True)
    return (x - m) / jnp.sqrt(v + eps)

def _scatter_add(tgt, idx, src, axis=0):
    return tgt.at[idx].add(src)

def _segment_sum(src, seg, n):
    return jax.ops.segment_sum(src, seg, n)
kernel_name = 'mk_decoder_postln_d1_seqx_r8_e80d7c'

def setup_inputs(seed: int=0):
    np.random.seed(seed)
    _w = jnp.asarray

    def _rec_inputs():
        import jax
        import jax.numpy as jnp
        _rk = jax.random.key(seed)
        x = -9.806e-05 + 1 * jax.random.normal(jax.random.fold_in(_rk, 1), (8, 256, 128), jnp.float32)
        _lenS = 256 - jax.random.randint(jax.random.fold_in(_rk, 7), (8,), 0, max(1, 256 // 4) + 1, jnp.int32)
        _lenS2 = 256 - jax.random.randint(jax.random.fold_in(_rk, 8), (8,), 0, max(1, 256 // 4) + 1, jnp.int32)
        _ctx_1024P = jax.random.normal(jax.random.fold_in(_rk, 11), (8, 16, 128), jnp.float32)
        _ctx_1024c = jax.random.dirichlet(jax.random.fold_in(_rk, 511), 0.3 * jnp.ones((16,), jnp.float32), (8, 256))
        _ctx_1024t = jnp.einsum('bsk,bkd->bsd', _ctx_1024c, _ctx_1024P)
        _ctx_1024t = _ctx_1024t * jax.lax.rsqrt(jnp.mean(jnp.square(_ctx_1024t)) + 1e-12) * 0.953939
        ctx_1024 = -1.52775e-05 + 0.999936 * (_ctx_1024t + 0.3 * jax.random.normal(jax.random.fold_in(_rk, 611), (8, 256, 128), jnp.float32))
        return (x, ctx_1024)
    x, ctx_1024 = _rec_inputs()

    def _L0_attn_setup():
        import jax, jax.numpy as jnp
        import numpy as np
        SEQ, BATCH, HIDDEN = (256, 2, 128)
        NUM_HEADS, HEAD_DIM = (16, 64)
        LN_EPS = 1e-06
        NEG_INF = -10000000000.0
        key = jax.random.key(seed)
        k1, k2, k3 = jax.random.split(key, 3)
        inputs_q = jax.random.normal(k1, (SEQ, BATCH, HIDDEN), dtype=jnp.float32)
        ln_scale = jnp.ones((HIDDEN,), dtype=jnp.float32)
        ln_bias = jnp.zeros((HIDDEN,), dtype=jnp.float32)
        qkv_kernel = jax.random.normal(k2, (HIDDEN, 3, NUM_HEADS * HEAD_DIM), dtype=jnp.float32) / np.sqrt(HIDDEN).astype(np.float32)
        out_kernel = jax.random.normal(k3, (NUM_HEADS * HEAD_DIM, HIDDEN), dtype=jnp.float32) / np.sqrt(NUM_HEADS * HEAD_DIM).astype(np.float32)
        return {'inputs_q': inputs_q, 'ln_scale': ln_scale, 'ln_bias': ln_bias, 'qkv_kernel': qkv_kernel, 'out_kernel': out_kernel}
    _L0_attn_all = _L0_attn_setup()
    _L0_attn_in = {k: v for k, v in _L0_attn_all.items() if k in ('ln_scale', 'ln_bias', 'qkv_kernel', 'out_kernel')}
    del _L0_attn_all

    def _L0_xattn_setup():
        import jax, jax.numpy as jnp
        import numpy as np
        D = 128
        NUM_ITERS = 3
        EPS = 1e-06
        SCALE = D ** (-0.5)

        def rmsnorm(x, w, eps=EPS):
            return x * jax.lax.rsqrt(jnp.mean(x * x, axis=-1, keepdims=True) + eps) * w

        def gru_cell(x, h, wih, whh, bih, bhh):
            gx = x @ wih.T + bih
            gh = h @ whh.T + bhh
            xr, xz, xn = jnp.split(gx, 3, axis=-1)
            hr, hz, hn = jnp.split(gh, 3, axis=-1)
            r = jax.nn.sigmoid(xr + hr)
            z = jax.nn.sigmoid(xz + hz)
            n = jnp.tanh(xn + r * hn)
            return (1.0 - z) * n + z * h
        key = jax.random.key(seed)
        ks = jax.random.split(key, 8)
        B, K, M, d = (8, 64, 512, D)
        w_std = d ** (-0.5)
        return {'slots': jax.random.normal(ks[0], (B, K, d), jnp.float32), 'P': jax.random.normal(ks[1], (B, M, d), jnp.float32), 'Wq': jax.random.normal(ks[2], (d, d), jnp.float32) * w_std, 'Wk': jax.random.normal(ks[3], (d, d), jnp.float32) * w_std, 'Wv': jax.random.normal(ks[4], (d, d), jnp.float32) * w_std, 'gru_wih': jax.random.normal(ks[5], (3 * d, d), jnp.float32) * w_std, 'gru_whh': jax.random.normal(ks[6], (3 * d, d), jnp.float32) * w_std, 'gru_bih': jnp.zeros((3 * d,), jnp.float32), 'gru_bhh': jnp.zeros((3 * d,), jnp.float32), 'slot_norm_w': jnp.ones((d,), jnp.float32), 'input_norm_w': jnp.ones((d,), jnp.float32)}
    _L0_xattn_all = _L0_xattn_setup()
    _L0_xattn_in = {k: v for k, v in _L0_xattn_all.items() if k in ('Wq', 'Wk', 'Wv', 'gru_wih', 'gru_whh', 'gru_bih', 'gru_bhh', 'slot_norm_w', 'input_norm_w')}
    del _L0_xattn_all

    def _L0_ffn_setup():
        import jax, jax.numpy as jnp
        import numpy as np
        N_EXP = 8
        TOP_K = 2
        CAP_FACTOR = 1.25
        NEG_INF = -1000000000.0

        def _moe_forward(x, w_g, c_fc, c_proj):
            B, T, D = x.shape
            N = B * T
            xf = x.reshape(N, D)
            logits = xf @ w_g
            topv, topi = jax.lax.top_k(logits, TOP_K)
            full = jnp.full_like(logits, NEG_INF)
            full = full.at[jnp.arange(N)[:, None], topi].set(topv)
            probs = jax.nn.softmax(full, axis=-1)
            capacity = int(TOP_K * CAP_FACTOR * N / N_EXP)
            capacity += capacity % 2
            mask = jax.nn.one_hot(jnp.swapaxes(topi, 0, 1), N_EXP, dtype=jnp.int32)
            rank = jnp.cumsum(mask.reshape(TOP_K * N, N_EXP), axis=0).reshape(TOP_K, N, N_EXP) - 1
            mask = mask * (rank < capacity)
            rank_sel = jnp.sum(mask * rank, axis=-1)
            wts = jnp.sum(mask * probs[None], axis=-1)
            cb = jnp.zeros((N, N_EXP, capacity), x.dtype)
            tok = jnp.arange(N)
            for k in range(TOP_K):
                cb = cb.at[tok, topi[:, k], rank_sel[k]].add(wts[k])
            sec_mask = (cb != 0).astype(x.dtype)
            exp_batches = jnp.einsum('nec,nd->ecd', sec_mask, xf)
            h = jax.nn.gelu(jnp.einsum('ecd,edh->ech', exp_batches, c_fc), approximate=False)
            exp_out = jnp.einsum('ech,ehd->ecd', h, c_proj)
            out = jnp.einsum('nec,ecd->nd', cb, exp_out)
            return out.reshape(B, T, D)
        key = jax.random.key(seed)
        k1, k2, k3, k4 = jax.random.split(key, 4)
        B, T, D = (4, 64, 128)
        H = 4 * D
        x = jax.random.normal(k1, (B, T, D), jnp.float32)
        w_g = jax.random.normal(k2, (D, N_EXP), jnp.float32) * 0.02
        c_fc = jax.random.normal(k3, (N_EXP, D, H), jnp.float32) * 0.02
        c_proj = jax.random.normal(k4, (N_EXP, H, D), jnp.float32) * 0.02
        return {'x': x, 'w_g': w_g, 'c_fc': c_fc, 'c_proj': c_proj}
    _L0_ffn_all = _L0_ffn_setup()
    _L0_ffn_in = {k: v for k, v in _L0_ffn_all.items() if k in ('w_g', 'c_fc', 'c_proj')}
    del _L0_ffn_all
    return {'x': x, 'ctx_1024': ctx_1024, 'L0_attn_ln_scale': _L0_attn_in['ln_scale'], 'L0_attn_ln_bias': _L0_attn_in['ln_bias'], 'L0_attn_qkv_kernel': _L0_attn_in['qkv_kernel'], 'L0_attn_out_kernel': _L0_attn_in['out_kernel'], 'L0_xattn_Wq': _L0_xattn_in['Wq'], 'L0_xattn_Wk': _L0_xattn_in['Wk'], 'L0_xattn_Wv': _L0_xattn_in['Wv'], 'L0_xattn_gru_wih': _L0_xattn_in['gru_wih'], 'L0_xattn_gru_whh': _L0_xattn_in['gru_whh'], 'L0_xattn_gru_bih': _L0_xattn_in['gru_bih'], 'L0_xattn_gru_bhh': _L0_xattn_in['gru_bhh'], 'L0_xattn_slot_norm_w': _L0_xattn_in['slot_norm_w'], 'L0_xattn_input_norm_w': _L0_xattn_in['input_norm_w'], 'L0_ffn_w_g': _L0_ffn_in['w_g'], 'L0_ffn_c_fc': _L0_ffn_in['c_fc'], 'L0_ffn_c_proj': _L0_ffn_in['c_proj']}

def reference(x, ctx_1024, L0_attn_ln_scale, L0_attn_ln_bias, L0_attn_qkv_kernel, L0_attn_out_kernel, L0_xattn_Wq, L0_xattn_Wk, L0_xattn_Wv, L0_xattn_gru_wih, L0_xattn_gru_whh, L0_xattn_gru_bih, L0_xattn_gru_bhh, L0_xattn_slot_norm_w, L0_xattn_input_norm_w, L0_ffn_w_g, L0_ffn_c_fc, L0_ffn_c_proj):
    import jax
    import jax.numpy as jnp

    def _L0_attn_ref(inputs_q, ln_scale, ln_bias, qkv_kernel, out_kernel):
        import jax, jax.numpy as jnp
        import numpy as np
        SEQ, BATCH, HIDDEN = (256, 2, 128)
        NUM_HEADS, HEAD_DIM = (16, 64)
        LN_EPS = 1e-06
        NEG_INF = -10000000000.0
        s, b, h = inputs_q.shape
        mu = jnp.mean(inputs_q, axis=-1, keepdims=True)
        var = jnp.mean(jnp.square(inputs_q - mu), axis=-1, keepdims=True)
        ln_out = (inputs_q - mu) * jax.lax.rsqrt(var + LN_EPS) * ln_scale + ln_bias
        qkv = jnp.einsum('sbh,htk->stbk', ln_out, qkv_kernel)
        q = qkv[:, 0].reshape(s, b, NUM_HEADS, HEAD_DIM)
        k = qkv[:, 1].reshape(s, b, NUM_HEADS, HEAD_DIM)
        v = qkv[:, 2].reshape(s, b, NUM_HEADS, HEAD_DIM)
        scale = 1.0 / np.sqrt(HEAD_DIM).astype(np.float32)
        logits = jnp.einsum('qbhd,kbhd->bhqk', q, k) * scale
        causal = jnp.tril(jnp.ones((s, s), dtype=bool))
        logits = jnp.where(causal[None, None], logits, jnp.asarray(NEG_INF, logits.dtype))
        attn = jax.nn.softmax(logits, axis=-1)
        ctx = jnp.einsum('bhqk,kbhd->qbhd', attn, v).reshape(s, b, NUM_HEADS * HEAD_DIM)
        return jnp.einsum('sbk,kh->sbh', ctx, out_kernel)

    def _L0_xattn_ref(slots, P, Wq, Wk, Wv, gru_wih, gru_whh, gru_bih, gru_bhh, slot_norm_w, input_norm_w):
        import jax, jax.numpy as jnp
        import numpy as np
        D = 128
        NUM_ITERS = 3
        EPS = 1e-06
        SCALE = D ** (-0.5)

        def rmsnorm(x, w, eps=EPS):
            return x * jax.lax.rsqrt(jnp.mean(x * x, axis=-1, keepdims=True) + eps) * w

        def gru_cell(x, h, wih, whh, bih, bhh):
            gx = x @ wih.T + bih
            gh = h @ whh.T + bhh
            xr, xz, xn = jnp.split(gx, 3, axis=-1)
            hr, hz, hn = jnp.split(gh, 3, axis=-1)
            r = jax.nn.sigmoid(xr + hr)
            z = jax.nn.sigmoid(xz + hz)
            n = jnp.tanh(xn + r * hn)
            return (1.0 - z) * n + z * h
        Pn = rmsnorm(P, input_norm_w)
        k_proj = Pn @ Wk.T
        v_proj = Pn @ Wv.T
        for _ in range(NUM_ITERS):
            sn = rmsnorm(slots, slot_norm_w)
            q_proj = sn @ Wq.T
            scores = jnp.einsum('bkd,bmd->bkm', q_proj, k_proj) * SCALE
            attn = jax.nn.softmax(scores, axis=-2)
            attn = attn / (jnp.sum(attn, axis=-1, keepdims=True) + EPS)
            updates = jnp.einsum('bkm,bmd->bkd', attn, v_proj)
            slots = gru_cell(updates, slots, gru_wih, gru_whh, gru_bih, gru_bhh)
        return slots

    def _L0_ffn_ref(x, w_g, c_fc, c_proj):
        import jax, jax.numpy as jnp
        import numpy as np
        N_EXP = 8
        TOP_K = 2
        CAP_FACTOR = 1.25
        NEG_INF = -1000000000.0

        def _moe_forward(x, w_g, c_fc, c_proj):
            B, T, D = x.shape
            N = B * T
            xf = x.reshape(N, D)
            logits = xf @ w_g
            topv, topi = jax.lax.top_k(logits, TOP_K)
            full = jnp.full_like(logits, NEG_INF)
            full = full.at[jnp.arange(N)[:, None], topi].set(topv)
            probs = jax.nn.softmax(full, axis=-1)
            capacity = int(TOP_K * CAP_FACTOR * N / N_EXP)
            capacity += capacity % 2
            mask = jax.nn.one_hot(jnp.swapaxes(topi, 0, 1), N_EXP, dtype=jnp.int32)
            rank = jnp.cumsum(mask.reshape(TOP_K * N, N_EXP), axis=0).reshape(TOP_K, N, N_EXP) - 1
            mask = mask * (rank < capacity)
            rank_sel = jnp.sum(mask * rank, axis=-1)
            wts = jnp.sum(mask * probs[None], axis=-1)
            cb = jnp.zeros((N, N_EXP, capacity), x.dtype)
            tok = jnp.arange(N)
            for k in range(TOP_K):
                cb = cb.at[tok, topi[:, k], rank_sel[k]].add(wts[k])
            sec_mask = (cb != 0).astype(x.dtype)
            exp_batches = jnp.einsum('nec,nd->ecd', sec_mask, xf)
            h = jax.nn.gelu(jnp.einsum('ecd,edh->ech', exp_batches, c_fc), approximate=False)
            exp_out = jnp.einsum('ech,ehd->ecd', h, c_proj)
            out = jnp.einsum('nec,ecd->nd', cb, exp_out)
            return out.reshape(B, T, D)
        return _moe_forward(x, w_g, c_fc, c_proj)
    x = _layernorm(x + _L0_attn_ref(x, L0_attn_ln_scale, L0_attn_ln_bias, L0_attn_qkv_kernel, L0_attn_out_kernel), axis=-1)
    x = _layernorm(x + _L0_xattn_ref(x, ctx_1024, L0_xattn_Wq, L0_xattn_Wk, L0_xattn_Wv, L0_xattn_gru_wih, L0_xattn_gru_whh, L0_xattn_gru_bih, L0_xattn_gru_bhh, L0_xattn_slot_norm_w, L0_xattn_input_norm_w), axis=-1)
    x = _layernorm(x + _L0_ffn_ref(x, L0_ffn_w_g, L0_ffn_c_fc, L0_ffn_c_proj), axis=-1)
    return x

_drawn_inputs = setup_inputs


def setup_inputs(seed=0):
    import zlib

    import numpy as np

    out = dict(_drawn_inputs(seed))
    spreads = {'L0_attn_ln_scale': (1.0, 0.2),
     'L0_attn_ln_bias': (0.0, 0.1),
     'L0_xattn_gru_bih': (0.0, 0.1),
     'L0_xattn_gru_bhh': (0.0, 0.1),
     'L0_xattn_slot_norm_w': (1.0, 0.6),
     'L0_xattn_input_norm_w': (1.0, 0.2)}
    factors = {}
    for name, (base, spread) in spreads.items():
        noise = np.random.default_rng([zlib.crc32(name.encode()), seed]).standard_normal(out[name].shape)
        drawn = base * np.exp(spread * noise) if base else spread * noise
        out[name] = jnp.asarray(drawn.astype(out[name].dtype))
    for name, factor in factors.items():
        out[name] = (out[name] * factor).astype(out[name].dtype)
    return out
```

```python
from contextlib import ExitStack

import concourse.bass as bass
from concourse import mybir

F32 = mybir.dt.float32
BF16 = mybir.dt.bfloat16
I32 = mybir.dt.int32
U32 = mybir.dt.uint32
ALU = mybir.AluOpType
ACT = mybir.ActivationFunctionType
AX = mybir.AxisListType

P = 128
B8 = 8
S, B, D = 8, 256, 128
N = S * B
T = N // P
H, DH = 16, 64
HP = H // 2
SG = 4
GL = T // SG
QB = 32
ITERS = 3
E, TOPK, F = 8, 2, 512
CAP = int(TOPK * 1.25 * N / E)
CAP += CAP % 2
CT = CAP // P
NT = E * CT
FC = F // P
NOWHERE = 1 << 20
OFF = -1.0e30
NEG_INF = -1.0e9
LN_EPS, RMS_EPS, SUM_EPS, OUT_EPS = 1e-6, 1e-6, 1e-6, 1e-5


def build(nc, x, ctx_in, ln_scale, ln_bias, qkv_w, out_w, Wq, Wk, Wv, wih, whh, bih, bhh,
          slot_w, input_w, w_g, c_fc, c_proj, out):
    with ExitStack() as ctx:
        def sb(name, shape, dt=F32):
            return ctx.enter_context(nc.sbuf_tensor(name, shape, dt))

        def sem(name):
            return ctx.enter_context(nc.semaphore(name))

        ps = ctx.enter_context(nc.psum_tensor("ps", [P, 8, 512], F32))

        xg = sb("xg", [P, T, D])
        ctx_t = sb("ctx_t", [P, T, D])
        wqkv = sb("wqkv", [P, 3 * H * DH])
        wo = sb("wo", [P, HP, D])
        x1T = sb("x1T", [P, N])
        x1n = sb("x1n", [P, T, D])
        h = wqkv[:, 0:N].rearrange("p (t d) -> p t d", t=T)
        kq = sb("kq", [P, N])
        vp = sb("vp", [P, T, D])
        ident = sb("ident", [P, P])
        full_mask = sb("full_mask", [P, P])
        mask = sb("mask", [P, QB])
        ones_b = sb("ones_b", [P, P], BF16)
        before = sb("before", [P, P], BF16)
        zeros = sb("zeros", [P, 8 * D])
        lnv = sb("lnv", [P, 8])
        st = sb("st", [P, T, 6])
        mv = sb("mv", [P, T, 2])
        var = sb("var", [P, T])
        rs = sb("rs", [P, T])
        rt = sb("rt", [P, T])

        xn = sb("xn", [P, GL, D])
        lnT = sb("lnT", [P, GL * P])
        pool_a = sb("pool_a", [P, HP * 512])
        pool_k = sb("pool_k", [P, HP * GL * 2 * P])
        pool_v = sb("pool_v", [P, GL * H * DH])
        pool_p = sb("pool_p", [P, 2 * H * P])
        qT = pool_a[:, :].rearrange("p (h n) -> p h n", h=HP)
        kz = pool_k[:, :].rearrange("p (h g z n) -> p h g z n", h=HP, g=GL, z=2)
        v = pool_v[:, :].rearrange("p (g n) -> p g n", g=GL)
        pbd = pool_p[:, :].rearrange("p (r h n) -> p r h n", r=2, h=H)
        sc = sb("sc", [P, 2, H, QB])
        pc = sb("pc", [P, 2, H, QB])
        pt = sb("pt", [P, 2, H, QB])
        mx = sb("mx", [P, H])
        sm = sb("sm", [P, H])
        ctxT = sb("ctxT", [P, HP, P])

        w_nat = sb("w_nat", [P, 9, D])
        w_kq = sb("w_kq", [P, D])
        w_v = sb("w_v", [P, D])
        w_ih = sb("w_ih", [P, 3 * D])
        w_hh = sb("w_hh", [P, 3 * D])
        b_rows = sb("b_rows", [3, 2, 3 * D])
        b_sum = sb("b_sum", [3, 4 * D])
        b_part = sb("b_part", [3, 4 * D])
        b_cut = sb("b_cut", [3, 4 * D], BF16)
        bias = sb("bias", [P, 4 * D], BF16)
        wg = sb("wg", [P, E])
        cfc = sb("cfc", [P, 2, F])
        cpr = sb("cpr", [P, 2, FC, D])
        c_st = sb("c_st", [P, T, 6])
        c_mv = sb("c_mv", [P, T, 2])
        c_r = sb("c_r", [P, T])
        sq = sb("sq", [P, T])
        r_h = sb("r_h", [P, T])

        cT = pool_a[:, 0:N]
        snh = pool_a[:, N:N + 4 * 512].rearrange("p (r n) -> p r n", r=4)
        at = [0]

        def carve(pool, n):
            at[0] += n
            assert at[0] <= pool.shape[1], at[0]
            return pool[:, at[0] - n:at[0]]

        e_m = carve(pool_k, 1024).rearrange("p (r m k) -> p r m k", r=2, m=2)
        vr = carve(pool_k, 4 * (D + 1)).rearrange("p (r m d) -> p r m d", r=2, m=2)
        upd = carve(pool_k, 512).rearrange("p (r t d) -> p r t d", r=2, t=2)
        updT = carve(pool_k, 512).rearrange("p (r n) -> p r n", r=2)
        trz = carve(pool_k, 1024).rearrange("p (r t d) -> p r t d", r=2, t=2)
        new = carve(pool_k, 512).rearrange("p (r t d) -> p r t d", r=2, t=2)
        sn = carve(pool_k, 512).rearrange("p (r t d) -> p r t d", r=2, t=2)
        tmp = carve(pool_k, 256).rearrange("p (t d) -> p t d", t=2)
        tmp2 = carve(pool_k, 256).rearrange("p (t d) -> p t d", t=2)
        sq_out = carve(pool_k, 256)
        n_mx = sb("n_mx", [P, 2, 2])
        den = sb("den", [P, 2, 2])
        r_sum = sb("r_sum", [P, 2])

        x2 = pool_v[:, 0:T * D].rearrange("p (t c) -> p t c", t=T)
        hot_lo = pool_p[:, :].rearrange("p (q l) -> p q l", l=P)
        hot_hi = pool_a[:, :].rearrange("p (q l) -> p q l", l=P)
        at[0] = 0
        xe = carve(pool_k, 2 * CAP).rearrange("p (r j c) -> p r j c", r=2, j=CT)
        xeT = carve(pool_k, 2 * CAP).rearrange("p (r n) -> p r n", r=2)
        hT = carve(pool_k, 2 * FC * CAP).rearrange("p (r f n) -> p r f n", r=2, f=FC)
        eo = pool_a[:, 0:2 * CAP].rearrange("p (r j d) -> p r j d", r=2, j=CT)
        tile_hot = pool_v[:, T * D:T * D + TOPK * T * NT].rearrange("p (q l) -> p q l", l=NT)
        part = [xg, ctx_t]
        row_i = sb("row_i", [P, TOPK * T], I32)
        row_f = sb("row_f", [P, TOPK * T])
        iota_pi = sb("iota_pi", [P, P], I32)
        iota_p = sb("iota_p", [P, P])
        slot_hi = sb("slot_hi", [P, TOPK * T], I32)
        slot_lo = sb("slot_lo", [P, TOPK * T], I32)
        hi_f = sb("hi_f", [P, TOPK * T])
        lo_f = sb("lo_f", [P, TOPK * T])
        wt = sb("wt", [P, TOPK * T])
        t_row = sb("t_row", [P, NT])
        t_wt = sb("t_wt", [P, NT])
        t_tmp = sb("t_tmp", [P, NT])
        t_tmp2 = sb("t_tmp2", [P, NT])
        t_dst = sb("t_dst", [P, NT], I32)
        t_src = sb("t_src", [P, NT], I32)
        iota_i = sb("iota_i", [P, E], I32)
        iota_e = sb("iota_e", [P, E])
        e_base = sb("e_base", [P, E])
        seg = sb("seg", [P, E, TOPK * T])
        lg = sb("lg", [P, T, E])
        v8 = sb("v8", [P, T, 8])
        i8 = sb("i8", [P, T, 8], U32)
        pick = sb("pick", [P, TOPK, T])
        hot = sb("hot", [P, E, TOPK * T], BF16)
        top = sb("top", [P, 3, T])
        top_m = sb("top_m", [P, T])
        expt = sb("expt", [P, 3, T])
        prob = sb("prob", [P, TOPK, T])
        tot = sb("tot", [P, E * TOPK * T])
        incl = sb("incl", [P, E * TOPK * T])
        kept = sb("kept", [P, E * TOPK * T])
        slot = sb("slot", [P, TOPK * T])
        keep = sb("keep", [P, TOPK * T])
        slot_i = sb("slot_i", [P, TOPK * T], I32)
        x2_rows = nc.dram_tensor("x2_rows", [N, D], F32, kind="Internal").ap()
        results = nc.dram_tensor("results", [TOPK * N, D], F32, kind="Internal").ap()

        ld_x, ld_ctx, ld_w, ld_wo, ld_vec = (sem(n) for n in ("ld_x", "ld_ctx", "ld_w", "ld_wo", "ld_vec"))
        consts = sem("consts")
        zeroed = sem("zeroed")
        dve_link = sem("dve_link")
        xn_ready = sem("xn_ready")
        b0_full, b0_free = sem("b0_full"), sem("b0_free")
        b1_full, b1_free_dve, b1_free_act = sem("b1_full"), sem("b1_free_dve"), sem("b1_free_act")
        s_full0, s_full1, s_free0, s_free1 = sem("s_full0"), sem("s_full1"), sem("s_free0"), sem("s_free1")
        shifted, exped, probs, spread = sem("shifted"), sem("exped"), sem("probs"), sem("spread")
        pv0, pv1, ctx0, ctx1 = sem("pv0"), sem("pv1"), sem("ctx0"), sem("ctx1")
        ld_small, ld_bias, ld_in = sem("ld_small"), sem("ld_bias"), sem("ld_in")
        turned_w, w_done_dve, w_done_act = sem("turned_w"), sem("w_done_dve"), sem("w_done_act")
        c_scaled, c_rs = sem("c_scaled"), sem("c_rs")
        cT_full, cT_free, kq_full, kq_free, v_full, v_free = (sem(n) for n in ("cT_full", "cT_free", "kq_full", "kq_free", "v_full", "v_free"))
        x1_ready, x1T_full, x1T_free, h0_full, h0_free, x1n_ready = (sem(n) for n in (
            "x1_ready", "x1T_full", "x1T_free", "h0_full", "h0_free", "x1n_ready"))
        (sn_ready, t12_full, snh_ready, sB_full, negmax, exB, vr_ready, u_full, upd_ready, t3_full, updT_ready,
         g_full, rz_ready, npre_ready, new_ready, h_ready) = (sem(n) for n in (
             "sn_ready", "t12_full", "snh_ready", "sB_full", "negmax", "exB", "vr_ready", "u_full", "upd_ready",
             "t3_full", "updT_ready", "g_full", "rz_ready", "npre_ready", "new_ready", "h_ready"))
        r_zeroed, x2_stored, padded, row_done, wt_done, table_full, dst_ready, src_ready = (sem(n) for n in (
            "r_zeroed", "x2_stored", "padded", "row_done", "wt_done", "table_full", "dst_ready", "src_ready"))
        lo_ready, hi_ready, idx_ready = sem("lo_ready"), sem("hi_ready"), sem("idx_ready")
        x2_ready, x2T_full, x2T_free, lg_full = (sem(n) for n in ("x2_ready", "x2T_full", "x2T_free", "lg_full"))
        hot_ready, rank_full, top_ready, expt_ready = (sem(n) for n in (
            "hot_ready", "rank_full", "top_ready", "expt_ready"))
        ld_xe0, ld_xe1, ld_we0, ld_we1 = (sem(n) for n in ("ld_xe0", "ld_xe1", "ld_we0", "ld_we1"))
        ld_xe, ld_we = [ld_xe0, ld_xe1], [ld_we0, ld_we1]
        xeT_full, xeT_free, fc_full, gelu_done, pr_full, eo_ready, returned0, returned1 = (sem(n) for n in (
            "xeT_full", "xeT_free", "fc_full", "gelu_done", "pr_full", "eo_ready", "returned0", "returned1"))
        returned = [returned0, returned1]
        ld_part = [sem(f"ld_part{q}") for q in range(4)]
        y_ready = sem("y_ready")
        stored = sem("stored")

        block = ctx.enter_context(nc.Block())

        B0_ITEMS = 1 + HP + GL
        B1_ITEMS = HP + GL + GL

        def b0_item(sg, k):
            return B0_ITEMS * sg + k

        def b1_item(sg, first, k):
            if first:
                return k if k <= HP else k - 2
            return B1_ITEMS * sg - 2 + k

        def wait(eng, s, value):
            if not (isinstance(value, int) and value <= 0):
                eng.wait_ge(s, value)

        BLOCKS = ITERS * B8

        @block.sync
        def _(sp):
            for s in range(S):
                sp.dma_start(xg[s:s + 8 * 15 + 1:8, :, :], x[s].rearrange("(g l) c -> l g c", l=16)).then_inc(ld_x, 16)
            sp.dma_start(wqkv[:, :], qkv_w.rearrange("c t k -> c (t k)")).then_inc(ld_w, 16)
            sp.dma_start(wo[:, :, :], out_w.rearrange("(h k) c -> k h c", k=P)).then_inc(ld_wo, 16)
            sp.dma_start(ctx_t[:, :, :], ctx_in.rearrange("s (t p) c -> p (s t) c", p=P)).then_inc(ld_ctx, 16)
            sp.wait_ge(zeroed, 3)
            for a in range(TOPK * N // (P * 8)):
                sp.dma_start(results[a * P * 8:(a + 1) * P * 8, :].rearrange("(p j) c -> p j c", j=8),
                             zeros[:, :].rearrange("p (j c) -> p j c", j=8)).then_inc(r_zeroed, 16)

            def load_weights(e, r, reuse):
                if reuse:
                    sp.wait_ge(pr_full, e - 1)
                sp.dma_start(cfc[:, r, :], c_fc[e]).then_inc(ld_we[r], 16)
                sp.dma_start(cpr[:, r, :, :], c_proj[e].rearrange("(f p) d -> p f d", p=P)).then_inc(ld_we[r], 16)

            load_weights(0, 0, False)
            load_weights(1, 1, False)
            for half in range(2):
                sp.wait_ge(x2_ready, 2 * half + 2)
                sp.dma_start(x2_rows[half * N // 2:(half + 1) * N // 2, :].rearrange("(t p) c -> p t c", p=P),
                             x2[:, half * T // 2:(half + 1) * T // 2, :]).then_inc(x2_stored, 16)
            for e in range(2, E):
                load_weights(e, e % 2, True)
            for r in range(2):
                sp.wait_ge(returned[r], 16 * NT // 2)
            for q in range(4):
                for k in range(TOPK):
                    sp.dma_start(part[k][:, 4 * q:4 * q + 4, :],
                                 results[k * N + q * 512:k * N + (q + 1) * 512, :].rearrange("(t p) c -> p t c", p=P)
                                 ).then_inc(ld_part[q], 16)
            out_t = out.rearrange("s (t p) c -> p (s t) c", p=P)
            for q in range(4):
                sp.wait_ge(y_ready, q + 1)
                sp.dma_start(out_t[:, 4 * q:4 * q + 4, :], h[:, 4 * q:4 * q + 4, :]).then_inc(stored, 16)
            sp.wait_ge(stored, 64)

        @block.gpsimd
        def _(pool):
            pool.memset(ident[:, :], 0.0).then_inc(consts, 1)
            pool.memset(full_mask[:, :], 0.0).then_inc(consts, 1)
            pool.wait_ge(consts, 2)
            pool.affine_select(out=ident[:, :], in_=ident[:, :], compare_op=ALU.not_equal, fill=1.0,
                               base=0, pattern=[[-1, P]], channel_multiplier=1).then_inc(consts, 1)
            pool.affine_select(out=full_mask[:, :], in_=full_mask[:, :], compare_op=ALU.is_ge, fill=OFF,
                               base=0, pattern=[[-1, P]], channel_multiplier=1).then_inc(consts, 1)
            pool.wait_ge(consts, 4)
            cols = full_mask[:, :].rearrange("p (a s) -> p a s", s=S)
            pool.affine_select(out=cols, in_=cols, compare_op=ALU.is_ge, fill=OFF,
                               base=S - 1, pattern=[[S, P // S], [0, S]], channel_multiplier=-1).then_inc(consts, 1)
            pool.memset(pool_k[:, :], 0.0).then_inc(zeroed, 1)
            pool.memset(pool_p[:, :], 0.0).then_inc(zeroed, 1)
            pool.memset(zeros[:, :], 0.0).then_inc(zeroed, 1)
            pool.memset(ones_b[:, :], 1.0).then_inc(consts, 1)
            pool.memset(before[:, :], 1.0).then_inc(consts, 1)
            pool.memset(bias[:, :], 0.0).then_inc(consts, 1)
            pool.memset(seg[:, :, :], 1.0).then_inc(consts, 1)
            pool.wait_ge(consts, 9)
            pool.affine_select(out=before[:, :], in_=before[:, :], compare_op=ALU.is_gt, fill=0.0,
                               base=0, pattern=[[1, P]], channel_multiplier=-1).then_inc(consts, 1)
            pool.memset(seg[:, :, 0:1], 0.0).then_inc(consts, 1)
            pool.iota(iota_i[:, :], pattern=[[1, E]], base=0, channel_multiplier=0).then_inc(consts, 1)
            pool.iota(row_i[:, :], pattern=[[P, TOPK * T]], base=1, channel_multiplier=1).then_inc(consts, 1)
            pool.iota(iota_pi[:, :], pattern=[[1, P]], base=0, channel_multiplier=0).then_inc(consts, 1)

            pool.wait_ge(c_rs, 1)
            for g in range(4):
                rows4 = ctx_t[:, 4 * g:4 * g + 4, :]
                pool.tensor_tensor(rows4, rows4, c_r[:, 4 * g:4 * g + 4].unsqueeze(2).to_broadcast([P, 4, D]), ALU.mult
                                   ).then_inc(c_scaled, 1)
            pool.wait_ge(h0_free, 4)
            pool.tensor_copy(x1n[:, :, :], h[:, :, :]).then_inc(x1n_ready, 1)

            pool.wait_ge(h_ready, BLOCKS)
            pool.memset(hot_hi[:, :, 2 * NT:P], 0.0).then_inc(padded, 1)
            pool.wait_ge(hi_ready, 1)
            pool.tensor_tensor(hot_hi[:, :, 0:NT], tile_hot, row_f[:, :].unsqueeze(2).to_broadcast([P, TOPK * T, NT]),
                               ALU.mult).then_inc(row_done, 1)

            def fetch(e, r):
                if e >= 2:
                    pool.wait_ge(xeT_full, e - 1)
                for j in range(CT):
                    c = e * CT + j
                    pool.indirect_dma_start(xe[:, r, j, :], None, x2_rows[:, :],
                                            bass.IndirectOffsetOnAxis(t_src[:, c:c + 1], 0),
                                            bounds_check=N - 1, oob_is_err=False).then_inc(ld_xe[r], 16)

            def send_back(e, r):
                pool.wait_ge(eo_ready, e + 1)
                for j in range(CT):
                    c = e * CT + j
                    pool.indirect_dma_start(results[:, :], bass.IndirectOffsetOnAxis(t_dst[:, c:c + 1], 0),
                                            eo[:, r, j, :], None, bounds_check=TOPK * N - 1, oob_is_err=False
                                            ).then_inc(returned[r], 16)

            pool.wait_ge(x2_stored, 32)
            pool.wait_ge(src_ready, 1)
            fetch(0, 0)
            fetch(1, 1)
            pool.wait_ge(r_zeroed, 16 * TOPK * N // (P * 8))
            pool.wait_ge(dst_ready, 1)
            for e in range(E):
                if e + 2 < E:
                    fetch(e + 2, e % 2)
                send_back(e, e % 2)

        @block.tensor
        def _(pe):
            def free_b0(item):
                if not (isinstance(item, int) and item == 0):
                    pe.wait_ge(b0_free, item)

            def free_b1(sg, first, k):
                item = b1_item(sg, first, k)
                if not (isinstance(item, int) and item == 0):
                    pe.wait_ge(b1_free_dve, item)
                if k <= HP and not (isinstance(sg, int) and sg == SG):
                    keys = HP * sg + k
                    if not (isinstance(keys, int) and keys == 0):
                        pe.wait_ge(b1_free_act, keys)

            def project(sg, first):
                pe.wait_ge(xn_ready, sg + 1)
                free_b0(b0_item(sg, 0))
                for g in range(GL):
                    last = pe.transpose(ps[:, 0, g * P:(g + 1) * P], xn[:, g, :], ident[:, :])
                last.then_inc(b0_full, 1)
                pe.wait_ge(b0_free, b0_item(sg, 1))
                for hp in range(HP):
                    free_b0(b0_item(sg, 1 + hp))
                    pe.matmul(ps[:, 0, :], wqkv[:, hp * P:(hp + 1) * P], lnT[:, :], start=True, stop=True
                              ).then_inc(b0_full, 1)
                    free_b1(sg, first, hp)
                    pe.matmul(ps[:, 1, :], wqkv[:, (HP + hp) * P:(HP + hp + 1) * P], lnT[:, :],
                              start=True, stop=True).then_inc(b1_full, 1)

            def values(sg, first):
                for g in range(GL):
                    for half in range(2):
                        if half == 0:
                            free_b0(b0_item(sg, 1 + HP + g))
                        else:
                            free_b1(sg, first, HP + 2 + g)
                        pe.matmul(ps[:, half, :], lnT[:, g * P:(g + 1) * P],
                                  wqkv[:, 2 * H * DH + half * 512:2 * H * DH + (half + 1) * 512],
                                  start=True, stop=True).then_inc(b1_full if half else b0_full, 1)

            def scores(sg, first, g):
                n = GL * sg + g
                if g == 0:
                    pe.wait_ge(b0_free, b0_item(sg, 1 + HP))
                    pe.wait_ge(b1_free_dve, b1_item(sg, first, HP))
                    pe.wait_ge(b1_free_act, HP * sg + HP)
                for half in range(2):
                    if not (first and g == 0):
                        pe.wait_ge(s_free1 if half else s_free0, n)
                    for k in range(4):
                        hp = 4 * half + k
                        last = pe.matmul(ps[:, 2 + 2 * half + k // 2, (k % 2) * 256:(k % 2) * 256 + 256],
                                         qT[:, hp, g * P:(g + 1) * P],
                                         kz[:, hp, g, :, :].rearrange("p z n -> p (z n)"), start=True, stop=True)
                    last.then_inc(s_full1 if half else s_full0, 1)

            def weigh(sg, g, first):
                n = GL * sg + g
                pe.wait_ge(spread, n + 1)
                pe.wait_ge(b0_free, b0_item(sg, 2 + HP + g))
                pe.wait_ge(b1_free_dve, b1_item(sg, first, HP + 3 + g))
                for half in range(2):
                    if not (first and g == 0):
                        pe.wait_ge(ctx1 if half else ctx0, n)
                    for hd in range(8 * half, 8 * half + 8):
                        lo = (hd % 2) * DH
                        last = pe.matmul(ps[lo:lo + DH, 6 + half, (hd // 2 % 4) * P:(hd // 2 % 4 + 1) * P],
                                         v[:, g, hd * DH:(hd + 1) * DH], pbd[:, g % 2, hd, :],
                                         start=True, stop=True)
                    last.then_inc(pv1 if half else pv0, 1)

            def output(body_sg, first, k, n):
                pe.wait_ge(ctx0, n + 1)
                pe.wait_ge(ctx1, n + 1)
                free_b1(body_sg, first, k)
                for hp in range(HP):
                    last = pe.matmul(ps[:, 1, 0:P], ctxT[:, hp, :], wo[:, hp, :], start=(hp == 0), stop=(hp == HP - 1))
                last.then_inc(b1_full, 1)

            def supergroup(sg, first):
                project(sg, first)
                if not first:
                    weigh(sg - 1, 2, False)
                scores(sg, first, 0)
                if not first:
                    output(sg, first, HP, GL * sg - 2)
                    weigh(sg - 1, 3, False)
                scores(sg, first, 1)
                if not first:
                    output(sg, first, HP + 1, GL * sg - 1)
                values(sg, first)
                weigh(sg, 0, first)
                scores(sg, first, 2)
                output(sg, first, HP + 2 + GL, GL * sg)
                weigh(sg, 1, first)
                scores(sg, first, 3)
                output(sg, first, HP + 3 + GL, GL * sg + 1)

            pe.wait_ge(consts, 5)
            pe.wait_ge(ld_small, 16 * 5)
            pe.matmul(ps[:, 2, 0:P], w_nat[:, 1, :], w_nat[:, 0, :], start=True, stop=True)
            for k in range(2, 5):
                pe.transpose(ps[:, 2, (k - 1) * P:k * P], w_nat[:, k, :], ident[:, :])
            for k in range(5, 9):
                last = pe.transpose(ps[:, 3, (k - 5) * P:(k - 4) * P], w_nat[:, k, :], ident[:, :])
            last.then_inc(turned_w, 1)
            pe.wait_ge(w_done_dve, 4)
            pe.wait_ge(ld_w, 16)
            pe.wait_ge(zeroed, 3)
            pe.wait_ge(ld_wo, 16)
            supergroup(0, True)
            with pe.Fori(1, SG) as sg:
                supergroup(sg, False)
            weigh(SG - 1, 2, False)
            output(SG, False, 0, GL * SG - 2)
            weigh(SG - 1, 3, False)
            output(SG, False, 1, GL * SG - 1)

            for q in range(4):
                pe.wait_ge(c_scaled, q + 1)
                for k in range(4):
                    last = pe.transpose(ps[:, 2 + q, k * P:(k + 1) * P], ctx_t[:, 4 * q + k, :], ident[:, :])
                last.then_inc(cT_full, 1)
            for q in range(4):
                pe.wait_ge(cT_free, q + 1)
                pe.matmul(ps[:, 2 + q, :], w_kq[:, :], cT[:, 512 * q:512 * q + 512], start=True, stop=True
                          ).then_inc(kq_full, 1)
            for q in range(4):
                pe.wait_ge(kq_free, q + 1)
                for k in range(4):
                    last = pe.matmul(ps[:, 2 + q, k * P:(k + 1) * P], cT[:, (4 * q + k) * P:(4 * q + k + 1) * P],
                                     w_v[:, :], start=True, stop=True)
                last.then_inc(v_full, 1)
            for q in range(4):
                pe.wait_ge(x1_ready, q + 1)
                if q > 1:
                    pe.wait_ge(v_free, q - 1)
                if q == 1:
                    pe.wait_ge(b1_free_dve, b1_item(SG, False, 2))
                bank = (0, 1, 2, 3)[q]
                for k in range(4):
                    last = pe.transpose(ps[:, bank, k * P:(k + 1) * P], xg[:, 4 * q + k, :], ident[:, :])
                last.then_inc(x1T_full, 1)
            pe.wait_ge(x1T_free, 4)
            for q in range(4):
                if q < 2:
                    pe.wait_ge(v_free, q + 3)
                for k in range(4):
                    last = pe.transpose(ps[:, 4 + q, k * P:(k + 1) * P], x1T[:, (4 * q + k) * P:(4 * q + k + 1) * P],
                                        ident[:, :])
                last.then_inc(h0_full, 1)

            def turn_slots(n, b):
                pe.wait_ge(sn_ready, n + 1)
                wait(pe, snh_ready, n)
                for t in range(2):
                    pe.transpose(ps[:, 0, t * P:(t + 1) * P], sn[:, b % 2, t, :], ident[:, :])
                for t in range(2):
                    last = pe.transpose(ps[:, 0, (2 + t) * P:(3 + t) * P], h[:, 2 * b + t, :], ident[:, :])
                last.then_inc(t12_full, 1)

            def score_slots(n, b):
                pe.wait_ge(snh_ready, n + 1)
                wait(pe, exB, n)
                for m in range(2):
                    last = pe.matmul(ps[:, 1, m * 256:(m + 1) * 256], kq[:, (2 * b + m) * P:(2 * b + m + 1) * P],
                                     snh[:, b % 4, 0:256], start=True, stop=True)
                last.then_inc(sB_full, 1)

            def update_slots(n, b):
                pe.wait_ge(vr_ready, n + 1)
                pe.wait_ge(exB, n + 1)
                wait(pe, upd_ready, n)
                for t in range(2):
                    for m in range(2):
                        last = pe.matmul(ps[:, 2, t * 256:t * 256 + D + 1], e_m[:, b % 2, m, t * P:(t + 1) * P],
                                         vr[:, b % 2, m, :], start=(m == 0), stop=(m == 1))
                last.then_inc(u_full, 1)

            def turn_updates(n, b):
                pe.wait_ge(upd_ready, n + 1)
                wait(pe, updT_ready, n)
                for t in range(2):
                    last = pe.transpose(ps[:, 3, t * P:(t + 1) * P], upd[:, b % 2, t, :], ident[:, :])
                last.then_inc(t3_full, 1)

            def gates(n, b):
                pe.wait_ge(updT_ready, n + 1)
                wait(pe, npre_ready, n - 1)
                for t in range(2):
                    bank = ps[:, 4 + 2 * (b % 2) + t, :]
                    pe.matmul(bank, ones_b[:, :], bias[:, :], start=True, stop=False)
                    pe.matmul(bank[:, 0:3 * D], updT[:, b % 2, t * P:(t + 1) * P], w_ih[:, :], start=False, stop=False)
                    last = pe.matmul(bank[:, D:4 * D], snh[:, b % 4, 256 + t * P:256 + (t + 1) * P], w_hh[:, :],
                                     start=False, stop=True)
                last.then_inc(g_full, 1)

            def step(n, k):
                if 0 <= k < BLOCKS:
                    turn_updates(n, k % 8)
                if 0 <= k + 3 < BLOCKS:
                    turn_slots(n + 3, (k + 3) % 8)
                if 0 <= k + 2 < BLOCKS:
                    score_slots(n + 2, (k + 2) % 8)
                if 0 <= k + 1 < BLOCKS:
                    update_slots(n + 1, (k + 1) % 8)
                if 0 <= k < BLOCKS:
                    gates(n, k % 8)

            pe.wait_ge(consts, 14)
            pe.wait_ge(h0_free, 4)
            pe.wait_ge(x1n_ready, 1)
            for k in range(-3, 3):
                step(k, k)
            with pe.Fori(0, ITERS - 1) as it:
                for k in range(3, 11):
                    step(8 * it + k, k)
            for k in range(8 * (ITERS - 1) + 3, BLOCKS):
                step(k, k)

            for q in range(4):
                pe.wait_ge(x2_ready, q + 1)
                for k in range(4):
                    last = pe.transpose(ps[:, q, k * P:(k + 1) * P], x2[:, 4 * q + k, :], ident[:, :])
                last.then_inc(x2T_full, 1)
            for q in range(4):
                pe.wait_ge(x2T_free, q + 1)
                for k in range(4):
                    t = 4 * q + k
                    last = pe.matmul(ps[:, 4, t * E:(t + 1) * E], x1T[:, t * P:(t + 1) * P], wg[:, :],
                                     start=True, stop=True)
            last.then_inc(lg_full, 1)
            pe.wait_ge(hot_ready, 1)
            hot_flat = hot[:, :, :].rearrange("p e q -> p (e q)")
            pe.matmul(ps[:, 5, 0:256], before[:, :], hot_flat, start=True, stop=True)
            pe.matmul(ps[:, 6, 0:256], ones_b[:, :], hot_flat, start=True, stop=True).then_inc(rank_full, 1)
            pe.wait_ge(padded, 1)
            pe.wait_ge(row_done, 1)
            pe.wait_ge(wt_done, 1)
            for k in range(TOPK):
                pe.wait_ge(lo_ready, k + 1)
                for q in range(k * T, (k + 1) * T):
                    last = pe.matmul(ps[:, 7, 0:P], hot_lo[:, q, :], hot_hi[:, q, :], start=(q == 0),
                                     stop=(q == TOPK * T - 1))
            last.then_inc(table_full, 1)

            def turn_expert(pair, r, e):
                pe.wait_ge(ld_xe[r], 16 * CT * pair + 16 * CT)
                wait(pe, xeT_free, e)
                for j in range(CT):
                    bank, col = divmod(j * P, 512)
                    last = pe.transpose(ps[:, bank, col:col + P], xe[:, r, j, :], ident[:, :])
                last.then_inc(xeT_full, 1)

            def expand_expert(pair, r, e):
                pe.wait_ge(ld_we[r], 32 * pair + 32)
                pe.wait_ge(xeT_free, e + 1)
                for f in range(FC):
                    wait(pe, gelu_done, FC * e + f - 1)
                    b0 = 2 + 2 * (f % 2)
                    w = cfc[:, r, f * P:(f + 1) * P]
                    pe.matmul(ps[:, b0, :], w, xeT[:, r, 0:512], start=True, stop=True)
                    pe.matmul(ps[:, b0 + 1, 0:CAP - 512], w, xeT[:, r, 512:CAP], start=True, stop=True
                              ).then_inc(fc_full, 1)

            def reduce_expert(e, r):
                pe.wait_ge(gelu_done, FC * e + FC)
                wait(pe, eo_ready, e)
                for j in range(CT):
                    bank, col = divmod(j * P, 512)
                    for f in range(FC):
                        last = pe.matmul(ps[:, 6 + bank, col:col + P], hT[:, r, f, j * P:(j + 1) * P], cpr[:, r, f, :],
                                         start=(f == 0), stop=(f == FC - 1))
                last.then_inc(pr_full, 1)

            def experts(pair, final):
                for r in range(2):
                    e = 2 * pair + r
                    expand_expert(pair, r, e)
                    if not (final and r == 1):
                        turn_expert(pair + r, 1 - r, e + 1)
                    reduce_expert(e, r)

            turn_expert(0, 0, 0)
            experts(0, False)
            with pe.Fori(1, E // 2 - 1) as pair:
                experts(pair, False)
            experts(E // 2 - 1, True)

        @block.vector
        def _(dve):
            links = [0]

            def link(ins, base=None):
                links[0] += 1
                ins.then_inc(dve_link, 1)
                dve.wait_ge(dve_link, links[0] if base is None else base + links[0])

            def rsqrt(base, a, y, t):
                link(dve.tensor_scalar(t.bitcast(I32), a.bitcast(I32), 1, None, ALU.logical_shift_right), base)
                link(dve.tensor_scalar(y.bitcast(I32), t.bitcast(I32), -1.0, float(0x5F3759DF), ALU.mult, ALU.add), base)
                for _ in range(3):
                    link(dve.tensor_tensor(t, y, y, ALU.mult), base)
                    link(dve.scalar_tensor_tensor(t, t, -0.5, a, ALU.mult, ALU.mult), base)
                    link(dve.scalar_tensor_tensor(y, t, 1.5, y, ALU.add, ALU.mult), base)

            def stats(g0, g1, src, eps):
                for g in range(g0, g1):
                    last = dve.bn_stats(st[:, g, :], src[:, g, :])
                link(last)
                for g in range(g0, g1):
                    last = dve.bn_aggr(mv[:, g, :], st[:, g, :])
                link(last)
                link(dve.tensor_scalar(var[:, g0:g1], mv[:, g0:g1, 1], eps, None, ALU.add))
                rsqrt(None, var[:, g0:g1], rs[:, g0:g1], rt[:, g0:g1])

            def normalise_in(sg, first):
                if not first:
                    dve.wait_ge(b0_full, b0_item(sg, 0) - B0_ITEMS + 1)
                for g in range(GL):
                    last = dve.tensor_scalar(xn[:, g, :], xg[:, GL * sg + g, :], mv[:, GL * sg + g, 0:1],
                                             rs[:, bass.ds(GL * sg + g, 1)] if not isinstance(sg, int) else rs[:, GL * sg + g:GL * sg + g + 1],
                                             ALU.subtract, ALU.mult)
                last.then_inc(xn_ready, 1)

            def key_low(sg, first, hp):
                dve.wait_ge(b1_full, b1_item(sg, first, hp) + 1)
                dve.tensor_copy(kz[0:DH, hp, :, 0, :], ps[0:DH, 1, :].rearrange("p (g n) -> p g n", g=GL)
                                ).then_inc(b1_free_dve, 1)

            def value_high(sg, first, g):
                dve.wait_ge(b1_full, b1_item(sg, first, HP + 2 + g) + 1)
                dve.tensor_copy(v[:, g, 512:1024], ps[:, 1, :]).then_inc(b1_free_dve, 1)

            def diagonal(n, g, base):
                dve.wait_ge(s_full0, n + 1)
                src = ps[:, 2:4, :].rearrange("p b (h k) -> p (b h) k", h=4)
                for q in range(4):
                    r = slice(QB * q, QB * q + QB)
                    last = dve.tensor_tensor(sc[r, g % 2, 0:8, :], src[r, :, QB * q:QB * q + QB],
                                             mask[r, :].unsqueeze(1).to_broadcast([QB, 8, QB]), ALU.add)
                last.then_inc(s_free0, 1)

            def shift(n, g, base):
                dve.wait_ge(s_free1, n + 1)
                hi = sc[:, g % 2, 8:16, :]
                link(dve.tensor_tensor(hi, hi, mask[:, :].unsqueeze(1).to_broadcast([P, 8, QB]), ALU.add), base)
                link(dve.tensor_reduce(mx[:, :], sc[:, g % 2, :, :], AX.X, ALU.max), base)
                dve.tensor_tensor(sc[:, g % 2, :, :], sc[:, g % 2, :, :],
                                  mx[:, :].unsqueeze(2).to_broadcast([P, H, QB]), ALU.subtract).then_inc(shifted, 1)

            def divide(n, g, base, reuse):
                dve.wait_ge(exped, n + 1)
                link(dve.tensor_reduce(sm[:, :], pc[:, g % 2, :, :], AX.X, ALU.add), base)
                link(dve.reciprocal(sm[:, :], sm[:, :]), base)
                link(dve.tensor_tensor(pc[:, g % 2, :, :], pc[:, g % 2, :, :],
                                       sm[:, :].unsqueeze(2).to_broadcast([P, H, QB]), ALU.mult), base)
                if reuse:
                    dve.wait_ge(spread, n - 1)
                dve.transpose(pt[:, g % 2, :, :].rearrange("p h k -> p (h k)"),
                              pc[:, g % 2, :, :].rearrange("p h k -> p (h k)")).then_inc(probs, 1)

            def context_high(n):
                dve.wait_ge(pv1, n + 1)
                dve.tensor_copy(ctxT[:, 4:8, :], ps[:, 7, :].rearrange("p (h n) -> p h n", h=4)).then_inc(ctx1, 1)

            def residual(body_sg, first, k, n):
                dve.wait_ge(b1_full, b1_item(body_sg, first, k) + 1)
                row = xg[:, n, :]
                dve.tensor_tensor(row, row, ps[:, 1, 0:P], ALU.add).then_inc(b1_free_dve, 1)
                dve.wait_ge(b1_free_dve, b1_item(body_sg, first, k) + 1)
                dve.bn_stats(st[:, n, :], row)

            def supergroup(sg, first, base):
                normalise_in(sg, first)
                if not first:
                    divide(GL * sg - 1, 3, base, True)
                for hp in range(HP):
                    key_low(sg, first, hp)
                if not first:
                    context_high(GL * sg - 2)
                diagonal(GL * sg, 0, base)
                shift(GL * sg, 0, base)
                if not first:
                    residual(sg, first, HP, GL * sg - 2)
                    context_high(GL * sg - 1)
                divide(GL * sg, 0, base, not first)
                diagonal(GL * sg + 1, 1, base)
                shift(GL * sg + 1, 1, base)
                if not first:
                    residual(sg, first, HP + 1, GL * sg - 1)
                for g in range(GL):
                    value_high(sg, first, g)
                    if g == 1:
                        divide(GL * sg + 1, 1, base, not first)
                if first:
                    stats(GL, T, xg, LN_EPS)
                    dve.wait_ge(ld_ctx, 16)
                for g in range(GL):
                    dve.bn_stats(c_st[:, GL * sg + g, :], ctx_t[:, GL * sg + g, :])
                context_high(GL * sg)
                diagonal(GL * sg + 2, 2, base)
                shift(GL * sg + 2, 2, base)
                residual(sg, first, HP + 2 + GL, GL * sg)
                divide(GL * sg + 2, 2, base, True)
                context_high(GL * sg + 1)
                diagonal(GL * sg + 3, 3, base)
                shift(GL * sg + 3, 3, base)
                residual(sg, first, HP + 3 + GL, GL * sg + 1)

            dve.wait_ge(consts, 5)
            dve.wait_ge(ld_small, 16 * 5)
            dve.wait_ge(ld_in, 32)
            dve.wait_ge(turned_w, 1)
            for dst, src, sc1 in ((w_kq[:, :], ps[:, 2, 0:P], lnv[:, 3:4]), (w_v[:, :], ps[:, 2, P:2 * P], lnv[:, 3:4])):
                dve.tensor_scalar(dst, src, sc1, None, ALU.mult).then_inc(w_done_dve, 1)
            dve.tensor_copy(w_ih[:, D:3 * D], ps[:, 2, 2 * P:4 * P])
            dve.tensor_copy(w_ih[:, 0:D], ps[:, 3, 0:P]).then_inc(w_done_dve, 1)
            dve.tensor_copy(w_hh[:, :], ps[:, 3, P:4 * P]).then_inc(w_done_dve, 1)
            for q in range(4):
                last = dve.tensor_copy(mask[QB * q:QB * q + QB, :], full_mask[QB * q:QB * q + QB, QB * q:QB * q + QB])
            link(last)
            dve.wait_ge(ld_x, 16 * S)
            dve.wait_ge(zeroed, 3)
            stats(0, GL, xg, LN_EPS)
            supergroup(0, True, None)
            done = links[0]
            PER = 5 * GL
            with dve.Fori(1, SG) as sg:
                supergroup(sg, False, sg * PER - PER)
                assert links[0] - done == PER, links[0] - done
            links[0] = done + PER * (SG - 1)
            divide(T - 1, 3, None, True)
            context_high(T - 2)
            residual(SG, False, 0, T - 2)
            context_high(T - 1)
            residual(SG, False, 1, T - 1)

            for g in range(T):
                last = dve.bn_aggr(c_mv[:, g, :], c_st[:, g, :])
            link(last)
            link(dve.tensor_tensor(var[:, :], c_mv[:, :, 0], c_mv[:, :, 0], ALU.mult))
            link(dve.scalar_tensor_tensor(var[:, :], var[:, :], RMS_EPS, c_mv[:, :, 1], ALU.add, ALU.add))
            rsqrt(None, var[:, :], c_r[:, :], rt[:, :])
            dve.tensor_copy(rt[:, :], c_r[:, :]).then_inc(c_rs, 1)
            for g in range(T):
                last = dve.bn_aggr(mv[:, g, :], st[:, g, :])
            link(last)
            link(dve.tensor_scalar(var[:, :], mv[:, :, 1], OUT_EPS, None, ALU.add))
            rsqrt(None, var[:, :], rs[:, :], rt[:, :])
            for g in range(T):
                last = dve.tensor_scalar(xg[:, g, :], xg[:, g, :], mv[:, g, 0:1], rs[:, g:g + 1], ALU.subtract, ALU.mult)
                if g % 4 == 3:
                    last.then_inc(x1_ready, 1)
            for q in range(4):
                dve.wait_ge(v_full, q + 1)
                dve.tensor_copy(vp[:, 4 * q:4 * q + 4, :], ps[:, 2 + q, :].rearrange("p (t d) -> p t d", t=4)
                                ).then_inc(v_free, 1)
            dve.wait_ge(ld_bias, 112)
            dve.tensor_copy(b_sum[:, 0:D], b_rows[:, 0, 2 * D:3 * D])
            dve.tensor_tensor(b_sum[:, D:3 * D], b_rows[:, 0, 0:2 * D], b_rows[:, 1, 0:2 * D], ALU.add)
            link(dve.tensor_copy(b_sum[:, 3 * D:4 * D], b_rows[:, 1, 2 * D:3 * D]))
            dve.wait_ge(consts, 14)
            link(dve.tensor_copy(b_cut[:, :], b_sum[:, :]))
            link(dve.tensor_scalar(b_part[:, :], b_cut[:, :], ident[0:3, 0:1], None, ALU.mult))
            for k in (1, 2):
                link(dve.tensor_tensor(b_sum[:, :], b_sum[:, :], b_cut[:, :], ALU.subtract))
                link(dve.tensor_copy(b_cut[:, :], b_sum[:, :]))
                link(dve.scalar_tensor_tensor(b_part[:, :], b_cut[:, :], ident[0:3, k:k + 1], b_part[:, :],
                                              ALU.mult, ALU.add))
            link(dve.tensor_copy(bias[0:3, :], b_part[:, :]))

            def squares(b):
                for t in (2 * b, 2 * b + 1):
                    last = dve.tensor_tensor_reduce(sq_out[:, t % 2 * D:t % 2 * D + D], h[:, t, :], h[:, t, :], 1.0, 0.0, ALU.mult, ALU.add,
                                                    sq[:, t:t + 1])
                return last

            def slot_scale(t0, t1, base):
                link(dve.tensor_scalar(var[:, t0:t1], sq[:, t0:t1], 1.0 / D, RMS_EPS, ALU.mult, ALU.add), base)
                rsqrt(base, var[:, t0:t1], r_h[:, t0:t1], rt[:, t0:t1])

            def normalise_slots(n, b):
                wait(dve, t12_full, n - 1)
                dve.tensor_tensor(sn[:, b % 2, :, :], h[:, 2 * b:2 * b + 2, :],
                                  r_h[:, 2 * b:2 * b + 2].unsqueeze(2).to_broadcast([P, 2, D]), ALU.mult
                                  ).then_inc(sn_ready, 1)

            def maxima(n, b):
                dve.wait_ge(sB_full, n + 1)
                wait(dve, exB, n - 1)
                dve.tensor_reduce(n_mx[:, b % 2, :], ps[:, 1, :].rearrange("p (m k) -> p m k", m=2), AX.X, ALU.max,
                                  negate=True).then_inc(negmax, 1)

            def scale_values(n, b, base):
                dve.wait_ge(exB, n + 1)
                wait(dve, u_full, n - 1)
                link(dve.reciprocal(vr[:, b % 2, :, D:D + 1], den[:, b % 2, :].unsqueeze(2)), base)
                dve.tensor_tensor(vr[:, b % 2, :, 0:D], vp[:, 2 * b:2 * b + 2, :],
                                  vr[:, b % 2, :, D:D + 1].to_broadcast([P, 2, D]), ALU.mult).then_inc(vr_ready, 1)

            def scale_updates(n, b, base):
                dve.wait_ge(u_full, n + 1)
                wait(dve, t3_full, n - 1)
                u = ps[:, 2, :].rearrange("p (t d) -> p t d", t=2)
                link(dve.tensor_scalar(r_sum[:, :], u[:, :, D], SUM_EPS, None, ALU.add), base)
                link(dve.reciprocal(r_sum[:, :], r_sum[:, :]), base)
                dve.tensor_tensor(upd[:, b % 2, :, :], u[:, :, 0:D], r_sum[:, :].unsqueeze(2).to_broadcast([P, 2, D]),
                                  ALU.mult).then_inc(upd_ready, 1)

            def candidate(n, b, base):
                dve.wait_ge(rz_ready, n + 1)
                g = ps[:, 4 + 2 * (b % 2):6 + 2 * (b % 2), :]
                link(dve.scalar_tensor_tensor(tmp, trz[:, b % 2, :, 0:D], 1.0, g[:, :, 3 * D:4 * D], ALU.add, ALU.mult), base)
                dve.scalar_tensor_tensor(new[:, b % 2, :, :], tmp, 0.5, g[:, :, 0:D], ALU.mult, ALU.add
                                         ).then_inc(npre_ready, 1)

            def blend(n, b, base, final):
                dve.wait_ge(new_ready, n + 1)
                hb = h[:, 2 * b:2 * b + 2, :]
                nb = new[:, b % 2, :, :]
                link(dve.tensor_tensor(tmp2, hb, nb, ALU.subtract), base)
                link(dve.scalar_tensor_tensor(tmp2, trz[:, b % 2, :, D:2 * D], 1.0, tmp2, ALU.add, ALU.mult), base)
                dve.scalar_tensor_tensor(hb, tmp2, 0.5, nb, ALU.mult, ALU.add).then_inc(h_ready, 1)
                if not final:
                    dve.wait_ge(h_ready, n + 1)
                    link(squares(b), base)

            def step(n, k, base):
                if 0 <= k - 1:
                    candidate(n - 1, (k - 1) % 8, base)
                if 0 <= k + 2 < BLOCKS:
                    maxima(n + 2, (k + 2) % 8)
                if 0 <= k - 1:
                    blend(n - 1, (k - 1) % 8, base, k - 1 >= BLOCKS - 8)
                    if (k - 1) % 4 == 3 and k - 1 < BLOCKS - 8:
                        b = (k - 1) % 8
                        slot_scale(2 * (b - 3), 2 * b + 2, base)
                if 0 <= k + 1 < BLOCKS:
                    scale_updates(n + 1, (k + 1) % 8, base)
                if 0 <= k + 2 < BLOCKS:
                    scale_values(n + 2, (k + 2) % 8, base)
                if 0 <= k + 4 < BLOCKS:
                    normalise_slots(n + 4, (k + 4) % 8)

            dve.wait_ge(h0_free, 4)
            for b in range(B8):
                link(squares(b))
            slot_scale(0, T, None)
            for k in range(-4, 3):
                step(k, k, None)
            done = links[0]
            PER_IT = 8 * (2 + 2 + 1 + 1 + 1) + 2 * 12
            with dve.Fori(0, ITERS - 1) as it:
                for k in range(3, 11):
                    step(8 * it + k, k, it * PER_IT)
                assert links[0] - done == PER_IT, links[0] - done
            links[0] = done + PER_IT * (ITERS - 1)
            for k in range(8 * (ITERS - 1) + 3, BLOCKS + 1):
                step(k, k, None)

            dve.wait_ge(h_ready, BLOCKS)
            for q in range(4):
                last = dve.tensor_tensor(h[:, 4 * q:4 * q + 4, :], h[:, 4 * q:4 * q + 4, :], x1n[:, 4 * q:4 * q + 4, :], ALU.add)
            link(last)
            stats(0, T, h, OUT_EPS)
            for t in range(T):
                last = dve.tensor_scalar(x2[:, t, :], h[:, t, :], mv[:, t, 0:1], rs[:, t:t + 1],
                                         ALU.subtract, ALU.mult)
                if t % 4 == 3:
                    last.then_inc(x2_ready, 1)
            dve.tensor_copy(iota_p[:, :], iota_pi[:, :])
            dve.tensor_copy(row_f[:, :], row_i[:, :])
            link(dve.tensor_copy(iota_e[:, :], iota_i[:, :]))
            dve.tensor_scalar(e_base[:, :], iota_e[:, :], float(CAP), None, ALU.mult)
            dve.memset(top[:, 2, :], NEG_INF)
            dve.wait_ge(lg_full, 1)
            link(dve.tensor_copy(lg[:, :, :], ps[:, 4, 0:T * E].rearrange("p (t e) -> p t e", t=T)))
            for t in range(T):
                last = dve.max(v8[:, t, :], lg[:, t, :])
            link(last)
            for t in range(T):
                last = dve.max_index(i8[:, t, :], v8[:, t, :], lg[:, t, :])
            link(last)
            link(dve.tensor_copy(pick[:, :, :], i8[:, :, 0:TOPK].rearrange("p t k -> p k t")))
            QN = TOPK * T
            dve.tensor_tensor(hot[:, :, :], pick[:, :, :].rearrange("p k t -> p (k t)").unsqueeze(1).to_broadcast([P, E, QN]),
                              iota_e[:, :].unsqueeze(2).to_broadcast([P, E, QN]), ALU.is_equal).then_inc(hot_ready, 1)
            link(dve.tensor_copy(top[:, 0:2, :], v8[:, :, 0:TOPK].rearrange("p t k -> p k t")))
            link(dve.tensor_tensor(top_m[:, :], top[:, 0, :], top[:, 2, :], ALU.max))
            dve.tensor_tensor(top[:, :, :], top[:, :, :], top_m[:, :].unsqueeze(1).to_broadcast([P, 3, T]), ALU.subtract
                              ).then_inc(top_ready, 1)
            dve.wait_ge(rank_full, 1)
            link(dve.tensor_copy(tot[:, :], ps[:, 6, 0:E * QN]))
            link(dve.tensor_tensor_scan(incl[:, :], seg[:, :, :].rearrange("p e q -> p (e q)"), tot[:, :], 0.0,
                                        ALU.mult, ALU.add))
            link(dve.tensor_tensor(incl[:, :], incl[:, :], tot[:, :], ALU.subtract))
            link(dve.tensor_tensor(incl[:, :], incl[:, :], ps[:, 5, 0:E * QN], ALU.add))
            link(dve.scalar_tensor_tensor(kept[:, :], incl[:, :], float(CAP), hot[:, :, :].rearrange("p e q -> p (e q)"),
                                          ALU.is_lt, ALU.mult))
            by_e = "p (e q) -> p e q"
            link(dve.tensor_tensor(incl[:, :].rearrange(by_e, e=E), incl[:, :].rearrange(by_e, e=E),
                                   e_base[:, :].unsqueeze(2).to_broadcast([P, E, QN]), ALU.add))
            link(dve.tensor_tensor(incl[:, :], incl[:, :], kept[:, :], ALU.mult))
            dve.tensor_reduce(slot[:, :], incl[:, :].rearrange("p (e q) -> p q e", e=E), AX.X, ALU.add)
            link(dve.tensor_reduce(keep[:, :], kept[:, :].rearrange("p (e q) -> p q e", e=E), AX.X, ALU.add))
            link(dve.scalar_tensor_tensor(slot[:, :], keep[:, :], -float(NOWHERE), slot[:, :], ALU.mult, ALU.add))
            link(dve.tensor_scalar(slot_i[:, :], slot[:, :], float(NOWHERE), None, ALU.add))
            dve.tensor_scalar(slot_lo[:, :], slot_i[:, :], P - 1, None, ALU.bitwise_and)
            link(dve.tensor_scalar(slot_hi[:, :], slot_i[:, :], P.bit_length() - 1, None, ALU.logical_shift_right))
            dve.tensor_copy(lo_f[:, :], slot_lo[:, :])
            link(dve.tensor_copy(hi_f[:, :], slot_hi[:, :]))
            dve.tensor_tensor(tile_hot, hi_f[:, :].unsqueeze(2).to_broadcast([P, QN, NT]),
                              iota_p[:, 0:NT].unsqueeze(1).to_broadcast([P, QN, NT]), ALU.is_equal).then_inc(hi_ready, 1)
            dve.wait_ge(expt_ready, 1)
            link(dve.scalar_tensor_tensor(top_m[:, :], expt[:, 2, :], float(E - TOPK), expt[:, 0, :], ALU.mult, ALU.add))
            link(dve.tensor_tensor(top_m[:, :], top_m[:, :], expt[:, 1, :], ALU.add))
            link(dve.reciprocal(top_m[:, :], top_m[:, :]))
            link(dve.tensor_tensor(prob[:, :, :], expt[:, 0:2, :], top_m[:, :].unsqueeze(1).to_broadcast([P, TOPK, T]), ALU.mult))
            link(dve.tensor_tensor(wt[:, :], prob[:, :, :].rearrange("p k t -> p (k t)"), keep[:, :], ALU.mult))
            dve.wait_ge(hi_ready, 1)
            dve.tensor_tensor(hot_hi[:, :, NT:2 * NT], tile_hot, wt[:, :].unsqueeze(2).to_broadcast([P, QN, NT]), ALU.mult
                              ).then_inc(wt_done, 1)
            for k in range(TOPK):
                half = slice(k * T, (k + 1) * T)
                dve.tensor_tensor(hot_lo[:, half, :], lo_f[:, half].unsqueeze(2).to_broadcast([P, T, P]),
                                  iota_p[:, :].unsqueeze(1).to_broadcast([P, T, P]), ALU.is_equal).then_inc(lo_ready, 1)
            dve.wait_ge(table_full, 1)
            dve.tensor_copy(t_wt[:, :], ps[:, 7, NT:2 * NT])
            link(dve.tensor_copy(t_row[:, :], ps[:, 7, 0:NT]))
            link(dve.tensor_scalar(t_tmp[:, :], t_row[:, :], float(N), -float(N), ALU.is_gt, ALU.mult))
            link(dve.scalar_tensor_tensor(t_tmp[:, :], t_row[:, :], -1.0, t_tmp[:, :], ALU.add, ALU.add))
            dve.tensor_scalar(t_src[:, :], t_tmp[:, :], 0.0, None, ALU.max).then_inc(src_ready, 1)
            link(dve.tensor_scalar(t_tmp2[:, :], t_row[:, :], 0.5, float(NOWHERE), ALU.is_lt, ALU.mult))
            dve.scalar_tensor_tensor(t_dst[:, :], t_row[:, :], -1.0, t_tmp2[:, :], ALU.add, ALU.add).then_inc(dst_ready, 1)

            def take_batch(e, r):
                dve.wait_ge(xeT_full, e + 1)
                src = ps[:, 0:2, :].rearrange("p b n -> p (b n)")[:, 0:CAP]
                dve.tensor_copy(xeT[:, r, :], src).then_inc(xeT_free, 1)

            def weigh_output(pair, e, r, reuse):
                dve.wait_ge(pr_full, e + 1)
                if reuse:
                    dve.wait_ge(returned[r], 16 * CT * pair)
                src = ps[:, 6:8, :].rearrange("p b n -> p (b n)")[:, 0:CAP].rearrange("p (j d) -> p j d", j=CT)
                w = t_wt[:, e * CT:(e + 1) * CT] if isinstance(e, int) else t_wt[:, bass.ds(e * CT, CT)]
                dve.tensor_tensor(eo[:, r, :, :], src, w.unsqueeze(2).to_broadcast([P, CT, D]), ALU.mult
                                  ).then_inc(eo_ready, 1)

            def experts(pair, reuse, final):
                for r in range(2):
                    e = 2 * pair + r
                    if not (final and r == 1):
                        take_batch(e + 1, 1 - r)
                    weigh_output(pair, e, r, reuse)

            take_batch(0, 0)
            experts(0, False, False)
            with dve.Fori(1, E // 2 - 1) as pair:
                experts(pair, True, False)
            experts(E // 2 - 1, True, True)
            for q in range(4):
                g0, g1 = 4 * q, 4 * q + 4
                dve.wait_ge(ld_part[q], 32)
                hq = h[:, g0:g1, :]
                link(dve.tensor_tensor(hq, xg[:, g0:g1, :], ctx_t[:, g0:g1, :], ALU.add))
                link(dve.tensor_tensor(hq, hq, x2[:, g0:g1, :], ALU.add))
                stats(g0, g1, h, OUT_EPS)
                for t in range(g0, g1):
                    last = dve.tensor_scalar(h[:, t, :], h[:, t, :], mv[:, t, 0:1], rs[:, t:t + 1],
                                             ALU.subtract, ALU.mult)
                last.then_inc(y_ready, 1)

        @block.scalar
        def _(act):
            def turned(sg):
                act.wait_ge(b0_full, b0_item(sg, 0) + 1)
                act.activation(lnT[:, :], ps[:, 0, :], ACT.Identity, bias=lnv[:, 1:2], scale=lnv[:, 0:1]
                               ).then_inc(b0_free, 1)

            def query(sg, hp):
                act.wait_ge(b0_full, b0_item(sg, 1 + hp) + 1)
                act.activation(qT[:, hp, :], ps[:, 0, :], ACT.Copy).then_inc(b0_free, 1)

            def key_high(sg, first, hp):
                act.wait_ge(b1_full, b1_item(sg, first, hp) + 1)
                act.activation(kz[DH:P, hp, :, 1, :], ps[DH:P, 1, :].rearrange("p (g n) -> p g n", g=GL), ACT.Copy
                               ).then_inc(b1_free_act, 1)

            def value_low(sg, g):
                act.wait_ge(b0_full, b0_item(sg, 1 + HP + g) + 1)
                act.activation(v[:, g, 0:512], ps[:, 0, :], ACT.Copy).then_inc(b0_free, 1)

            def diagonal(n, g, reuse):
                act.wait_ge(s_full1, n + 1)
                if reuse:
                    act.wait_ge(shifted, n - 1)
                src = ps[:, 4:6, :].rearrange("p b (h k) -> p (b h) k", h=4)
                for q in range(4):
                    r = slice(QB * q, QB * q + QB)
                    last = act.activation(sc[r, g % 2, 8:16, :], src[r, :, QB * q:QB * q + QB], ACT.Copy)
                last.then_inc(s_free1, 1)

            def exponent(n, g, reuse):
                act.wait_ge(shifted, n + 1)
                if reuse:
                    act.wait_ge(probs, n - 1)
                act.activation(pc[:, g % 2, :, :], sc[:, g % 2, :, :], ACT.Exp, scale=float(DH) ** -0.5
                               ).then_inc(exped, 1)

            def expand(n, g, reuse):
                act.wait_ge(probs, n + 1)
                if reuse:
                    act.wait_ge(pv1, n - 1)
                for q in range(4):
                    r = slice(QB * q, QB * q + QB)
                    last = act.activation(pbd[r, g % 2, :, QB * q:QB * q + QB], pt[r, g % 2, :, :], ACT.Copy)
                last.then_inc(spread, 1)

            def context_low(n):
                act.wait_ge(pv0, n + 1)
                act.activation(ctxT[:, 0:4, :], ps[:, 6, :].rearrange("p (h n) -> p h n", h=4), ACT.Copy
                               ).then_inc(ctx0, 1)

            def supergroup(sg, first):
                turned(sg)
                for hp in range(HP):
                    query(sg, hp)
                    key_high(sg, first, hp)
                    if hp == 1 and not first:
                        expand(GL * sg - 1, 3, True)
                if not first:
                    context_low(GL * sg - 2)
                diagonal(GL * sg, 0, not first)
                exponent(GL * sg, 0, not first)
                if not first:
                    context_low(GL * sg - 1)
                expand(GL * sg, 0, not first)
                diagonal(GL * sg + 1, 1, not first)
                exponent(GL * sg + 1, 1, not first)
                for g in range(GL):
                    value_low(sg, g)
                    if g == 1:
                        expand(GL * sg + 1, 1, not first)
                context_low(GL * sg)
                diagonal(GL * sg + 2, 2, True)
                exponent(GL * sg + 2, 2, True)
                expand(GL * sg + 2, 2, True)
                context_low(GL * sg + 1)
                diagonal(GL * sg + 3, 3, True)
                exponent(GL * sg + 3, 3, True)

            act.dma_start(lnv[:, 0:1], ln_scale.rearrange("(p a) -> p a", a=1)).then_inc(ld_vec, 16)
            act.dma_start(lnv[:, 1:2], ln_bias.rearrange("(p a) -> p a", a=1)).then_inc(ld_vec, 16)
            act.dma_start(lnv[:, 2:3], slot_w.rearrange("(p a) -> p a", a=1)).then_inc(ld_in, 16)
            act.dma_start(lnv[:, 3:4], input_w.rearrange("(p a) -> p a", a=1)).then_inc(ld_in, 16)
            for k, w in enumerate((Wq, Wk, Wv)):
                act.dma_start(w_nat[:, k, :], w).then_inc(ld_small, 16)
            act.dma_start(w_nat[:, 3:6, :], wih.rearrange("(g p) c -> p g c", p=P)).then_inc(ld_small, 16)
            act.dma_start(w_nat[:, 6:9, :], whh.rearrange("(g p) c -> p g c", p=P)).then_inc(ld_small, 16)
            for k in range(3):
                act.dma_start(b_rows[k:k + 1, 0, :], bih.rearrange("(a n) -> a n", a=1)).then_inc(ld_bias, 16)
                act.dma_start(b_rows[k:k + 1, 1, :], bhh.rearrange("(a n) -> a n", a=1)).then_inc(ld_bias, 16)
            act.dma_start(wg[:, :], w_g).then_inc(ld_bias, 16)
            act.wait_ge(ld_vec, 32)
            act.wait_ge(zeroed, 3)
            supergroup(0, True)
            with act.Fori(1, SG) as sg:
                supergroup(sg, False)
            expand(T - 1, 3, True)
            context_low(T - 2)
            context_low(T - 1)

            for q in range(4):
                act.wait_ge(cT_full, q + 1)
                act.activation(cT[:, 512 * q:512 * q + 512], ps[:, 2 + q, :], ACT.Copy).then_inc(cT_free, 1)
            act.wait_ge(ld_in, 32)
            act.activation(lnv[:, 4:5], lnv[:, 2:3], ACT.Copy, scale=float(D) ** -0.5).then_inc(w_done_act, 1)
            act.wait_ge(w_done_act, 1)
            for q in range(4):
                act.wait_ge(kq_full, q + 1)
                act.activation(kq[:, 512 * q:512 * q + 512], ps[:, 2 + q, :], ACT.Copy, scale=lnv[:, 4:5]
                               ).then_inc(kq_free, 1)
            for q in range(4):
                act.wait_ge(x1T_full, q + 1)
                for g in range(4):
                    base = (4 * q + g) * 16
                    last = act.activation(x1T[:, :].rearrange("p (s b) -> p s b", s=S)[:, :, base:base + 16],
                                          ps[:, q, g * P:(g + 1) * P].rearrange("p (l s) -> p s l", s=S), ACT.Copy)
                last.then_inc(x1T_free, 1)
            for q in range(4):
                act.wait_ge(h0_full, q + 1)
                act.activation(h[:, 4 * q:4 * q + 4, :], ps[:, 4 + q, :].rearrange("p (t d) -> p t d", t=4), ACT.Copy
                               ).then_inc(h0_free, 1)

            def keep_turned(n, b):
                act.wait_ge(t12_full, n + 1)
                act.activation(snh[:, b % 4, :], ps[:, 0, :], ACT.Copy).then_inc(snh_ready, 1)

            def exponents(n, b):
                act.wait_ge(negmax, n + 1)
                wait(act, u_full, n - 1)
                wait(act, vr_ready, n - 1)
                for m in range(2):
                    last = act.activation(e_m[:, b % 2, m, :], ps[:, 1, m * 256:(m + 1) * 256], ACT.Exp,
                                          bias=n_mx[:, b % 2, m:m + 1], accum_out=den[:, b % 2, m:m + 1])
                last.then_inc(exB, 1)

            def keep_updates(n, b):
                act.wait_ge(t3_full, n + 1)
                act.activation(updT[:, b % 2, :], ps[:, 3, 0:256], ACT.Copy).then_inc(updT_ready, 1)

            def half_tanh(n, b):
                act.wait_ge(g_full, n + 1)
                wait(act, h_ready, n - 1)
                act.activation(trz[:, b % 2, :, :], ps[:, 4 + 2 * (b % 2):6 + 2 * (b % 2), D:3 * D], ACT.Tanh, scale=0.5
                               ).then_inc(rz_ready, 1)

            def new_tanh(n, b):
                act.wait_ge(npre_ready, n + 1)
                act.activation(new[:, b % 2, :, :], new[:, b % 2, :, :], ACT.Tanh).then_inc(new_ready, 1)

            def step(n, k):
                if 0 <= k < BLOCKS:
                    keep_updates(n, k % 8)
                if 0 <= k - 1:
                    half_tanh(n - 1, (k - 1) % 8)
                if 0 <= k + 3 < BLOCKS:
                    keep_turned(n + 3, (k + 3) % 8)
                if 0 <= k - 1:
                    new_tanh(n - 1, (k - 1) % 8)
                if 0 <= k + 2 < BLOCKS:
                    exponents(n + 2, (k + 2) % 8)

            for k in range(-3, 3):
                step(k, k)
            with act.Fori(0, ITERS - 1) as it:
                for k in range(3, 11):
                    step(8 * it + k, k)
            for k in range(8 * (ITERS - 1) + 3, BLOCKS + 1):
                step(k, k)

            for q in range(4):
                act.wait_ge(x2T_full, q + 1)
                act.activation(x1T[:, 512 * q:512 * q + 512], ps[:, q, :], ACT.Copy).then_inc(x2T_free, 1)
            act.wait_ge(top_ready, 1)
            act.activation(expt[:, :, :], top[:, :, :], ACT.Exp).then_inc(expt_ready, 1)

            def gelu(pair, r, e):
                for f in range(FC):
                    act.wait_ge(fc_full, FC * e + f + 1)
                    wait(act, pr_full, e - 1)
                    b0 = 2 + 2 * (f % 2)
                    src = ps[:, b0:b0 + 2, :].rearrange("p b n -> p (b n)")[:, 0:CAP]
                    act.activation(hT[:, r, f, :], src, ACT.Gelu).then_inc(gelu_done, 1)

            def experts(pair):
                for r in range(2):
                    gelu(pair, r, 2 * pair + r)

            experts(0)
            with act.Fori(1, E // 2) as pair:
                experts(pair)


_INS = ['x', 'ctx_1024', 'L0_attn_ln_scale', 'L0_attn_ln_bias', 'L0_attn_qkv_kernel', 'L0_attn_out_kernel',
        'L0_xattn_Wq', 'L0_xattn_Wk', 'L0_xattn_Wv', 'L0_xattn_gru_wih', 'L0_xattn_gru_whh', 'L0_xattn_gru_bih',
        'L0_xattn_gru_bhh', 'L0_xattn_slot_norm_w', 'L0_xattn_input_norm_w', 'L0_ffn_w_g', 'L0_ffn_c_fc',
        'L0_ffn_c_proj']


def kernel(**inputs):
    import numpy as np
    import concourse.bacc as bacc
    from concourse.bass_utils import run_bass_kernel_spmd

    nc = bacc.Bacc("TRN2", target_bir_lowering=False, num_devices=1)
    arrays, args = {}, []
    for name in _INS:
        a = np.ascontiguousarray(inputs[name])
        arrays[f"in_{name}"] = a
        args.append(nc.dram_tensor(f"in_{name}", a.shape, mybir.dt.from_np(a.dtype), kind="ExternalInput").ap())
    args.append(nc.dram_tensor("out", (S, B, D), F32, kind="ExternalOutput").ap())
    build(nc, *args)
    r = run_bass_kernel_spmd(nc, [arrays], core_ids=[0])
    return r.results[0]["out"]
```

```python
from contextlib import ExitStack

import concourse.bass as bass
from concourse import mybir

F32 = mybir.dt.float32
BF16 = mybir.dt.bfloat16
I32 = mybir.dt.int32
U32 = mybir.dt.uint32
ALU = mybir.AluOpType
ACT = mybir.ActivationFunctionType
AX = mybir.AxisListType

P = 128
B8 = 8
S, B, D = 8, 256, 128
N = S * B
T = N // P
H, DH = 16, 64
HP = H // 2
SG = 4
GL = T // SG
QB = 32
ITERS = 3
E, TOPK, F = 8, 2, 512
CAP = int(TOPK * 1.25 * N / E)
CAP += CAP % 2
CT = CAP // P
NT = E * CT
FC = F // P
NOWHERE = 1 << 20
OFF = -1.0e30
NEG_INF = -1.0e9
LN_EPS, RMS_EPS, SUM_EPS, OUT_EPS = 1e-6, 1e-6, 1e-6, 1e-5


def build(nc, x, ctx_in, ln_scale, ln_bias, qkv_w, out_w, Wq, Wk, Wv, wih, whh, bih, bhh,
          slot_w, input_w, w_g, c_fc, c_proj, out):
    with ExitStack() as ctx:
        def sb(name, shape, dt=F32):
            return ctx.enter_context(nc.sbuf_tensor(name, shape, dt))

        def sem(name):
            return ctx.enter_context(nc.semaphore(name))

        ps = ctx.enter_context(nc.psum_tensor("ps", [P, 8, 512], F32))

        xg = sb("xg", [P, T, D])
        ctx_t = sb("ctx_t", [P, T, D])
        wqkv = sb("wqkv", [P, 3 * H * DH])
        wo = sb("wo", [P, HP, D])
        x1T = sb("x1T", [P, N])
        x1n = sb("x1n", [P, T, D])
        h = wqkv[:, 0:N].rearrange("p (t d) -> p t d", t=T)
        kq = sb("kq", [P, N])
        vp = sb("vp", [P, T, D])
        ident = sb("ident", [P, P])
        full_mask = sb("full_mask", [P, P])
        mask = sb("mask", [P, QB])
        ones_b = sb("ones_b", [P, P], BF16)
        before = sb("before", [P, P], BF16)
        zeros = sb("zeros", [P, 8 * D])
        lnv = sb("lnv", [P, 8])
        st = sb("st", [P, T, 6])
        mv = sb("mv", [P, T, 2])
        var = sb("var", [P, T])
        rs = sb("rs", [P, T])
        rt = sb("rt", [P, T])

        xn = sb("xn", [P, GL, D])
        lnT = sb("lnT", [P, GL * P])
        pool_a = sb("pool_a", [P, HP * 512])
        pool_k = sb("pool_k", [P, HP * GL * 2 * P])
        pool_v = sb("pool_v", [P, GL * H * DH])
        pool_p = sb("pool_p", [P, 2 * H * P])
        qT = pool_a[:, :].rearrange("p (h n) -> p h n", h=HP)
        kz = pool_k[:, :].rearrange("p (h g z n) -> p h g z n", h=HP, g=GL, z=2)
        v = pool_v[:, :].rearrange("p (g n) -> p g n", g=GL)
        pbd = pool_p[:, :].rearrange("p (r h n) -> p r h n", r=2, h=H)
        sc = sb("sc", [P, 2, H, QB])
        pc = sb("pc", [P, 2, H, QB])
        pt = sb("pt", [P, 2, H, QB])
        mx = sb("mx", [P, H])
        sm = sb("sm", [P, H])
        ctxT = sb("ctxT", [P, HP, P])

        w_nat = sb("w_nat", [P, 9, D])
        w_kq = sb("w_kq", [P, D])
        w_v = sb("w_v", [P, D])
        w_ih = sb("w_ih", [P, 3 * D])
        w_hh = sb("w_hh", [P, 3 * D])
        b_rows = sb("b_rows", [3, 2, 3 * D])
        b_sum = sb("b_sum", [3, 4 * D])
        b_part = sb("b_part", [3, 4 * D])
        b_cut = sb("b_cut", [3, 4 * D], BF16)
        bias = sb("bias", [P, 4 * D], BF16)
        wg = sb("wg", [P, E])
        cfc = sb("cfc", [P, 2, F])
        cpr = sb("cpr", [P, 2, FC, D])
        c_st = sb("c_st", [P, T, 6])
        c_mv = sb("c_mv", [P, T, 2])
        c_r = sb("c_r", [P, T])
        sq = sb("sq", [P, T])
        r_h = sb("r_h", [P, T])

        cT = pool_a[:, 0:N]
        snh = pool_a[:, N:N + 4 * 512].rearrange("p (r n) -> p r n", r=4)
        at = [0]

        def carve(pool, n):
            at[0] += n
            assert at[0] <= pool.shape[1], at[0]
            return pool[:, at[0] - n:at[0]]

        e_m = carve(pool_k, 1024).rearrange("p (r m k) -> p r m k", r=2, m=2)
        vr = carve(pool_k, 4 * (D + 1)).rearrange("p (r m d) -> p r m d", r=2, m=2)
        upd = carve(pool_k, 512).rearrange("p (r t d) -> p r t d", r=2, t=2)
        updT = carve(pool_k, 512).rearrange("p (r n) -> p r n", r=2)
        trz = carve(pool_k, 1024).rearrange("p (r t d) -> p r t d", r=2, t=2)
        new = carve(pool_k, 512).rearrange("p (r t d) -> p r t d", r=2, t=2)
        sn = carve(pool_k, 512).rearrange("p (r t d) -> p r t d", r=2, t=2)
        tmp = carve(pool_k, 256).rearrange("p (t d) -> p t d", t=2)
        tmp2 = carve(pool_k, 256).rearrange("p (t d) -> p t d", t=2)
        sq_out = carve(pool_k, 256)
        n_mx = sb("n_mx", [P, 2, 2])
        den = sb("den", [P, 2, 2])
        r_sum = sb("r_sum", [P, 2])

        x2 = pool_v[:, 0:T * D].rearrange("p (t c) -> p t c", t=T)
        hot_lo = pool_p[:, :].rearrange("p (q l) -> p q l", l=P)
        hot_hi = pool_a[:, :].rearrange("p (q l) -> p q l", l=P)
        at[0] = 0
        xe = carve(pool_k, 2 * CAP).rearrange("p (r j c) -> p r j c", r=2, j=CT)
        xeT = carve(pool_k, 2 * CAP).rearrange("p (r n) -> p r n", r=2)
        hT = carve(pool_k, 2 * FC * CAP).rearrange("p (r f n) -> p r f n", r=2, f=FC)
        eo = pool_a[:, 0:2 * CAP].rearrange("p (r j d) -> p r j d", r=2, j=CT)
        tile_hot = pool_v[:, T * D:T * D + TOPK * T * NT].rearrange("p (q l) -> p q l", l=NT)
        part = [xg, ctx_t]
        row_i = sb("row_i", [P, TOPK * T], I32)
        row_f = sb("row_f", [P, TOPK * T])
        iota_pi = sb("iota_pi", [P, P], I32)
        iota_p = sb("iota_p", [P, P])
        slot_hi = sb("slot_hi", [P, TOPK * T], I32)
        slot_lo = sb("slot_lo", [P, TOPK * T], I32)
        hi_f = sb("hi_f", [P, TOPK * T])
        lo_f = sb("lo_f", [P, TOPK * T])
        wt = sb("wt", [P, TOPK * T])
        t_row = sb("t_row", [P, NT])
        t_wt = sb("t_wt", [P, NT])
        t_tmp = sb("t_tmp", [P, NT])
        t_tmp2 = sb("t_tmp2", [P, NT])
        t_dst = sb("t_dst", [P, NT], I32)
        t_src = sb("t_src", [P, NT], I32)
        iota_i = sb("iota_i", [P, E], I32)
        iota_e = sb("iota_e", [P, E])
        e_base = sb("e_base", [P, E])
        seg = sb("seg", [P, E, TOPK * T])
        lg = sb("lg", [P, T, E])
        v8 = sb("v8", [P, T, 8])
        i8 = sb("i8", [P, T, 8], U32)
        pick = sb("pick", [P, TOPK, T])
        hot = sb("hot", [P, E, TOPK * T], BF16)
        top = sb("top", [P, 3, T])
        top_m = sb("top_m", [P, T])
        expt = sb("expt", [P, 3, T])
        prob = sb("prob", [P, TOPK, T])
        tot = sb("tot", [P, E * TOPK * T])
        incl = sb("incl", [P, E * TOPK * T])
        kept = sb("kept", [P, E * TOPK * T])
        slot = sb("slot", [P, TOPK * T])
        keep = sb("keep", [P, TOPK * T])
        slot_i = sb("slot_i", [P, TOPK * T], I32)
        x2_rows = nc.dram_tensor("x2_rows", [N, D], F32, kind="Internal").ap()
        results = nc.dram_tensor("results", [TOPK * N, D], F32, kind="Internal").ap()

        ld_x, ld_x_rest, ld_ctx, ld_w, ld_wo, ld_vec = (sem(n) for n in ("ld_x", "ld_x_rest", "ld_ctx", "ld_w", "ld_wo", "ld_vec"))
        consts = sem("consts")
        zeroed = sem("zeroed")
        dve_link = sem("dve_link")
        xn_ready = sem("xn_ready")
        b0_full, b0_free = sem("b0_full"), sem("b0_free")
        b1_full, b1_free_dve, b1_free_act = sem("b1_full"), sem("b1_free_dve"), sem("b1_free_act")
        o_full, o_free = sem("o_full"), sem("o_free")
        s_full0, s_full1, s_free0, s_free1 = sem("s_full0"), sem("s_full1"), sem("s_free0"), sem("s_free1")
        shifted, exped, probs, spread = sem("shifted"), sem("exped"), sem("probs"), sem("spread")
        pv0, pv1, ctx0, ctx1 = sem("pv0"), sem("pv1"), sem("ctx0"), sem("ctx1")
        ld_small, ld_bias, ld_in = sem("ld_small"), sem("ld_bias"), sem("ld_in")
        turned_w, w_done_dve, w_done_act = sem("turned_w"), sem("w_done_dve"), sem("w_done_act")
        c_scaled, c_rs = sem("c_scaled"), sem("c_rs")
        cT_full, cT_free, kq_full, kq_free, v_full, v_free = (sem(n) for n in ("cT_full", "cT_free", "kq_full", "kq_free", "v_full", "v_free"))
        x1_ready, x1T_full, x1T_free, h0_full, h0_free, x1n_ready = (sem(n) for n in (
            "x1_ready", "x1T_full", "x1T_free", "h0_full", "h0_free", "x1n_ready"))
        (sn_ready, t12_full, snh_ready, sB_full, negmax, exB, vr_ready, u_full, upd_ready, t3_full, updT_ready,
         g_full, rz_ready, npre_ready, new_ready, h_ready) = (sem(n) for n in (
             "sn_ready", "t12_full", "snh_ready", "sB_full", "negmax", "exB", "vr_ready", "u_full", "upd_ready",
             "t3_full", "updT_ready", "g_full", "rz_ready", "npre_ready", "new_ready", "h_ready"))
        r_zeroed, x2_stored, padded, row_done, wt_done, table_full, dst_ready, src_ready = (sem(n) for n in (
            "r_zeroed", "x2_stored", "padded", "row_done", "wt_done", "table_full", "dst_ready", "src_ready"))
        lo_ready, hi_ready, idx_ready = sem("lo_ready"), sem("hi_ready"), sem("idx_ready")
        x2_ready, x2T_full, x2T_free, lg_full = (sem(n) for n in ("x2_ready", "x2T_full", "x2T_free", "lg_full"))
        hot_ready, rank_full, top_ready, expt_ready = (sem(n) for n in (
            "hot_ready", "rank_full", "top_ready", "expt_ready"))
        ld_xe0, ld_xe1, ld_we0, ld_we1 = (sem(n) for n in ("ld_xe0", "ld_xe1", "ld_we0", "ld_we1"))
        ld_xe, ld_we = [ld_xe0, ld_xe1], [ld_we0, ld_we1]
        xeT_full, xeT_free, fc_full, gelu_done, pr_full, eo_ready, returned0, returned1 = (sem(n) for n in (
            "xeT_full", "xeT_free", "fc_full", "gelu_done", "pr_full", "eo_ready", "returned0", "returned1"))
        returned = [returned0, returned1]
        ld_part = [sem(f"ld_part{q}") for q in range(4)]
        y_ready = sem("y_ready")
        stored = sem("stored")

        block = ctx.enter_context(nc.Block())

        B0_ITEMS = 1 + HP + GL
        B1_ITEMS = HP + GL

        def b0_item(sg, k):
            return B0_ITEMS * sg + k

        def b1_item(sg, k):
            return B1_ITEMS * sg + k

        def wait(eng, s, value):
            if not (isinstance(value, int) and value <= 0):
                eng.wait_ge(s, value)

        BLOCKS = ITERS * B8

        @block.sync
        def _(sp):
            def load_tokens(g0, g1, loaded):
                for g in range(g0, g1):
                    sp.dma_start(xg[:, g, :], x[:, g * 16:(g + 1) * 16, :].rearrange("s l c -> l s c")
                                 ).then_inc(loaded, 16)

            load_tokens(0, GL, ld_x)
            sp.dma_start(wqkv[:, :], qkv_w.rearrange("c t k -> c (t k)")).then_inc(ld_w, 16)
            load_tokens(GL, T, ld_x_rest)
            sp.dma_start(wo[:, :, :], out_w.rearrange("(h k) c -> k h c", k=P)).then_inc(ld_wo, 16)
            sp.dma_start(ctx_t[:, :, :], ctx_in.rearrange("s (t p) c -> p (s t) c", p=P)).then_inc(ld_ctx, 16)
            for k, w in enumerate((Wq, Wk, Wv)):
                sp.dma_start(w_nat[:, k, :], w).then_inc(ld_small, 16)
            sp.dma_start(w_nat[:, 3:6, :], wih.rearrange("(g p) c -> p g c", p=P)).then_inc(ld_small, 16)
            sp.dma_start(w_nat[:, 6:9, :], whh.rearrange("(g p) c -> p g c", p=P)).then_inc(ld_small, 16)
            for k in range(3):
                sp.dma_start(b_rows[k:k + 1, 0, :], bih.rearrange("(a n) -> a n", a=1)).then_inc(ld_bias, 16)
                sp.dma_start(b_rows[k:k + 1, 1, :], bhh.rearrange("(a n) -> a n", a=1)).then_inc(ld_bias, 16)
            sp.dma_start(wg[:, :], w_g).then_inc(ld_bias, 16)
            sp.wait_ge(zeroed, 4)
            for a in range(TOPK * N // (P * 8)):
                sp.dma_start(results[a * P * 8:(a + 1) * P * 8, :].rearrange("(p j) c -> p j c", j=8),
                             zeros[:, :].rearrange("p (j c) -> p j c", j=8)).then_inc(r_zeroed, 16)

            def load_weights(e, r, reuse):
                if reuse:
                    sp.wait_ge(pr_full, e - 1)
                sp.dma_start(cfc[:, r, :], c_fc[e]).then_inc(ld_we[r], 16)
                sp.dma_start(cpr[:, r, :, :], c_proj[e].rearrange("(f p) d -> p f d", p=P)).then_inc(ld_we[r], 16)

            load_weights(0, 0, False)
            load_weights(1, 1, False)
            for half in range(2):
                sp.wait_ge(x2_ready, 2 * half + 2)
                sp.dma_start(x2_rows[half * N // 2:(half + 1) * N // 2, :].rearrange("(t p) c -> p t c", p=P),
                             x2[:, half * T // 2:(half + 1) * T // 2, :]).then_inc(x2_stored, 16)
            for e in range(2, E):
                load_weights(e, e % 2, True)
            for r in range(2):
                sp.wait_ge(returned[r], 16 * NT // 2)
            for q in range(4):
                for k in range(TOPK):
                    sp.dma_start(part[k][:, 4 * q:4 * q + 4, :],
                                 results[k * N + q * 512:k * N + (q + 1) * 512, :].rearrange("(t p) c -> p t c", p=P)
                                 ).then_inc(ld_part[q], 16)
            out_t = out.rearrange("s (t p) c -> p (s t) c", p=P)
            for q in range(4):
                sp.wait_ge(y_ready, q + 1)
                sp.dma_start(out_t[:, 4 * q:4 * q + 4, :], h[:, 4 * q:4 * q + 4, :]).then_inc(stored, 16)
            sp.wait_ge(stored, 64)

        @block.gpsimd
        def _(pool):
            pool.memset(ident[:, :], 0.0).then_inc(consts, 1)
            pool.memset(full_mask[:, :], 0.0).then_inc(consts, 1)
            pool.wait_ge(consts, 2)
            pool.affine_select(out=ident[:, :], in_=ident[:, :], compare_op=ALU.not_equal, fill=1.0,
                               base=0, pattern=[[-1, P]], channel_multiplier=1).then_inc(consts, 1)
            pool.affine_select(out=full_mask[:, :], in_=full_mask[:, :], compare_op=ALU.is_ge, fill=OFF,
                               base=0, pattern=[[-1, P]], channel_multiplier=1).then_inc(consts, 1)
            pool.wait_ge(consts, 4)
            cols = full_mask[:, :].rearrange("p (a s) -> p a s", s=S)
            pool.affine_select(out=cols, in_=cols, compare_op=ALU.is_ge, fill=OFF,
                               base=S - 1, pattern=[[S, P // S], [0, S]], channel_multiplier=-1).then_inc(consts, 1)
            pool.memset(kz[0:DH, :, :, 1, :], 0.0).then_inc(zeroed, 1)
            pool.memset(pool_p[:, :], 0.0).then_inc(zeroed, 1)
            pool.memset(zeros[:, :], 0.0).then_inc(zeroed, 1)
            pool.memset(ones_b[:, :], 1.0).then_inc(consts, 1)
            pool.memset(before[:, :], 1.0).then_inc(consts, 1)
            pool.memset(bias[:, :], 0.0).then_inc(consts, 1)
            pool.memset(seg[:, :, :], 1.0).then_inc(consts, 1)
            pool.wait_ge(consts, 9)
            pool.affine_select(out=before[:, :], in_=before[:, :], compare_op=ALU.is_gt, fill=0.0,
                               base=0, pattern=[[1, P]], channel_multiplier=-1).then_inc(consts, 1)
            pool.memset(seg[:, :, 0:1], 0.0).then_inc(consts, 1)
            pool.iota(iota_i[:, :], pattern=[[1, E]], base=0, channel_multiplier=0).then_inc(consts, 1)
            pool.iota(row_i[:, :], pattern=[[P, TOPK * T]], base=1, channel_multiplier=1).then_inc(consts, 1)
            pool.iota(iota_pi[:, :], pattern=[[1, P]], base=0, channel_multiplier=0).then_inc(consts, 1)

            pool.wait_ge(c_rs, 1)
            for g in range(4):
                rows4 = ctx_t[:, 4 * g:4 * g + 4, :]
                pool.tensor_tensor(rows4, rows4, c_r[:, 4 * g:4 * g + 4].unsqueeze(2).to_broadcast([P, 4, D]), ALU.mult
                                   ).then_inc(c_scaled, 1)
            pool.wait_ge(h0_free, 4)
            pool.tensor_copy(x1n[:, :, :], h[:, :, :]).then_inc(x1n_ready, 1)

            pool.wait_ge(h_ready, BLOCKS)
            pool.memset(hot_hi[:, :, 2 * NT:P], 0.0).then_inc(padded, 1)
            pool.wait_ge(hi_ready, 1)
            pool.tensor_tensor(hot_hi[:, :, 0:NT], tile_hot, row_f[:, :].unsqueeze(2).to_broadcast([P, TOPK * T, NT]),
                               ALU.mult).then_inc(row_done, 1)

            def fetch(e, r):
                if e >= 2:
                    pool.wait_ge(xeT_full, e - 1)
                for j in range(CT):
                    c = e * CT + j
                    pool.indirect_dma_start(xe[:, r, j, :], None, x2_rows[:, :],
                                            bass.IndirectOffsetOnAxis(t_src[:, c:c + 1], 0),
                                            bounds_check=N - 1, oob_is_err=False).then_inc(ld_xe[r], 16)

            def send_back(e, r):
                pool.wait_ge(eo_ready, e + 1)
                for j in range(CT):
                    c = e * CT + j
                    pool.indirect_dma_start(results[:, :], bass.IndirectOffsetOnAxis(t_dst[:, c:c + 1], 0),
                                            eo[:, r, j, :], None, bounds_check=TOPK * N - 1, oob_is_err=False
                                            ).then_inc(returned[r], 16)

            pool.wait_ge(x2_stored, 32)
            pool.wait_ge(src_ready, 1)
            fetch(0, 0)
            fetch(1, 1)
            pool.wait_ge(r_zeroed, 16 * TOPK * N // (P * 8))
            pool.wait_ge(dst_ready, 1)
            for e in range(E):
                if e + 2 < E:
                    fetch(e + 2, e % 2)
                send_back(e, e % 2)

        @block.tensor
        def _(pe):
            def turn_tokens(sg):
                pe.wait_ge(xn_ready, sg + 1)
                wait(pe, b0_free, b0_item(sg, 0))
                for g in range(GL):
                    last = pe.transpose(ps[:, 0, g * P:(g + 1) * P], xn[:, g, :], ident[:, :])
                last.then_inc(b0_full, 1)

            def project(sg):
                for hp in range(HP):
                    pe.wait_ge(b0_free, b0_item(sg, 1 + hp))
                    pe.matmul(ps[:, 0, :], wqkv[:, hp * P:(hp + 1) * P], lnT[:, :], start=True, stop=True
                              ).then_inc(b0_full, 1)
                    wait(pe, b1_free_dve, b1_item(sg, hp))
                    wait(pe, b1_free_act, HP * sg + hp)
                    pe.matmul(ps[:, 1, :], wqkv[:, (HP + hp) * P:(HP + hp + 1) * P], lnT[:, :],
                              start=True, stop=True).then_inc(b1_full, 1)

            def values(sg):
                for g in range(GL):
                    pe.wait_ge(b0_free, b0_item(sg, 1 + HP + g))
                    pe.matmul(ps[:, 0, :], lnT[:, g * P:(g + 1) * P], wqkv[:, 2 * H * DH:2 * H * DH + 512],
                              start=True, stop=True).then_inc(b0_full, 1)
                    pe.wait_ge(b1_free_dve, b1_item(sg, HP + g))
                    if g == 0:
                        pe.wait_ge(b1_free_act, HP * sg + HP)
                    pe.matmul(ps[:, 1, :], lnT[:, g * P:(g + 1) * P], wqkv[:, 2 * H * DH + 512:3 * H * DH],
                              start=True, stop=True).then_inc(b1_full, 1)

            def scores(sg, first, g):
                n = GL * sg + g
                if g == 0:
                    pe.wait_ge(b0_free, b0_item(sg, 1 + HP))
                    pe.wait_ge(b1_free_dve, b1_item(sg, HP))
                    pe.wait_ge(b1_free_act, HP * sg + HP)
                for half in range(2):
                    if not (first and g == 0):
                        pe.wait_ge(s_free1 if half else s_free0, n)
                    for k in range(4):
                        hp = 4 * half + k
                        last = pe.matmul(ps[:, 2 + 2 * half + k // 2, (k % 2) * 256:(k % 2) * 256 + 256],
                                         qT[:, hp, g * P:(g + 1) * P],
                                         kz[:, hp, g, :, :].rearrange("p z n -> p (z n)"), start=True, stop=True)
                    last.then_inc(s_full1 if half else s_full0, 1)

            def weigh(sg, g, first):
                n = GL * sg + g
                pe.wait_ge(spread, n + 1)
                pe.wait_ge(b0_free, b0_item(sg, 2 + HP + g))
                pe.wait_ge(b1_free_dve, b1_item(sg, HP + 1 + g))
                for half in range(2):
                    if not (first and g == 0):
                        pe.wait_ge(ctx1 if half else ctx0, n)
                        if half == 1:
                            pe.wait_ge(o_free, n)
                    for hd in range(8 * half, 8 * half + 8):
                        lo = (hd % 2) * DH
                        last = pe.matmul(ps[lo:lo + DH, 6 + half, (hd // 2 % 4) * P:(hd // 2 % 4 + 1) * P],
                                         v[:, g, hd * DH:(hd + 1) * DH], pbd[:, g % 2, hd, :],
                                         start=True, stop=True)
                    last.then_inc(pv1 if half else pv0, 1)

            def output(n):
                pe.wait_ge(ld_wo, 16)
                pe.wait_ge(ctx0, n + 1)
                pe.wait_ge(ctx1, n + 1)
                for hp in range(HP):
                    last = pe.matmul(ps[:, 7, 0:P], ctxT[:, hp, :], wo[:, hp, :], start=(hp == 0), stop=(hp == HP - 1))
                last.then_inc(o_full, 1)

            def supergroup(sg, first, final):
                project(sg)
                if not first:
                    weigh(sg - 1, 2, False)
                scores(sg, first, 0)
                if not first:
                    output(GL * sg - 2)
                    weigh(sg - 1, 3, False)
                scores(sg, first, 1)
                if not first:
                    output(GL * sg - 1)
                values(sg)
                weigh(sg, 0, first)
                scores(sg, first, 2)
                if not final:
                    turn_tokens(sg + 1)
                output(GL * sg)
                weigh(sg, 1, first)
                scores(sg, first, 3)
                output(GL * sg + 1)

            pe.wait_ge(consts, 5)
            turn_tokens(0)
            pe.wait_ge(ld_w, 16)
            pe.wait_ge(zeroed, 4)
            supergroup(0, True, False)
            with pe.Fori(1, SG - 1) as sg:
                supergroup(sg, False, False)
            supergroup(SG - 1, False, True)
            weigh(SG - 1, 2, False)
            output(T - 2)
            weigh(SG - 1, 3, False)
            output(T - 1)

            pe.wait_ge(ld_small, 16 * 5)
            pe.wait_ge(s_free0, T)
            pe.wait_ge(s_free1, T)
            pe.matmul(ps[:, 2, 0:P], w_nat[:, 1, :], w_nat[:, 0, :], start=True, stop=True)
            for k in range(2, 5):
                pe.transpose(ps[:, 2, (k - 1) * P:k * P], w_nat[:, k, :], ident[:, :])
            for k in range(5, 9):
                last = pe.transpose(ps[:, 3, (k - 5) * P:(k - 4) * P], w_nat[:, k, :], ident[:, :])
            last.then_inc(turned_w, 1)
            pe.wait_ge(w_done_dve, 4)
            for q in range(4):
                pe.wait_ge(c_scaled, q + 1)
                for k in range(4):
                    last = pe.transpose(ps[:, 2 + q, k * P:(k + 1) * P], ctx_t[:, 4 * q + k, :], ident[:, :])
                last.then_inc(cT_full, 1)
            for q in range(4):
                pe.wait_ge(cT_free, q + 1)
                pe.matmul(ps[:, 2 + q, :], w_kq[:, :], cT[:, 512 * q:512 * q + 512], start=True, stop=True
                          ).then_inc(kq_full, 1)
            for q in range(4):
                pe.wait_ge(kq_free, q + 1)
                for k in range(4):
                    last = pe.matmul(ps[:, 2 + q, k * P:(k + 1) * P], cT[:, (4 * q + k) * P:(4 * q + k + 1) * P],
                                     w_v[:, :], start=True, stop=True)
                last.then_inc(v_full, 1)
            for q in range(4):
                pe.wait_ge(x1_ready, q + 1)
                if q > 1:
                    pe.wait_ge(v_free, q - 1)
                bank = (0, 1, 2, 3)[q]
                for k in range(4):
                    last = pe.transpose(ps[:, bank, k * P:(k + 1) * P], xg[:, 4 * q + k, :], ident[:, :])
                last.then_inc(x1T_full, 1)
            pe.wait_ge(x1T_free, 4)
            for q in range(4):
                if q < 2:
                    pe.wait_ge(v_free, q + 3)
                for k in range(4):
                    last = pe.transpose(ps[:, 4 + q, k * P:(k + 1) * P], x1T[:, (4 * q + k) * P:(4 * q + k + 1) * P],
                                        ident[:, :])
                last.then_inc(h0_full, 1)

            def turn_slots(n, b):
                pe.wait_ge(sn_ready, n + 1)
                wait(pe, snh_ready, n)
                for t in range(2):
                    pe.transpose(ps[:, 0, t * P:(t + 1) * P], sn[:, b % 2, t, :], ident[:, :])
                for t in range(2):
                    last = pe.transpose(ps[:, 0, (2 + t) * P:(3 + t) * P], h[:, 2 * b + t, :], ident[:, :])
                last.then_inc(t12_full, 1)

            def score_slots(n, b):
                pe.wait_ge(snh_ready, n + 1)
                wait(pe, exB, n)
                for m in range(2):
                    last = pe.matmul(ps[:, 1, m * 256:(m + 1) * 256], kq[:, (2 * b + m) * P:(2 * b + m + 1) * P],
                                     snh[:, b % 4, 0:256], start=True, stop=True)
                last.then_inc(sB_full, 1)

            def update_slots(n, b):
                pe.wait_ge(vr_ready, n + 1)
                pe.wait_ge(exB, n + 1)
                wait(pe, upd_ready, n)
                for t in range(2):
                    for m in range(2):
                        last = pe.matmul(ps[:, 2, t * 256:t * 256 + D + 1], e_m[:, b % 2, m, t * P:(t + 1) * P],
                                         vr[:, b % 2, m, :], start=(m == 0), stop=(m == 1))
                last.then_inc(u_full, 1)

            def turn_updates(n, b):
                pe.wait_ge(upd_ready, n + 1)
                wait(pe, updT_ready, n)
                for t in range(2):
                    last = pe.transpose(ps[:, 3, t * P:(t + 1) * P], upd[:, b % 2, t, :], ident[:, :])
                last.then_inc(t3_full, 1)

            def gates(n, b):
                pe.wait_ge(updT_ready, n + 1)
                wait(pe, npre_ready, n - 1)
                for t in range(2):
                    bank = ps[:, 4 + 2 * (b % 2) + t, :]
                    pe.matmul(bank, ones_b[:, :], bias[:, :], start=True, stop=False)
                    pe.matmul(bank[:, 0:3 * D], updT[:, b % 2, t * P:(t + 1) * P], w_ih[:, :], start=False, stop=False)
                    last = pe.matmul(bank[:, D:4 * D], snh[:, b % 4, 256 + t * P:256 + (t + 1) * P], w_hh[:, :],
                                     start=False, stop=True)
                last.then_inc(g_full, 1)

            def step(n, k):
                if 0 <= k < BLOCKS:
                    turn_updates(n, k % 8)
                if 0 <= k + 3 < BLOCKS:
                    turn_slots(n + 3, (k + 3) % 8)
                if 0 <= k + 2 < BLOCKS:
                    score_slots(n + 2, (k + 2) % 8)
                if 0 <= k + 1 < BLOCKS:
                    update_slots(n + 1, (k + 1) % 8)
                if 0 <= k < BLOCKS:
                    gates(n, k % 8)

            pe.wait_ge(consts, 14)
            pe.wait_ge(h0_free, 4)
            pe.wait_ge(x1n_ready, 1)
            for k in range(-3, 3):
                step(k, k)
            with pe.Fori(0, ITERS - 1) as it:
                for k in range(3, 11):
                    step(8 * it + k, k)
            for k in range(8 * (ITERS - 1) + 3, BLOCKS):
                step(k, k)

            for q in range(4):
                pe.wait_ge(x2_ready, q + 1)
                for k in range(4):
                    last = pe.transpose(ps[:, q, k * P:(k + 1) * P], x2[:, 4 * q + k, :], ident[:, :])
                last.then_inc(x2T_full, 1)
            for q in range(4):
                pe.wait_ge(x2T_free, q + 1)
                for k in range(4):
                    t = 4 * q + k
                    last = pe.matmul(ps[:, 4, t * E:(t + 1) * E], x1T[:, t * P:(t + 1) * P], wg[:, :],
                                     start=True, stop=True)
            last.then_inc(lg_full, 1)
            pe.wait_ge(hot_ready, 1)
            hot_flat = hot[:, :, :].rearrange("p e q -> p (e q)")
            pe.matmul(ps[:, 5, 0:256], before[:, :], hot_flat, start=True, stop=True)
            pe.matmul(ps[:, 6, 0:256], ones_b[:, :], hot_flat, start=True, stop=True).then_inc(rank_full, 1)
            pe.wait_ge(padded, 1)
            pe.wait_ge(row_done, 1)
            pe.wait_ge(wt_done, 1)
            for k in range(TOPK):
                pe.wait_ge(lo_ready, k + 1)
                for q in range(k * T, (k + 1) * T):
                    last = pe.matmul(ps[:, 7, 0:P], hot_lo[:, q, :], hot_hi[:, q, :], start=(q == 0),
                                     stop=(q == TOPK * T - 1))
            last.then_inc(table_full, 1)

            def turn_expert(pair, r, e):
                pe.wait_ge(ld_xe[r], 16 * CT * pair + 16 * CT)
                wait(pe, xeT_free, e)
                for j in range(CT):
                    bank, col = divmod(j * P, 512)
                    last = pe.transpose(ps[:, bank, col:col + P], xe[:, r, j, :], ident[:, :])
                last.then_inc(xeT_full, 1)

            def expand_expert(pair, r, e):
                pe.wait_ge(ld_we[r], 32 * pair + 32)
                pe.wait_ge(xeT_free, e + 1)
                for f in range(FC):
                    wait(pe, gelu_done, FC * e + f - 1)
                    b0 = 2 + 2 * (f % 2)
                    w = cfc[:, r, f * P:(f + 1) * P]
                    pe.matmul(ps[:, b0, :], w, xeT[:, r, 0:512], start=True, stop=True)
                    pe.matmul(ps[:, b0 + 1, 0:CAP - 512], w, xeT[:, r, 512:CAP], start=True, stop=True
                              ).then_inc(fc_full, 1)

            def reduce_expert(e, r):
                pe.wait_ge(gelu_done, FC * e + FC)
                wait(pe, eo_ready, e)
                for j in range(CT):
                    bank, col = divmod(j * P, 512)
                    for f in range(FC):
                        last = pe.matmul(ps[:, 6 + bank, col:col + P], hT[:, r, f, j * P:(j + 1) * P], cpr[:, r, f, :],
                                         start=(f == 0), stop=(f == FC - 1))
                last.then_inc(pr_full, 1)

            def experts(pair, final):
                for r in range(2):
                    e = 2 * pair + r
                    expand_expert(pair, r, e)
                    if not (final and r == 1):
                        turn_expert(pair + r, 1 - r, e + 1)
                    reduce_expert(e, r)

            turn_expert(0, 0, 0)
            experts(0, False)
            with pe.Fori(1, E // 2 - 1) as pair:
                experts(pair, False)
            experts(E // 2 - 1, True)

        @block.vector
        def _(dve):
            links = [0]

            def link(ins, base=None):
                links[0] += 1
                ins.then_inc(dve_link, 1)
                dve.wait_ge(dve_link, links[0] if base is None else base + links[0])

            def rsqrt(base, a, y, t):
                link(dve.tensor_scalar(t.bitcast(I32), a.bitcast(I32), 1, None, ALU.logical_shift_right), base)
                link(dve.tensor_scalar(y.bitcast(I32), t.bitcast(I32), -1.0, float(0x5F3759DF), ALU.mult, ALU.add), base)
                for _ in range(3):
                    link(dve.tensor_tensor(t, y, y, ALU.mult), base)
                    link(dve.scalar_tensor_tensor(t, t, -0.5, a, ALU.mult, ALU.mult), base)
                    link(dve.scalar_tensor_tensor(y, t, 1.5, y, ALU.add, ALU.mult), base)

            def stats(g0, g1, src, eps):
                if src is not None:
                    for g in range(g0, g1):
                        last = dve.bn_stats(st[:, g, :], src[:, g, :])
                    link(last)
                for g in range(g0, g1):
                    last = dve.bn_aggr(mv[:, g, :], st[:, g, :])
                link(last)
                link(dve.tensor_scalar(var[:, g0:g1], mv[:, g0:g1, 1], eps, None, ALU.add))
                rsqrt(None, var[:, g0:g1], rs[:, g0:g1], rt[:, g0:g1])

            def normalise_in(sg):
                wait(dve, b0_full, b0_item(sg - 1, 1))
                for g in range(GL):
                    n = GL * sg + g
                    last = dve.tensor_scalar(xn[:, g, :], xg[:, n, :], mv[:, n, 0:1],
                                             rs[:, n:n + 1] if isinstance(n, int) else rs[:, bass.ds(n, 1)],
                                             ALU.subtract, ALU.mult)
                last.then_inc(xn_ready, 1)

            def key_low(sg, hp):
                dve.wait_ge(b1_full, b1_item(sg, hp) + 1)
                dve.tensor_copy(kz[0:DH, hp, :, 0, :], ps[0:DH, 1, :].rearrange("p (g n) -> p g n", g=GL)
                                ).then_inc(b1_free_dve, 1)

            def value_high(sg, g):
                dve.wait_ge(b1_full, b1_item(sg, HP + g) + 1)
                dve.tensor_copy(v[:, g, 512:1024], ps[:, 1, :]).then_inc(b1_free_dve, 1)

            def diagonal(n, g, base):
                dve.wait_ge(s_full0, n + 1)
                src = ps[:, 2:4, :].rearrange("p b (h k) -> p (b h) k", h=4)
                for q in range(4):
                    r = slice(QB * q, QB * q + QB)
                    last = dve.tensor_tensor(sc[r, g % 2, 0:8, :], src[r, :, QB * q:QB * q + QB],
                                             mask[r, :].unsqueeze(1).to_broadcast([QB, 8, QB]), ALU.add)
                last.then_inc(s_free0, 1)

            def mask_high(n, g, base):
                dve.wait_ge(s_free1, n + 1)
                hi = sc[:, g % 2, 8:16, :]
                link(dve.tensor_tensor(hi, hi, mask[:, :].unsqueeze(1).to_broadcast([P, 8, QB]), ALU.add), base)

            def shift(n, g, base):
                link(dve.tensor_reduce(mx[:, :], sc[:, g % 2, :, :], AX.X, ALU.max), base)
                dve.tensor_tensor(sc[:, g % 2, :, :], sc[:, g % 2, :, :],
                                  mx[:, :].unsqueeze(2).to_broadcast([P, H, QB]), ALU.subtract).then_inc(shifted, 1)

            def divide(n, g, base):
                dve.wait_ge(exped, n + 1)
                link(dve.tensor_reduce(sm[:, :], pc[:, g % 2, :, :], AX.X, ALU.add), base)
                link(dve.reciprocal(sm[:, :], sm[:, :]), base)
                link(dve.tensor_tensor(pc[:, g % 2, :, :], pc[:, g % 2, :, :],
                                       sm[:, :].unsqueeze(2).to_broadcast([P, H, QB]), ALU.mult), base)

            def turn_blocks(n, g, reuse):
                if reuse:
                    dve.wait_ge(spread, n - 1)
                dve.transpose(pt[:, g % 2, :, :].rearrange("p h k -> p (h k)"),
                              pc[:, g % 2, :, :].rearrange("p h k -> p (h k)")).then_inc(probs, 1)

            def context_high(n):
                dve.wait_ge(pv1, n + 1)
                dve.tensor_copy(ctxT[:, 4:8, :], ps[:, 7, :].rearrange("p (h n) -> p h n", h=4)).then_inc(ctx1, 1)

            def residual(n):
                dve.wait_ge(o_full, n + 1)
                row = xg[:, n, :]
                dve.tensor_tensor(row, row, ps[:, 7, 0:P], ALU.add).then_inc(o_free, 1)
                dve.wait_ge(o_free, n + 1)
                dve.bn_stats(st[:, n, :], row)

            def supergroup(sg, first, final, base):
                for hp in range(HP):
                    key_low(sg, hp)
                    if first and hp < 6:
                        if hp == 0:
                            dve.wait_ge(ld_x_rest, 16 * (T - GL))
                        for g in (GL + 2 * hp, GL + 2 * hp + 1):
                            dve.bn_stats(st[:, g, :], xg[:, g, :])
                    if not first:
                        if hp == 0:
                            residual(GL * sg - 3)
                        if hp == 2:
                            divide(GL * sg - 1, 3, base)
                        if hp == 3:
                            turn_blocks(GL * sg - 1, 3, True)
                if first:
                    stats(GL, T, None, LN_EPS)
                else:
                    context_high(GL * sg - 2)
                diagonal(GL * sg, 0, base)
                mask_high(GL * sg, 0, base)
                if not first:
                    residual(GL * sg - 2)
                shift(GL * sg, 0, base)
                divide(GL * sg, 0, base)
                turn_blocks(GL * sg, 0, not first)
                if not first:
                    context_high(GL * sg - 1)
                diagonal(GL * sg + 1, 1, base)
                mask_high(GL * sg + 1, 1, base)
                shift(GL * sg + 1, 1, base)
                if not first:
                    residual(GL * sg - 1)
                for g in range(GL):
                    value_high(sg, g)
                divide(GL * sg + 1, 1, base)
                turn_blocks(GL * sg + 1, 1, not first)
                if not final:
                    normalise_in(sg + 1)
                context_high(GL * sg)
                if first:
                    dve.wait_ge(ld_ctx, 16)
                for g in range(GL):
                    dve.bn_stats(c_st[:, GL * sg + g, :], ctx_t[:, GL * sg + g, :])
                diagonal(GL * sg + 2, 2, base)
                mask_high(GL * sg + 2, 2, base)
                residual(GL * sg)
                shift(GL * sg + 2, 2, base)
                divide(GL * sg + 2, 2, base)
                turn_blocks(GL * sg + 2, 2, True)
                context_high(GL * sg + 1)
                diagonal(GL * sg + 3, 3, base)
                mask_high(GL * sg + 3, 3, base)
                shift(GL * sg + 3, 3, base)

            dve.memset(kz[DH:P, :, :, 0, :], 0.0).then_inc(zeroed, 1)
            dve.wait_ge(ld_x, 16 * GL)
            stats(0, GL, xg, LN_EPS)
            normalise_in(0)
            dve.wait_ge(consts, 5)
            for q in range(4):
                last = dve.tensor_copy(mask[QB * q:QB * q + QB, :], full_mask[QB * q:QB * q + QB, QB * q:QB * q + QB])
            link(last)
            dve.wait_ge(zeroed, 4)
            supergroup(0, True, False, None)
            done = links[0]
            PER = 5 * GL
            with dve.Fori(1, SG - 1) as sg:
                supergroup(sg, False, False, sg * PER - PER)
                assert links[0] - done == PER, links[0] - done
            links[0] = done + PER * (SG - 2)
            supergroup(SG - 1, False, True, None)
            residual(T - 3)
            divide(T - 1, 3, None)
            turn_blocks(T - 1, 3, True)
            context_high(T - 2)
            residual(T - 2)
            context_high(T - 1)
            residual(T - 1)

            dve.wait_ge(ld_in, 32)
            dve.wait_ge(turned_w, 1)
            for dst, src, sc1 in ((w_kq[:, :], ps[:, 2, 0:P], lnv[:, 3:4]), (w_v[:, :], ps[:, 2, P:2 * P], lnv[:, 3:4])):
                dve.tensor_scalar(dst, src, sc1, None, ALU.mult).then_inc(w_done_dve, 1)
            dve.tensor_copy(w_ih[:, D:3 * D], ps[:, 2, 2 * P:4 * P])
            dve.tensor_copy(w_ih[:, 0:D], ps[:, 3, 0:P]).then_inc(w_done_dve, 1)
            dve.tensor_copy(w_hh[:, :], ps[:, 3, P:4 * P]).then_inc(w_done_dve, 1)

            for g in range(T):
                last = dve.bn_aggr(c_mv[:, g, :], c_st[:, g, :])
            link(last)
            link(dve.tensor_tensor(var[:, :], c_mv[:, :, 0], c_mv[:, :, 0], ALU.mult))
            link(dve.scalar_tensor_tensor(var[:, :], var[:, :], RMS_EPS, c_mv[:, :, 1], ALU.add, ALU.add))
            rsqrt(None, var[:, :], c_r[:, :], rt[:, :])
            dve.tensor_copy(rt[:, :], c_r[:, :]).then_inc(c_rs, 1)
            for g in range(T):
                last = dve.bn_aggr(mv[:, g, :], st[:, g, :])
            link(last)
            link(dve.tensor_scalar(var[:, :], mv[:, :, 1], OUT_EPS, None, ALU.add))
            rsqrt(None, var[:, :], rs[:, :], rt[:, :])
            for g in range(T):
                last = dve.tensor_scalar(xg[:, g, :], xg[:, g, :], mv[:, g, 0:1], rs[:, g:g + 1], ALU.subtract, ALU.mult)
                if g % 4 == 3:
                    last.then_inc(x1_ready, 1)
            for q in range(4):
                dve.wait_ge(v_full, q + 1)
                dve.tensor_copy(vp[:, 4 * q:4 * q + 4, :], ps[:, 2 + q, :].rearrange("p (t d) -> p t d", t=4)
                                ).then_inc(v_free, 1)
            dve.wait_ge(ld_bias, 112)
            dve.tensor_copy(b_sum[:, 0:D], b_rows[:, 0, 2 * D:3 * D])
            dve.tensor_tensor(b_sum[:, D:3 * D], b_rows[:, 0, 0:2 * D], b_rows[:, 1, 0:2 * D], ALU.add)
            link(dve.tensor_copy(b_sum[:, 3 * D:4 * D], b_rows[:, 1, 2 * D:3 * D]))
            dve.wait_ge(consts, 14)
            link(dve.tensor_copy(b_cut[:, :], b_sum[:, :]))
            link(dve.tensor_scalar(b_part[:, :], b_cut[:, :], ident[0:3, 0:1], None, ALU.mult))
            for k in (1, 2):
                link(dve.tensor_tensor(b_sum[:, :], b_sum[:, :], b_cut[:, :], ALU.subtract))
                link(dve.tensor_copy(b_cut[:, :], b_sum[:, :]))
                link(dve.scalar_tensor_tensor(b_part[:, :], b_cut[:, :], ident[0:3, k:k + 1], b_part[:, :],
                                              ALU.mult, ALU.add))
            link(dve.tensor_copy(bias[0:3, :], b_part[:, :]))

            def squares(b):
                for t in (2 * b, 2 * b + 1):
                    last = dve.tensor_tensor_reduce(sq_out[:, t % 2 * D:t % 2 * D + D], h[:, t, :], h[:, t, :], 1.0, 0.0, ALU.mult, ALU.add,
                                                    sq[:, t:t + 1])
                return last

            def slot_scale(t0, t1, base):
                link(dve.tensor_scalar(var[:, t0:t1], sq[:, t0:t1], 1.0 / D, RMS_EPS, ALU.mult, ALU.add), base)
                rsqrt(base, var[:, t0:t1], r_h[:, t0:t1], rt[:, t0:t1])

            def normalise_slots(n, b):
                wait(dve, t12_full, n - 1)
                dve.tensor_tensor(sn[:, b % 2, :, :], h[:, 2 * b:2 * b + 2, :],
                                  r_h[:, 2 * b:2 * b + 2].unsqueeze(2).to_broadcast([P, 2, D]), ALU.mult
                                  ).then_inc(sn_ready, 1)

            def maxima(n, b):
                dve.wait_ge(sB_full, n + 1)
                wait(dve, exB, n - 1)
                dve.tensor_reduce(n_mx[:, b % 2, :], ps[:, 1, :].rearrange("p (m k) -> p m k", m=2), AX.X, ALU.max,
                                  negate=True).then_inc(negmax, 1)

            def scale_values(n, b, base):
                dve.wait_ge(exB, n + 1)
                wait(dve, u_full, n - 1)
                link(dve.reciprocal(vr[:, b % 2, :, D:D + 1], den[:, b % 2, :].unsqueeze(2)), base)
                dve.tensor_tensor(vr[:, b % 2, :, 0:D], vp[:, 2 * b:2 * b + 2, :],
                                  vr[:, b % 2, :, D:D + 1].to_broadcast([P, 2, D]), ALU.mult).then_inc(vr_ready, 1)

            def scale_updates(n, b, base):
                dve.wait_ge(u_full, n + 1)
                wait(dve, t3_full, n - 1)
                u = ps[:, 2, :].rearrange("p (t d) -> p t d", t=2)
                link(dve.tensor_scalar(r_sum[:, :], u[:, :, D], SUM_EPS, None, ALU.add), base)
                link(dve.reciprocal(r_sum[:, :], r_sum[:, :]), base)
                dve.tensor_tensor(upd[:, b % 2, :, :], u[:, :, 0:D], r_sum[:, :].unsqueeze(2).to_broadcast([P, 2, D]),
                                  ALU.mult).then_inc(upd_ready, 1)

            def candidate(n, b, base):
                dve.wait_ge(rz_ready, n + 1)
                g = ps[:, 4 + 2 * (b % 2):6 + 2 * (b % 2), :]
                link(dve.scalar_tensor_tensor(tmp, trz[:, b % 2, :, 0:D], 1.0, g[:, :, 3 * D:4 * D], ALU.add, ALU.mult), base)
                dve.scalar_tensor_tensor(new[:, b % 2, :, :], tmp, 0.5, g[:, :, 0:D], ALU.mult, ALU.add
                                         ).then_inc(npre_ready, 1)

            def blend(n, b, base, final):
                dve.wait_ge(new_ready, n + 1)
                hb = h[:, 2 * b:2 * b + 2, :]
                nb = new[:, b % 2, :, :]
                link(dve.tensor_tensor(tmp2, hb, nb, ALU.subtract), base)
                link(dve.scalar_tensor_tensor(tmp2, trz[:, b % 2, :, D:2 * D], 1.0, tmp2, ALU.add, ALU.mult), base)
                dve.scalar_tensor_tensor(hb, tmp2, 0.5, nb, ALU.mult, ALU.add).then_inc(h_ready, 1)
                if not final:
                    dve.wait_ge(h_ready, n + 1)
                    link(squares(b), base)

            def step(n, k, base):
                if 0 <= k - 1:
                    candidate(n - 1, (k - 1) % 8, base)
                if 0 <= k + 2 < BLOCKS:
                    maxima(n + 2, (k + 2) % 8)
                if 0 <= k - 1:
                    blend(n - 1, (k - 1) % 8, base, k - 1 >= BLOCKS - 8)
                    if (k - 1) % 4 == 3 and k - 1 < BLOCKS - 8:
                        b = (k - 1) % 8
                        slot_scale(2 * (b - 3), 2 * b + 2, base)
                if 0 <= k + 1 < BLOCKS:
                    scale_updates(n + 1, (k + 1) % 8, base)
                if 0 <= k + 2 < BLOCKS:
                    scale_values(n + 2, (k + 2) % 8, base)
                if 0 <= k + 4 < BLOCKS:
                    normalise_slots(n + 4, (k + 4) % 8)

            dve.wait_ge(h0_free, 4)
            for b in range(B8):
                link(squares(b))
            slot_scale(0, T, None)
            for k in range(-4, 3):
                step(k, k, None)
            done = links[0]
            PER_IT = 8 * (2 + 2 + 1 + 1 + 1) + 2 * 12
            with dve.Fori(0, ITERS - 1) as it:
                for k in range(3, 11):
                    step(8 * it + k, k, it * PER_IT)
                assert links[0] - done == PER_IT, links[0] - done
            links[0] = done + PER_IT * (ITERS - 1)
            for k in range(8 * (ITERS - 1) + 3, BLOCKS + 1):
                step(k, k, None)

            dve.wait_ge(h_ready, BLOCKS)
            for q in range(4):
                last = dve.tensor_tensor(h[:, 4 * q:4 * q + 4, :], h[:, 4 * q:4 * q + 4, :], x1n[:, 4 * q:4 * q + 4, :], ALU.add)
            link(last)
            stats(0, T, h, OUT_EPS)
            for t in range(T):
                last = dve.tensor_scalar(x2[:, t, :], h[:, t, :], mv[:, t, 0:1], rs[:, t:t + 1],
                                         ALU.subtract, ALU.mult)
                if t % 4 == 3:
                    last.then_inc(x2_ready, 1)
            dve.tensor_copy(iota_p[:, :], iota_pi[:, :])
            dve.tensor_copy(row_f[:, :], row_i[:, :])
            link(dve.tensor_copy(iota_e[:, :], iota_i[:, :]))
            dve.tensor_scalar(e_base[:, :], iota_e[:, :], float(CAP), None, ALU.mult)
            dve.memset(top[:, 2, :], NEG_INF)
            dve.wait_ge(lg_full, 1)
            link(dve.tensor_copy(lg[:, :, :], ps[:, 4, 0:T * E].rearrange("p (t e) -> p t e", t=T)))
            for t in range(T):
                last = dve.max(v8[:, t, :], lg[:, t, :])
            link(last)
            for t in range(T):
                last = dve.max_index(i8[:, t, :], v8[:, t, :], lg[:, t, :])
            link(last)
            link(dve.tensor_copy(pick[:, :, :], i8[:, :, 0:TOPK].rearrange("p t k -> p k t")))
            QN = TOPK * T
            dve.tensor_tensor(hot[:, :, :], pick[:, :, :].rearrange("p k t -> p (k t)").unsqueeze(1).to_broadcast([P, E, QN]),
                              iota_e[:, :].unsqueeze(2).to_broadcast([P, E, QN]), ALU.is_equal).then_inc(hot_ready, 1)
            link(dve.tensor_copy(top[:, 0:2, :], v8[:, :, 0:TOPK].rearrange("p t k -> p k t")))
            link(dve.tensor_tensor(top_m[:, :], top[:, 0, :], top[:, 2, :], ALU.max))
            dve.tensor_tensor(top[:, :, :], top[:, :, :], top_m[:, :].unsqueeze(1).to_broadcast([P, 3, T]), ALU.subtract
                              ).then_inc(top_ready, 1)
            dve.wait_ge(rank_full, 1)
            link(dve.tensor_copy(tot[:, :], ps[:, 6, 0:E * QN]))
            link(dve.tensor_tensor_scan(incl[:, :], seg[:, :, :].rearrange("p e q -> p (e q)"), tot[:, :], 0.0,
                                        ALU.mult, ALU.add))
            link(dve.tensor_tensor(incl[:, :], incl[:, :], tot[:, :], ALU.subtract))
            link(dve.tensor_tensor(incl[:, :], incl[:, :], ps[:, 5, 0:E * QN], ALU.add))
            link(dve.scalar_tensor_tensor(kept[:, :], incl[:, :], float(CAP), hot[:, :, :].rearrange("p e q -> p (e q)"),
                                          ALU.is_lt, ALU.mult))
            by_e = "p (e q) -> p e q"
            link(dve.tensor_tensor(incl[:, :].rearrange(by_e, e=E), incl[:, :].rearrange(by_e, e=E),
                                   e_base[:, :].unsqueeze(2).to_broadcast([P, E, QN]), ALU.add))
            link(dve.tensor_tensor(incl[:, :], incl[:, :], kept[:, :], ALU.mult))
            dve.tensor_reduce(slot[:, :], incl[:, :].rearrange("p (e q) -> p q e", e=E), AX.X, ALU.add)
            link(dve.tensor_reduce(keep[:, :], kept[:, :].rearrange("p (e q) -> p q e", e=E), AX.X, ALU.add))
            link(dve.scalar_tensor_tensor(slot[:, :], keep[:, :], -float(NOWHERE), slot[:, :], ALU.mult, ALU.add))
            link(dve.tensor_scalar(slot_i[:, :], slot[:, :], float(NOWHERE), None, ALU.add))
            dve.tensor_scalar(slot_lo[:, :], slot_i[:, :], P - 1, None, ALU.bitwise_and)
            link(dve.tensor_scalar(slot_hi[:, :], slot_i[:, :], P.bit_length() - 1, None, ALU.logical_shift_right))
            dve.tensor_copy(lo_f[:, :], slot_lo[:, :])
            link(dve.tensor_copy(hi_f[:, :], slot_hi[:, :]))
            dve.tensor_tensor(tile_hot, hi_f[:, :].unsqueeze(2).to_broadcast([P, QN, NT]),
                              iota_p[:, 0:NT].unsqueeze(1).to_broadcast([P, QN, NT]), ALU.is_equal).then_inc(hi_ready, 1)
            dve.wait_ge(expt_ready, 1)
            link(dve.scalar_tensor_tensor(top_m[:, :], expt[:, 2, :], float(E - TOPK), expt[:, 0, :], ALU.mult, ALU.add))
            link(dve.tensor_tensor(top_m[:, :], top_m[:, :], expt[:, 1, :], ALU.add))
            link(dve.reciprocal(top_m[:, :], top_m[:, :]))
            link(dve.tensor_tensor(prob[:, :, :], expt[:, 0:2, :], top_m[:, :].unsqueeze(1).to_broadcast([P, TOPK, T]), ALU.mult))
            link(dve.tensor_tensor(wt[:, :], prob[:, :, :].rearrange("p k t -> p (k t)"), keep[:, :], ALU.mult))
            dve.wait_ge(hi_ready, 1)
            dve.tensor_tensor(hot_hi[:, :, NT:2 * NT], tile_hot, wt[:, :].unsqueeze(2).to_broadcast([P, QN, NT]), ALU.mult
                              ).then_inc(wt_done, 1)
            for k in range(TOPK):
                half = slice(k * T, (k + 1) * T)
                dve.tensor_tensor(hot_lo[:, half, :], lo_f[:, half].unsqueeze(2).to_broadcast([P, T, P]),
                                  iota_p[:, :].unsqueeze(1).to_broadcast([P, T, P]), ALU.is_equal).then_inc(lo_ready, 1)
            dve.wait_ge(table_full, 1)
            dve.tensor_copy(t_wt[:, :], ps[:, 7, NT:2 * NT])
            link(dve.tensor_copy(t_row[:, :], ps[:, 7, 0:NT]))
            link(dve.tensor_scalar(t_tmp[:, :], t_row[:, :], float(N), -float(N), ALU.is_gt, ALU.mult))
            link(dve.scalar_tensor_tensor(t_tmp[:, :], t_row[:, :], -1.0, t_tmp[:, :], ALU.add, ALU.add))
            dve.tensor_scalar(t_src[:, :], t_tmp[:, :], 0.0, None, ALU.max).then_inc(src_ready, 1)
            link(dve.tensor_scalar(t_tmp2[:, :], t_row[:, :], 0.5, float(NOWHERE), ALU.is_lt, ALU.mult))
            dve.scalar_tensor_tensor(t_dst[:, :], t_row[:, :], -1.0, t_tmp2[:, :], ALU.add, ALU.add).then_inc(dst_ready, 1)

            def take_batch(e, r):
                dve.wait_ge(xeT_full, e + 1)
                src = ps[:, 0:2, :].rearrange("p b n -> p (b n)")[:, 0:CAP]
                dve.tensor_copy(xeT[:, r, :], src).then_inc(xeT_free, 1)

            def weigh_output(pair, e, r, reuse):
                dve.wait_ge(pr_full, e + 1)
                if reuse:
                    dve.wait_ge(returned[r], 16 * CT * pair)
                src = ps[:, 6:8, :].rearrange("p b n -> p (b n)")[:, 0:CAP].rearrange("p (j d) -> p j d", j=CT)
                w = t_wt[:, e * CT:(e + 1) * CT] if isinstance(e, int) else t_wt[:, bass.ds(e * CT, CT)]
                dve.tensor_tensor(eo[:, r, :, :], src, w.unsqueeze(2).to_broadcast([P, CT, D]), ALU.mult
                                  ).then_inc(eo_ready, 1)

            def experts(pair, reuse, final):
                for r in range(2):
                    e = 2 * pair + r
                    if not (final and r == 1):
                        take_batch(e + 1, 1 - r)
                    weigh_output(pair, e, r, reuse)

            take_batch(0, 0)
            experts(0, False, False)
            with dve.Fori(1, E // 2 - 1) as pair:
                experts(pair, True, False)
            experts(E // 2 - 1, True, True)
            for q in range(4):
                g0, g1 = 4 * q, 4 * q + 4
                dve.wait_ge(ld_part[q], 32)
                hq = h[:, g0:g1, :]
                link(dve.tensor_tensor(hq, xg[:, g0:g1, :], ctx_t[:, g0:g1, :], ALU.add))
                link(dve.tensor_tensor(hq, hq, x2[:, g0:g1, :], ALU.add))
                stats(g0, g1, h, OUT_EPS)
                for t in range(g0, g1):
                    last = dve.tensor_scalar(h[:, t, :], h[:, t, :], mv[:, t, 0:1], rs[:, t:t + 1],
                                             ALU.subtract, ALU.mult)
                last.then_inc(y_ready, 1)

        @block.scalar
        def _(act):
            def turned(sg):
                act.wait_ge(b0_full, b0_item(sg, 0) + 1)
                act.activation(lnT[:, :], ps[:, 0, :], ACT.Identity, bias=lnv[:, 1:2], scale=lnv[:, 0:1]
                               ).then_inc(b0_free, 1)

            def query(sg, hp):
                act.wait_ge(b0_full, b0_item(sg, 1 + hp) + 1)
                act.activation(qT[:, hp, :], ps[:, 0, :], ACT.Copy).then_inc(b0_free, 1)

            def key_high(sg, hp):
                act.wait_ge(b1_full, b1_item(sg, hp) + 1)
                act.activation(kz[DH:P, hp, :, 1, :], ps[DH:P, 1, :].rearrange("p (g n) -> p g n", g=GL), ACT.Copy
                               ).then_inc(b1_free_act, 1)

            def value_low(sg, g):
                act.wait_ge(b0_full, b0_item(sg, 1 + HP + g) + 1)
                act.activation(v[:, g, 0:512], ps[:, 0, :], ACT.Copy).then_inc(b0_free, 1)

            def diagonal(n, g, reuse):
                act.wait_ge(s_full1, n + 1)
                if reuse:
                    act.wait_ge(shifted, n - 1)
                src = ps[:, 4:6, :].rearrange("p b (h k) -> p (b h) k", h=4)
                for q in range(4):
                    r = slice(QB * q, QB * q + QB)
                    last = act.activation(sc[r, g % 2, 8:16, :], src[r, :, QB * q:QB * q + QB], ACT.Copy)
                last.then_inc(s_free1, 1)

            def exponent(n, g, reuse):
                act.wait_ge(shifted, n + 1)
                if reuse:
                    act.wait_ge(probs, n - 1)
                act.activation(pc[:, g % 2, :, :], sc[:, g % 2, :, :], ACT.Exp, scale=float(DH) ** -0.5
                               ).then_inc(exped, 1)

            def expand(n, g, reuse, quadrants=range(4)):
                act.wait_ge(probs, n + 1)
                if reuse:
                    act.wait_ge(pv1, n - 1)
                for q in quadrants:
                    r = slice(QB * q, QB * q + QB)
                    last = act.activation(pbd[r, g % 2, :, QB * q:QB * q + QB], pt[r, g % 2, :, :], ACT.Copy)
                if 3 in quadrants:
                    last.then_inc(spread, 1)

            def context_low(n):
                act.wait_ge(pv0, n + 1)
                act.activation(ctxT[:, 0:4, :], ps[:, 6, :].rearrange("p (h n) -> p h n", h=4), ACT.Copy
                               ).then_inc(ctx0, 1)

            def supergroup(sg, first, final):
                for hp in range(HP):
                    query(sg, hp)
                    key_high(sg, hp)
                    if not first:
                        if hp == 1:
                            exponent(GL * sg - 1, 3, True)
                        if hp in (4, 5, 6):
                            expand(GL * sg - 1, 3, True, ((0,), (1, 2), (3,))[hp - 4])
                if not first:
                    context_low(GL * sg - 2)
                diagonal(GL * sg, 0, not first)
                exponent(GL * sg, 0, not first)
                if not first:
                    context_low(GL * sg - 1)
                expand(GL * sg, 0, not first)
                diagonal(GL * sg + 1, 1, not first)
                value_low(sg, 0)
                value_low(sg, 1)
                exponent(GL * sg + 1, 1, not first)
                value_low(sg, 2)
                value_low(sg, 3)
                context_low(GL * sg)
                expand(GL * sg + 1, 1, not first)
                diagonal(GL * sg + 2, 2, True)
                if not final:
                    turned(sg + 1)
                exponent(GL * sg + 2, 2, True)
                context_low(GL * sg + 1)
                expand(GL * sg + 2, 2, True)
                diagonal(GL * sg + 3, 3, True)

            act.dma_start(lnv[:, 2:3], slot_w.rearrange("(p a) -> p a", a=1)).then_inc(ld_in, 16)
            act.dma_start(lnv[:, 3:4], input_w.rearrange("(p a) -> p a", a=1)).then_inc(ld_in, 16)
            act.dma_start(lnv[:, 0:1], ln_scale.rearrange("(p a) -> p a", a=1)).then_inc(ld_vec, 16)
            act.dma_start(lnv[:, 1:2], ln_bias.rearrange("(p a) -> p a", a=1)).then_inc(ld_vec, 16)
            act.wait_ge(ld_in, 32)
            act.activation(lnv[:, 4:5], lnv[:, 2:3], ACT.Copy, scale=float(D) ** -0.5).then_inc(w_done_act, 1)
            act.wait_ge(ld_vec, 32)
            turned(0)
            act.wait_ge(zeroed, 4)
            supergroup(0, True, False)
            with act.Fori(1, SG - 1) as sg:
                supergroup(sg, False, False)
            supergroup(SG - 1, False, True)
            exponent(T - 1, 3, True)
            expand(T - 1, 3, True)
            context_low(T - 2)
            context_low(T - 1)

            for q in range(4):
                act.wait_ge(cT_full, q + 1)
                act.activation(cT[:, 512 * q:512 * q + 512], ps[:, 2 + q, :], ACT.Copy).then_inc(cT_free, 1)
            act.wait_ge(w_done_act, 1)
            for q in range(4):
                act.wait_ge(kq_full, q + 1)
                act.activation(kq[:, 512 * q:512 * q + 512], ps[:, 2 + q, :], ACT.Copy, scale=lnv[:, 4:5]
                               ).then_inc(kq_free, 1)
            for q in range(4):
                act.wait_ge(x1T_full, q + 1)
                for g in range(4):
                    base = (4 * q + g) * 16
                    last = act.activation(x1T[:, :].rearrange("p (s b) -> p s b", s=S)[:, :, base:base + 16],
                                          ps[:, q, g * P:(g + 1) * P].rearrange("p (l s) -> p s l", s=S), ACT.Copy)
                last.then_inc(x1T_free, 1)
            for q in range(4):
                act.wait_ge(h0_full, q + 1)
                act.activation(h[:, 4 * q:4 * q + 4, :], ps[:, 4 + q, :].rearrange("p (t d) -> p t d", t=4), ACT.Copy
                               ).then_inc(h0_free, 1)

            def keep_turned(n, b):
                act.wait_ge(t12_full, n + 1)
                act.activation(snh[:, b % 4, :], ps[:, 0, :], ACT.Copy).then_inc(snh_ready, 1)

            def exponents(n, b):
                act.wait_ge(negmax, n + 1)
                wait(act, u_full, n - 1)
                wait(act, vr_ready, n - 1)
                for m in range(2):
                    last = act.activation(e_m[:, b % 2, m, :], ps[:, 1, m * 256:(m + 1) * 256], ACT.Exp,
                                          bias=n_mx[:, b % 2, m:m + 1], accum_out=den[:, b % 2, m:m + 1])
                last.then_inc(exB, 1)

            def keep_updates(n, b):
                act.wait_ge(t3_full, n + 1)
                act.activation(updT[:, b % 2, :], ps[:, 3, 0:256], ACT.Copy).then_inc(updT_ready, 1)

            def half_tanh(n, b):
                act.wait_ge(g_full, n + 1)
                wait(act, h_ready, n - 1)
                act.activation(trz[:, b % 2, :, :], ps[:, 4 + 2 * (b % 2):6 + 2 * (b % 2), D:3 * D], ACT.Tanh, scale=0.5
                               ).then_inc(rz_ready, 1)

            def new_tanh(n, b):
                act.wait_ge(npre_ready, n + 1)
                act.activation(new[:, b % 2, :, :], new[:, b % 2, :, :], ACT.Tanh).then_inc(new_ready, 1)

            def step(n, k):
                if 0 <= k < BLOCKS:
                    keep_updates(n, k % 8)
                if 0 <= k - 1:
                    half_tanh(n - 1, (k - 1) % 8)
                if 0 <= k + 3 < BLOCKS:
                    keep_turned(n + 3, (k + 3) % 8)
                if 0 <= k - 1:
                    new_tanh(n - 1, (k - 1) % 8)
                if 0 <= k + 2 < BLOCKS:
                    exponents(n + 2, (k + 2) % 8)

            for k in range(-3, 3):
                step(k, k)
            with act.Fori(0, ITERS - 1) as it:
                for k in range(3, 11):
                    step(8 * it + k, k)
            for k in range(8 * (ITERS - 1) + 3, BLOCKS + 1):
                step(k, k)

            for q in range(4):
                act.wait_ge(x2T_full, q + 1)
                act.activation(x1T[:, 512 * q:512 * q + 512], ps[:, q, :], ACT.Copy).then_inc(x2T_free, 1)
            act.wait_ge(top_ready, 1)
            act.activation(expt[:, :, :], top[:, :, :], ACT.Exp).then_inc(expt_ready, 1)

            def gelu(pair, r, e):
                for f in range(FC):
                    act.wait_ge(fc_full, FC * e + f + 1)
                    wait(act, pr_full, e - 1)
                    b0 = 2 + 2 * (f % 2)
                    src = ps[:, b0:b0 + 2, :].rearrange("p b n -> p (b n)")[:, 0:CAP]
                    act.activation(hT[:, r, f, :], src, ACT.Gelu).then_inc(gelu_done, 1)

            def experts(pair):
                for r in range(2):
                    gelu(pair, r, 2 * pair + r)

            experts(0)
            with act.Fori(1, E // 2) as pair:
                experts(pair)


_INS = ['x', 'ctx_1024', 'L0_attn_ln_scale', 'L0_attn_ln_bias', 'L0_attn_qkv_kernel', 'L0_attn_out_kernel',
        'L0_xattn_Wq', 'L0_xattn_Wk', 'L0_xattn_Wv', 'L0_xattn_gru_wih', 'L0_xattn_gru_whh', 'L0_xattn_gru_bih',
        'L0_xattn_gru_bhh', 'L0_xattn_slot_norm_w', 'L0_xattn_input_norm_w', 'L0_ffn_w_g', 'L0_ffn_c_fc',
        'L0_ffn_c_proj']


def kernel(**inputs):
    import numpy as np
    import concourse.bacc as bacc
    from concourse.bass_utils import run_bass_kernel_spmd

    nc = bacc.Bacc("TRN2", target_bir_lowering=False, num_devices=1)
    arrays, args = {}, []
    for name in _INS:
        a = np.ascontiguousarray(inputs[name])
        arrays[f"in_{name}"] = a
        args.append(nc.dram_tensor(f"in_{name}", a.shape, mybir.dt.from_np(a.dtype), kind="ExternalInput").ap())
    args.append(nc.dram_tensor("out", (S, B, D), F32, kind="ExternalOutput").ap())
    build(nc, *args)
    r = run_bass_kernel_spmd(nc, [arrays], core_ids=[0])
    return r.results[0]["out"]
```

```python
from contextlib import ExitStack

import concourse.bass as bass
from concourse import mybir

F32 = mybir.dt.float32
F32R = mybir.dt.float32r
BF16 = mybir.dt.bfloat16
I32 = mybir.dt.int32
U32 = mybir.dt.uint32
ALU = mybir.AluOpType
ACT = mybir.ActivationFunctionType
AX = mybir.AxisListType

P = 128
B8 = 8
S, B, D = 8, 256, 128
N = S * B
T = N // P
H, DH = 16, 64
HP = H // 2
SG = 4
GL = T // SG
QB = 32
ITERS = 3
E, TOPK, F = 8, 2, 512
CAP = int(TOPK * 1.25 * N / E)
CAP += CAP % 2
CT = CAP // P
NT = E * CT
FC = F // P
NOWHERE = 1 << 20
OFF = -1.0e30
NEG_INF = -1.0e9
LN_EPS, RMS_EPS, SUM_EPS, OUT_EPS = 1e-6, 1e-6, 1e-6, 1e-5


def build(nc, x, ctx_in, ln_scale, ln_bias, qkv_w, out_w, Wq, Wk, Wv, wih, whh, bih, bhh,
          slot_w, input_w, w_g, c_fc, c_proj, out):
    with ExitStack() as ctx:
        def sb(name, shape, dt=F32):
            return ctx.enter_context(nc.sbuf_tensor(name, shape, dt))

        def sem(name):
            return ctx.enter_context(nc.semaphore(name))

        ps = ctx.enter_context(nc.psum_tensor("ps", [P, 8, 512], F32))

        xg = sb("xg", [P, T, D])
        ctx_t = sb("ctx_t", [P, T, D])
        wqkv = sb("wqkv", [P, 3 * H * DH])
        wo = sb("wo", [P, HP, D])
        x1T = sb("x1T", [P, N])
        h = wqkv[:, 0:N].rearrange("p (t d) -> p t d", t=T)
        ident = sb("ident", [P, P])
        full_mask = sb("full_mask", [P, P])
        mask = sb("mask", [P, QB])
        ones_b = sb("ones_b", [P, P], BF16)
        not_before = sb("not_before", [P, P], BF16)
        zeros = sb("zeros", [P, D])
        lnv = sb("lnv", [P, 8])
        st = sb("st", [P, T, 6])
        mv = sb("mv", [P, T, 2])
        var = sb("var", [P, T])
        rs = sb("rs", [P, T])
        rt = sb("rt", [P, T])

        xn = sb("xn", [P, GL, D])
        lnT = xn[:, :, :].rearrange("p g d -> p (g d)")
        pool_a = sb("pool_a", [P, HP * 512])
        pool_v = sb("pool_v", [P, GL * H * DH])
        qT = pool_a[:, :].rearrange("p (h n) -> p h n", h=HP)
        v = pool_v[:, :].rearrange("p (g n) -> p g n", g=GL)
        sc = sb("sc", [P, 2, H, QB])
        pc = sb("pc", [P, 2, H, QB])
        pt = sb("pt", [P, 2, H, QB])
        mx = sb("mx", [P, H])
        sm = sb("sm", [P, H])
        ctxT = sb("ctxT", [P, HP, P])

        w_nat = sb("w_nat", [P, 9, D])
        w_kq = sb("w_kq", [P, D])
        w_v = sb("w_v", [P, D])
        w_ih = sb("w_ih", [P, 3 * D])
        w_hh = sb("w_hh", [P, 3 * D])
        b_rows = sb("b_rows", [3, 2, 3 * D])
        b_one = b_rows[:, :, :].rearrange("p a n -> p (a n)")[:, 0:4 * D]
        b_sum = sb("b_sum", [3, 4 * D])
        b_part = sb("b_part", [3, 4 * D])
        c_var = sb("c_var", [P, T])
        c_rt = sb("c_rt", [P, T])
        b_cut = sb("b_cut", [3, 4 * D], BF16)
        bias = sb("bias", [P, 4 * D], BF16)
        wg = sb("wg", [P, E])
        cfc = sb("cfc", [P, 2, F])
        cpr = sb("cpr", [P, 2, FC, D])
        c_st = sb("c_st", [P, T, 6])
        c_mv = sb("c_mv", [P, T, 2])
        c_r = sb("c_r", [P, T])
        sq = sb("sq", [P, T])
        r_h = sb("r_h", [P, T])

        cT = x1T[:, :]
        snh = pool_a[:, N:N + 4 * 512].rearrange("p (r n) -> p r n", r=4)
        n_mx = sb("n_mx", [P, 2, 2])
        den = sb("den", [P, 2, 2])
        r_sum = sb("r_sum", [P, 2])

        x2 = pool_v[:, 0:T * D].rearrange("p (t c) -> p t c", t=T)
        QN = TOPK * T
        rows_hi = pool_a[:, 0:QN * NT].bitcast(BF16).rearrange("p (q l) -> p q l", l=2 * NT)
        wts_hi = pool_a[:, QN * NT:QN * NT * 5 // 2].bitcast(BF16).rearrange("p (q l) -> p q l", l=3 * NT)
        eo = pool_a[:, 0:2 * CAP].rearrange("p (r j d) -> p r j d", r=2, j=CT)
        tile_hot = pool_v[:, T * D:T * D + QN * NT // 2].bitcast(BF16).rearrange("p (q l) -> p q l", l=NT)
        part = [xg, ctx_t]
        row_i = sb("row_i", [P, TOPK * T + 1], I32)
        row_f = sb("row_f", [P, TOPK * T + 1])
        iota_pi = sb("iota_pi", [P, P], I32)
        iota_p = sb("iota_p", [P, P])
        slot_hi = sb("slot_hi", [P, TOPK * T], I32)
        slot_lo = sb("slot_lo", [P, TOPK * T], I32)
        hi_f = sb("hi_f", [P, TOPK * T])
        lo_f = sb("lo_f", [P, TOPK * T])
        wt = sb("wt", [P, TOPK * T])
        t_row = sb("t_row", [P, NT])
        t_wt = sb("t_wt", [P, NT])
        t_tmp = sb("t_tmp", [P, NT])
        w_cut = sb("w_cut", [P, 3, TOPK * T], BF16)
        t_dst = sb("t_dst", [P, NT], I32)
        t_src = sb("t_src", [P, NT], I32)
        iota_i = sb("iota_i", [P, E], I32)
        iota_e = sb("iota_e", [P, E])
        seg = sb("seg", [P, E, TOPK * T])
        lg = sb("lg", [P, T, E])
        v8 = sb("v8", [P, T, 8])
        i8 = sb("i8", [P, T, 8], U32)
        pick = sb("pick", [P, TOPK, T])
        hot = sb("hot", [P, E, TOPK * T], BF16)
        top = sb("top", [P, 3, T])
        top_m = sb("top_m", [P, T])
        expt = sb("expt", [P, 3, T])
        prob = sb("prob", [P, TOPK, T])
        incl = sb("incl", [P, E * TOPK * T])
        over = sb("over", [P, TOPK * T])
        slot = sb("slot", [P, TOPK * T])
        keep = sb("keep", [P, TOPK * T])
        slot_i = sb("slot_i", [P, TOPK * T], I32)

        with ExitStack() as early:
            w_hi = early.enter_context(nc.sbuf_tensor("w_hi", [P, 3 * H * DH], F32R))
            w_lo = early.enter_context(nc.sbuf_tensor("w_lo", [P, 3 * H * DH], F32R))
            lnT_hi = early.enter_context(nc.sbuf_tensor("lnT_hi", [P, GL * P], F32R))
            lnT_lo = early.enter_context(nc.sbuf_tensor("lnT_lo", [P, GL * P], F32R))
            pool_p = early.enter_context(nc.sbuf_tensor("pool_p", [P, 2 * H * P], F32))
            pool_k = early.enter_context(nc.sbuf_tensor("pool_k", [P, HP * GL * 2 * P], F32))
        pool_x = sb("pool_x", [P, 2 * 3 * H * DH + 2 * GL * P])
        kq = pool_x[:, 0:N]
        vp = pool_x[:, N:2 * N].rearrange("p (t d) -> p t d", t=T)
        x1n = pool_x[:, 2 * N:3 * N].rearrange("p (t d) -> p t d", t=T)
        xe = pool_x[:, 0:NT * D].rearrange("p (j c) -> p j c", j=NT)
        pbd = pool_p[:, :].rearrange("p (r h n) -> p r h n", r=2, h=H)
        kz = pool_k[:, :].rearrange("p (h g z n) -> p h g z n", h=HP, g=GL, z=2)
        at = [0]

        def carve(pool, n):
            at[0] += n
            assert at[0] <= pool.shape[1], at[0]
            return pool[:, at[0] - n:at[0]]

        e_m = carve(pool_k, 1024).rearrange("p (r m k) -> p r m k", r=2, m=2)
        vr = carve(pool_k, 4 * (D + 1)).rearrange("p (r m d) -> p r m d", r=2, m=2)
        upd = carve(pool_k, 512).rearrange("p (r t d) -> p r t d", r=2, t=2)
        updT = carve(pool_k, 512).rearrange("p (r n) -> p r n", r=2)
        trz = carve(pool_k, 1024).rearrange("p (r t d) -> p r t d", r=2, t=2)
        new = carve(pool_k, 512).rearrange("p (r t d) -> p r t d", r=2, t=2)
        sn = carve(pool_k, 512).rearrange("p (r t d) -> p r t d", r=2, t=2)
        tmp = carve(pool_k, 256).rearrange("p (t d) -> p t d", t=2)
        tmp2 = carve(pool_k, 256).rearrange("p (t d) -> p t d", t=2)
        sq_out = carve(pool_k, 8 * D)
        hot_lo = sb("hot_lo", [P, QN, P], BF16)
        cfc_hi = sb("cfc_hi", [P, 2, F], F32R)
        cfc_lo = sb("cfc_lo", [P, 2, F], F32R)
        hT = sb("hT", [P, 2, FC, CAP])
        xeT_hi = sb("xeT_hi", [P, 2, CAP], F32R)
        xeT_lo = sb("xeT_lo", [P, 2, CAP], F32R)
        x2_rows = nc.dram_tensor("x2_rows", [N, D], F32, kind="Internal").ap()
        results = nc.dram_tensor("results", [TOPK * N, D], F32, kind="Internal").ap()

        ld_x, ld_x_rest, ld_ctx, ld_wo, ld_vec = (sem(n) for n in ("ld_x", "ld_x_rest", "ld_ctx", "ld_wo", "ld_vec"))
        ld_w = [sem(f"ld_w{i}") for i in range(3)]
        pool_link = sem("pool_link")
        biases = sem("biases")
        ones_ready = sem("ones_ready")
        consts = sem("consts")
        zeroed = sem("zeroed")
        dve_link = sem("dve_link")
        xn_ready = sem("xn_ready")
        w_hi_ready, w_split, lnT_hi_ready, lnT_split = (sem(n) for n in ("w_hi_ready", "w_split", "lnT_hi_ready", "lnT_split"))
        b0_full, b0_free = sem("b0_full"), sem("b0_free")
        b1_full, b1_free_dve, b1_free_act = sem("b1_full"), sem("b1_free_dve"), sem("b1_free_act")
        o_full, o_free = sem("o_full"), sem("o_free")
        s_full0, s_full1, s_free0, s_free1 = sem("s_full0"), sem("s_full1"), sem("s_free0"), sem("s_free1")
        shifted, exped, probs, spread = sem("shifted"), sem("exped"), sem("probs"), sem("spread")
        pv0, pv1, ctx0, ctx1 = sem("pv0"), sem("pv1"), sem("ctx0"), sem("ctx1")
        ld_small, ld_bias, ld_in = sem("ld_small"), sem("ld_bias"), sem("ld_in")
        turned_w, w_done_dve, w_done_act = sem("turned_w"), sem("w_done_dve"), sem("w_done_act")
        c_scaled, c_rs = sem("c_scaled"), sem("c_rs")
        cT_full, cT_free, kq_full, kq_free, v_full, v_free = (sem(n) for n in ("cT_full", "cT_free", "kq_full", "kq_free", "v_full", "v_free"))
        x1_ready, x1T_full, x1T_free, h0_full, h0_free, x1n_ready = (sem(n) for n in (
            "x1_ready", "x1T_full", "x1T_free", "h0_full", "h0_free", "x1n_ready"))
        (sn_ready, t12_full, snh_ready, sB_full, negmax, exB, vr_ready, u_full, upd_ready, t3_full, updT_ready,
         g_full, sq_ready, rz_ready, npre_ready, new_ready, h_ready) = (sem(n) for n in (
             "sn_ready", "t12_full", "snh_ready", "sB_full", "negmax", "exB", "vr_ready", "u_full", "upd_ready",
             "t3_full", "updT_ready", "g_full", "sq_ready", "rz_ready", "npre_ready", "new_ready", "h_ready"))
        r_zeroed, x2_stored, rows_a, rows_b, wts_ready, rows_full, wts_full, wts_kept, dst_ready, src_ready = (sem(n) for n in (
            "r_zeroed", "x2_stored", "rows_a", "rows_b", "wts_ready", "rows_full", "wts_full", "wts_kept", "dst_ready", "src_ready"))
        sum_ready, x2_scale, x2_low, x2_high = (sem(n) for n in ("sum_ready", "x2_scale", "x2_low", "x2_high"))
        halves_added, y_sums = sem("halves_added"), sem("y_sums")
        lo_ready, hi_ready = sem("lo_ready"), sem("hi_ready")
        x2T_full, x2T_free, lg_full = (sem(n) for n in ("x2T_full", "x2T_free", "lg_full"))
        hot_ready, rank_full, top_ready, expt_ready = (sem(n) for n in (
            "hot_ready", "rank_full", "top_ready", "expt_ready"))
        ld_xe = [sem(f"ld_xe{e}") for e in range(E)]
        ld_we = [sem(f"ld_we{r}") for r in range(2)]
        we_hi, we_split, xeT_kept = sem("we_hi"), sem("we_split"), sem("xeT_kept")
        tile_full, tile_ready = sem("tile_full"), sem("tile_ready")
        xeT_full, xeT_free, fc_full, gelu_done, pr_full, eo_ready, returned0, returned1 = (sem(n) for n in (
            "xeT_full", "xeT_free", "fc_full", "gelu_done", "pr_full", "eo_ready", "returned0", "returned1"))
        returned = [returned0, returned1]
        ld_part = [sem(f"ld_part{q}") for q in range(4)]
        y_ready, y_act, y_pool = sem("y_ready"), sem("y_act"), sem("y_pool")
        stored = sem("stored")

        block = ctx.enter_context(nc.Block())

        B0_ITEMS = 1 + HP + GL
        B1_ITEMS = HP + GL

        def b0_item(sg, k):
            return B0_ITEMS * sg + k

        def b1_item(sg, k):
            return B1_ITEMS * sg + k

        def query_bank(hp):
            return 7 if hp in (2, 4, 6) else 0

        def value_bank(g):
            return 7 if g == 2 else 0

        def b1_bank(k):
            return 1 if k % 2 else 6

        def wait(eng, s, value):
            if not (isinstance(value, int) and value <= 0):
                eng.wait_ge(s, value)

        def quarter(tiles, j):
            return tiles[:, 8 * (j % 2) + j // 2:8 * (j % 2) + j // 2 + 7:2, :]

        W_PIECES = (0, 2, 1, 3, 4, 5)
        NEXT_PIECE = {0: 2, 1: 3, 4: 4, 5: 5}
        LAST_BANKS = (6, 7, 0, 1, 2)
        BLOCKS = ITERS * B8

        @block.sync
        def _(sp):
            def load_tokens(g0, g1, loaded):
                for g in range(g0, g1):
                    sp.dma_start(xg[:, g, :], x[:, g * 16:(g + 1) * 16, :].rearrange("s l c -> l s c")
                                 ).then_inc(loaded, 16)

            load_tokens(0, GL, ld_x)
            for i, piece in enumerate(W_PIECES):
                cols = slice(piece * 512, piece * 512 + 512)
                sp.dma_start(wqkv[:, cols], qkv_w.rearrange("c t k -> c (t k)")[:, cols]).then_inc(ld_w[i // 2], 16)
            load_tokens(GL, T, ld_x_rest)
            sp.dma_start(wo[:, :, :], out_w.rearrange("(h k) c -> k h c", k=P)).then_inc(ld_wo, 16)
            sp.dma_start(ctx_t[:, :, :], ctx_in.rearrange("s (t p) c -> p (s t) c", p=P)).then_inc(ld_ctx, 16)
            for k, w in enumerate((Wq, Wk, Wv)):
                sp.dma_start(w_nat[:, k, :], w).then_inc(ld_small, 16)
            sp.dma_start(w_nat[:, 3:6, :], wih.rearrange("(g p) c -> p g c", p=P)).then_inc(ld_small, 16)
            sp.dma_start(w_nat[:, 6:9, :], whh.rearrange("(g p) c -> p g c", p=P)).then_inc(ld_small, 16)
            for k in range(3):
                sp.dma_start(b_rows[k:k + 1, 0, :], bih.rearrange("(a n) -> a n", a=1)).then_inc(ld_bias, 16)
                sp.dma_start(b_rows[k:k + 1, 1, :], bhh.rearrange("(a n) -> a n", a=1)).then_inc(ld_bias, 16)
            sp.dma_start(wg[:, :], w_g).then_inc(ld_bias, 16)
            sp.wait_ge(zeroed, 4)
            for a in range(TOPK * N // (P * 8)):
                sp.dma_start(results[a * P * 8:(a + 1) * P * 8, :].rearrange("(p j) c -> p j c", j=8),
                             zeros[:, :].unsqueeze(1).to_broadcast([P, 8, D])).then_inc(r_zeroed, 16)

            def load_weights(e, r, reuse):
                if reuse:
                    sp.wait_ge(pr_full, e - 1)
                sp.dma_start(cfc[:, r, :], c_fc[e]).then_inc(ld_we[r], 16)
                sp.dma_start(cpr[:, r, :, :], c_proj[e].rearrange("(f p) d -> p f d", p=P)).then_inc(ld_we[r], 16)

            load_weights(0, 0, False)
            load_weights(1, 1, False)
            for half in range(2):
                sp.wait_ge(x2_high if half else x2_low, 2)
                sp.dma_start(x2_rows[half * N // 2:(half + 1) * N // 2, :].rearrange("(t p) c -> p t c", p=P),
                             x2[:, half * T // 2:(half + 1) * T // 2, :]).then_inc(x2_stored, 16)
            for e in range(2, E):
                load_weights(e, e % 2, True)
            for r in range(2):
                sp.wait_ge(returned[r], 16 * NT // 2)
            for q in range(4):
                for k in range(TOPK):
                    sp.dma_start(part[k][:, 4 * q:4 * q + 4, :],
                                 results[k * N + q * 512:k * N + (q + 1) * 512, :].rearrange("(t p) c -> p t c", p=P)
                                 ).then_inc(ld_part[q], 16)
            out_t = out.rearrange("s (t p) c -> p (s t) c", p=P)
            for q in (0, 2, 1, 3):
                sp.wait_ge(y_act if q < 2 else y_ready, q % 2 + 1)
                if q == 1:
                    sp.wait_ge(y_pool, 1)
                sp.dma_start(out_t[:, 4 * q:4 * q + 4, :], h[:, 4 * q:4 * q + 4, :]).then_inc(stored, 16)
            sp.wait_ge(stored, 64)

        @block.gpsimd
        def _(pool):
            pool.memset(ones_b[:, :], 1.0).then_inc(ones_ready, 1)
            pool.memset(ident[:, :], 0.0).then_inc(consts, 1)
            pool.memset(full_mask[:, :], 0.0).then_inc(consts, 1)
            pool.wait_ge(consts, 2)
            pool.affine_select(out=ident[:, :], in_=ident[:, :], compare_op=ALU.not_equal, fill=1.0,
                               base=0, pattern=[[-1, P]], channel_multiplier=1).then_inc(consts, 1)
            pool.affine_select(out=full_mask[:, :], in_=full_mask[:, :], compare_op=ALU.is_ge, fill=OFF,
                               base=0, pattern=[[-1, P]], channel_multiplier=1).then_inc(consts, 1)
            pool.wait_ge(consts, 4)
            cols = full_mask[:, :].rearrange("p (a s) -> p a s", s=S)
            pool.affine_select(out=cols, in_=cols, compare_op=ALU.is_ge, fill=OFF,
                               base=S - 1, pattern=[[S, P // S], [0, S]], channel_multiplier=-1).then_inc(consts, 1)
            pool.memset(kz[0:DH, :, :, 1, :], 0.0).then_inc(zeroed, 1)
            pool.memset(pool_p[:, :], 0.0).then_inc(zeroed, 1)
            pool.memset(zeros[:, :], 0.0).then_inc(zeroed, 1)
            pool.memset(not_before[:, :], 0.0).then_inc(consts, 1)
            pool.memset(bias[:, :], 0.0).then_inc(consts, 1)
            pool.memset(seg[:, :, :], 1.0).then_inc(consts, 1)
            pool.wait_ge(consts, 8)
            pool.affine_select(out=not_before[:, :], in_=not_before[:, :], compare_op=ALU.is_gt, fill=-1.0,
                               base=0, pattern=[[1, P]], channel_multiplier=-1).then_inc(consts, 1)
            pool.memset(seg[:, :, 0:1], 0.0).then_inc(consts, 1)
            pool.iota(iota_i[:, :], pattern=[[1, E]], base=0, channel_multiplier=0).then_inc(consts, 1)
            pool.iota(row_i[:, 0:TOPK * T], pattern=[[P, TOPK * T]], base=0, channel_multiplier=0).then_inc(consts, 1)
            pool.iota(row_i[:, TOPK * T:TOPK * T + 1], pattern=[[1, 1]], base=1, channel_multiplier=1).then_inc(consts, 1)
            pool.iota(iota_pi[:, :], pattern=[[1, P]], base=0, channel_multiplier=0).then_inc(consts, 1)

            def link(count, ins):
                ins.then_inc(pool_link, 1)
                pool.wait_ge(pool_link, count)

            pool.wait_ge(ld_bias, 112)
            pool.tensor_copy(b_sum[:, 0:D], b_rows[:, 0, 2 * D:3 * D]).then_inc(pool_link, 1)
            pool.tensor_tensor(b_sum[:, D:3 * D], b_rows[:, 0, 0:2 * D], b_rows[:, 1, 0:2 * D], ALU.add).then_inc(pool_link, 1)
            link(3, pool.tensor_copy(b_sum[:, 3 * D:4 * D], b_rows[:, 1, 2 * D:3 * D]))
            link(4, pool.tensor_copy(b_cut[:, :], b_sum[:, :]))
            pool.wait_ge(consts, 14)
            link(5, pool.tensor_scalar(b_part[:, :], b_cut[:, :], ident[0:3, 0:1], None, ALU.mult))
            for k in (1, 2):
                link(4 * k + 2, pool.tensor_tensor(b_sum[:, :], b_sum[:, :], b_cut[:, :], ALU.subtract))
                link(4 * k + 3, pool.tensor_copy(b_cut[:, :], b_sum[:, :]))
                link(4 * k + 4, pool.tensor_scalar(b_one[:, :], b_cut[:, :], ident[0:3, k:k + 1], None, ALU.mult))
                link(4 * k + 5, pool.tensor_tensor(b_part[:, :], b_part[:, :], b_one[:, :], ALU.add))
            pool.tensor_copy(bias[0:3, :], b_part[:, :]).then_inc(biases, 1)

            pool.wait_ge(c_rs, 1)
            for g in range(4):
                rows4 = ctx_t[:, 4 * g:4 * g + 4, :]
                pool.tensor_tensor(rows4, rows4, c_r[:, 4 * g:4 * g + 4].unsqueeze(2).to_broadcast([P, 4, D]), ALU.mult
                                   ).then_inc(c_scaled, 1)
            for j in range(4):
                pool.wait_ge(h0_free, j + 1)
                pool.tensor_copy(quarter(x1n, j), quarter(h, j)).then_inc(x1n_ready, 1)

            def second_sum(b):
                pool.wait_ge(h_ready, BLOCKS - B8 + b + (2 if b < 2 else 1))
                hb = h[:, 2 * b:2 * b + 2, :]
                pool.tensor_tensor(hb, hb, x1n[:, 2 * b:2 * b + 2, :], ALU.add).then_inc(sum_ready, 1)

            for b in range(5):
                second_sum(b)
            pool.wait_ge(x2_scale, 1)
            for t in range(T // 2):
                last = pool.tensor_scalar(x2[:, t, :], h[:, t, :], mv[:, t, 0:1], rs[:, t:t + 1], ALU.subtract, ALU.mult)
                if t % 4 == 3:
                    last.then_inc(x2_low, 1)
                if t == 1:
                    second_sum(5)
                if t == 5:
                    second_sum(6)
            pool.wait_ge(hi_ready, 1)
            pool.tensor_tensor(rows_hi[:, :, 0:NT], tile_hot, row_f[:, 0:QN].unsqueeze(2).to_broadcast([P, QN, NT]),
                               ALU.mult).then_inc(rows_a, 1)

            def fetch(e):
                for c in range(e * CT, (e + 1) * CT):
                    pool.indirect_dma_start(xe[:, c, :], None, x2_rows[:, :],
                                            bass.IndirectOffsetOnAxis(t_src[:, c:c + 1], 0),
                                            bounds_check=N - 1, oob_is_err=False).then_inc(ld_xe[e], 16)

            def send_back(e, r):
                if e < E - 1:
                    pool.wait_ge(eo_ready, e + 1)
                for j in range(CT):
                    if e == E - 1:
                        pool.wait_ge(tile_ready, j + 1)
                    c = e * CT + j
                    pool.indirect_dma_start(results[:, :], bass.IndirectOffsetOnAxis(t_dst[:, c:c + 1], 0),
                                            eo[:, r, j, :], None, bounds_check=TOPK * N - 1, oob_is_err=False
                                            ).then_inc(returned[r], 16)

            pool.wait_ge(x2_stored, 32)
            pool.wait_ge(src_ready, 1)
            AHEAD = 5
            for e in range(AHEAD):
                fetch(e)
            pool.wait_ge(r_zeroed, 16 * TOPK * N // (P * 8))
            pool.wait_ge(dst_ready, 1)
            for e in range(E):
                send_back(e, e % 2)
                if e + AHEAD < E:
                    fetch(e + AHEAD)
            for q in range(4):
                pool.wait_ge(ld_part[q], 32)
                pool.tensor_tensor(xg[:, 4 * q:4 * q + 4, :], xg[:, 4 * q:4 * q + 4, :], ctx_t[:, 4 * q:4 * q + 4, :], ALU.add
                                   ).then_inc(halves_added, 1)
            pool.wait_ge(y_sums, 1)
            for t in (6, 7):
                last = pool.tensor_scalar(h[:, t, :], h[:, t, :], mv[:, t, 0:1], rs[:, t:t + 1], ALU.subtract, ALU.mult)
            last.then_inc(y_pool, 1)

        @block.tensor
        def _(pe):
            def stay_warm(bank, count):
                for _ in range(count):
                    pe.matmul(ps[:, bank, :], ones_b[:, :], ones_b[:, :].unsqueeze(1).to_broadcast([P, 4, P]),
                              start=True, stop=True)

            def turn_tokens(sg):
                pe.wait_ge(xn_ready, sg + 1)
                wait(pe, b0_free, b0_item(sg, 0))
                for g in range(GL):
                    last = pe.transpose(ps[:, 0, g * P:(g + 1) * P], xn[:, g, :], ident[:, :])
                last.then_inc(b0_full, 1)

            def exact(bank, lhs, rhs):
                (lhs_hi, lhs_lo), (rhs_hi, rhs_lo) = lhs, rhs
                pe.matmul(bank, lhs_hi, rhs_hi, start=True, stop=False)
                pe.matmul(bank, lhs_hi, rhs_lo, start=False, stop=False)
                return pe.matmul(bank, lhs_lo, rhs_hi, start=False, stop=True)

            def halves(hi, lo, start, size):
                return hi[:, start:start + size], lo[:, start:start + size]

            def project(sg, first):
                tokens = halves(lnT_hi, lnT_lo, 0, GL * P)
                pe.wait_ge(lnT_split, sg + 1)
                for hp in range(HP):
                    if first and hp % 4 == 0:
                        pe.wait_ge(w_split, 2 if hp == 0 else 4)
                    wait(pe, b0_free, b0_item(sg, 1 + hp) - (1 if hp >= 2 else 0))
                    if hp == 2 and not first:
                        pe.wait_ge(o_free, GL * sg - 2)
                    exact(ps[:, query_bank(hp), :], halves(w_hi, w_lo, hp * P, P), tokens).then_inc(b0_full, 1)
                    if not (first and hp < 2):
                        pe.wait_ge(b1_free_dve, b1_item(sg, hp) - 1)
                    if hp >= 2:
                        pe.wait_ge(b1_free_act, HP * sg + hp - 1)
                    exact(ps[:, b1_bank(hp), :], halves(w_hi, w_lo, (HP + hp) * P, P), tokens).then_inc(b1_full, 1)

            def values(sg, first):
                if first:
                    pe.wait_ge(w_split, 6)
                for g in range(GL):
                    tokens = halves(lnT_hi, lnT_lo, g * P, P)
                    pe.wait_ge(b0_free, b0_item(sg, 1 + HP + g) - (1 if g >= 2 else 0))
                    if g == 2 and not first:
                        pe.wait_ge(o_free, GL * sg)
                    exact(ps[:, value_bank(g), :], tokens, halves(w_hi, w_lo, 2 * H * DH, 512)).then_inc(b0_full, 1)
                    pe.wait_ge(b1_free_dve, b1_item(sg, HP + g) - 1)
                    if g < 2:
                        pe.wait_ge(b1_free_act, HP * sg + HP + g - 1)
                    exact(ps[:, b1_bank(g), :], tokens, halves(w_hi, w_lo, 2 * H * DH + 512, 512)).then_inc(b1_full, 1)

            def scores(sg, first, g):
                n = GL * sg + g
                if g == 0:
                    pe.wait_ge(b0_free, b0_item(sg, 1 + HP))
                    pe.wait_ge(b1_free_dve, b1_item(sg, HP))
                    pe.wait_ge(b1_free_act, HP * sg + HP)
                for half in range(2):
                    if not (first and g == 0):
                        pe.wait_ge(s_free1 if half else s_free0, n)
                    for k in range(4):
                        hp = 4 * half + k
                        last = pe.matmul(ps[:, 2 + 2 * half + k // 2, (k % 2) * 256:(k % 2) * 256 + 256],
                                         qT[:, hp, g * P:(g + 1) * P],
                                         kz[:, hp, g, :, :].rearrange("p z n -> p (z n)"), start=True, stop=True)
                    last.then_inc(s_full1 if half else s_full0, 1)

            def weigh(sg, g, first, keys=None):
                n = GL * sg + g
                pe.wait_ge(spread, n + 1)
                pe.wait_ge(b0_free, b0_item(sg, 2 + HP + g))
                pe.wait_ge(b1_free_dve, b1_item(sg, HP + 1 + g))
                if g == 0:
                    pe.wait_ge(b1_free_dve, b1_item(sg, HP + 3))
                if keys is not None:
                    pe.wait_ge(b1_free_dve, b1_item(keys, HP - 1))
                    pe.wait_ge(b1_free_act, HP * keys + HP - 1)
                for half in range(2):
                    if half == 1 and g == 0:
                        pe.wait_ge(b0_free, b0_item(sg, 1 + HP + GL))
                    if half == 1 and keys is not None:
                        pe.wait_ge(b0_free, b0_item(keys, HP))
                    if not (first and g == 0):
                        pe.wait_ge(ctx1 if half else ctx0, n)
                        if half == 1:
                            pe.wait_ge(o_free, n)
                    for hd in range(8 * half, 8 * half + 8):
                        lo = (hd % 2) * DH
                        last = pe.matmul(ps[lo:lo + DH, 6 + half, (hd // 2 % 4) * P:(hd // 2 % 4 + 1) * P],
                                         v[:, g, hd * DH:(hd + 1) * DH], pbd[:, g % 2, hd, :],
                                         start=True, stop=True)
                    last.then_inc(pv1 if half else pv0, 1)

            def output(n):
                pe.wait_ge(ld_wo, 16)
                pe.wait_ge(ctx0, n + 1)
                pe.wait_ge(ctx1, n + 1)
                for hp in range(HP):
                    last = pe.matmul(ps[:, 7, 0:P], ctxT[:, hp, :], wo[:, hp, :], start=(hp == 0), stop=(hp == HP - 1))
                last.then_inc(o_full, 1)

            def supergroup(sg, first, final):
                project(sg, first)
                if not first:
                    weigh(sg - 1, 2, False, sg)
                scores(sg, first, 0)
                if not first:
                    output(GL * sg - 2)
                    weigh(sg - 1, 3, False)
                scores(sg, first, 1)
                if not first:
                    output(GL * sg - 1)
                values(sg, first)
                weigh(sg, 0, first)
                scores(sg, first, 2)
                if final:
                    turn_weights()
                else:
                    turn_tokens(sg + 1)
                output(GL * sg)
                weigh(sg, 1, first)
                scores(sg, first, 3)
                output(GL * sg + 1)

            def turn_weights():
                pe.wait_ge(ld_small, 16 * 5)
                pe.wait_ge(b0_free, b0_item(SG, 0))
                pe.matmul(ps[:, 0, 0:P], w_nat[:, 1, :], w_nat[:, 0, :], start=True, stop=True)
                for k in range(2, 5):
                    last = pe.transpose(ps[:, 0, (k - 1) * P:k * P], w_nat[:, k, :], ident[:, :])
                last.then_inc(turned_w, 1)
                pe.wait_ge(b1_free_dve, b1_item(SG, 0))
                for k in range(5, 9):
                    last = pe.transpose(ps[:, 1, (k - 5) * P:(k - 4) * P], w_nat[:, k, :], ident[:, :])
                last.then_inc(turned_w, 1)

            def turn_context(q):
                pe.wait_ge(c_scaled, q + 1)
                if q < 2:
                    pe.wait_ge(w_done_dve, 3)
                    pe.wait_ge(w_done_act, 3)
                else:
                    pe.wait_ge(cT_free, q - 1)
                for k in range(4):
                    last = pe.transpose(ps[:, q % 2, k * P:(k + 1) * P], ctx_t[:, 4 * q + k, :], ident[:, :])
                last.then_inc(cT_full, 1)

            def turn_x1(q):
                pe.wait_ge(x1_ready, q + 1)
                if q < 2:
                    pe.wait_ge(cT_free, q + 3)
                else:
                    pe.wait_ge(x1T_free, q - 1)
                for k in range(4):
                    last = pe.transpose(ps[:, q % 2, k * P:(k + 1) * P], xg[:, 4 * q + k, :], ident[:, :])
                last.then_inc(x1T_full, 1)

            pe.wait_ge(ones_ready, 1)
            pe.wait_ge(ld_x, 16 * GL)
            stay_warm(1, 8)
            pe.wait_ge(consts, 5)
            turn_tokens(0)
            stay_warm(1, 9)
            pe.wait_ge(zeroed, 4)
            supergroup(0, True, False)
            with pe.Fori(1, SG - 1) as sg:
                supergroup(sg, False, False)
            supergroup(SG - 1, False, True)
            turn_context(0)
            turn_context(1)
            weigh(SG - 1, 2, False)
            turn_context(2)
            turn_context(3)
            output(T - 2)
            for q in range(4):
                pe.wait_ge(s_free1 if q >= 2 else s_free0, T)
                pe.wait_ge(w_done_dve, 3)
                pe.wait_ge(cT_free, q + 1)
                pe.matmul(ps[:, 2 + q, :], w_kq[:, :], cT[:, 512 * q:512 * q + 512], start=True, stop=True
                          ).then_inc(kq_full, 1)
            weigh(SG - 1, 3, False)
            turn_x1(0)
            turn_x1(1)
            for q in range(4):
                pe.wait_ge(kq_free, q + 1)
                for k in range(4):
                    last = pe.matmul(ps[:, 2 + q, k * P:(k + 1) * P], cT[:, (4 * q + k) * P:(4 * q + k + 1) * P],
                                     w_v[:, :], start=True, stop=True)
                last.then_inc(v_full, 1)
                if q == 1:
                    output(T - 1)
            turn_x1(2)
            pe.wait_ge(v_free, 3)
            stay_warm(4, 5)
            for j in range(4):
                if j == 2:
                    turn_x1(3)
                pe.wait_ge(x1T_free, 2 + 2 * (j // 2))
                if j < 2:
                    pe.wait_ge(v_free, j + 3)
                else:
                    pe.wait_ge(o_free, T)
                for k in range(4):
                    t = 2 * (4 * (j % 2) + k) + j // 2
                    last = pe.transpose(ps[:, 4 + j, k * P:(k + 1) * P], x1T[:, t * P:(t + 1) * P], ident[:, :])
                last.then_inc(h0_full, 1)
            pe.wait_ge(v_free, 2)
            stay_warm(3, 20)

            def turn_slots(n, b):
                pe.wait_ge(sn_ready, n + 1)
                wait(pe, snh_ready, n)
                for t in range(2):
                    pe.transpose(ps[:, 0, t * P:(t + 1) * P], sn[:, b % 2, t, :], ident[:, :])
                for t in range(2):
                    last = pe.transpose(ps[:, 0, (2 + t) * P:(3 + t) * P], h[:, 2 * b + t, :], ident[:, :])
                last.then_inc(t12_full, 1)

            def score_slots(n, b):
                pe.wait_ge(snh_ready, n + 1)
                wait(pe, exB, n)
                for m in range(2):
                    last = pe.matmul(ps[:, 1, m * 256:(m + 1) * 256], kq[:, (2 * b + m) * P:(2 * b + m + 1) * P],
                                     snh[:, b % 4, 0:256], start=True, stop=True)
                last.then_inc(sB_full, 1)

            def update_slots(n, b):
                pe.wait_ge(vr_ready, n + 1)
                pe.wait_ge(exB, n + 1)
                wait(pe, upd_ready, n)
                for t in range(2):
                    for m in range(2):
                        last = pe.matmul(ps[:, 2, t * 256:t * 256 + D + 1], e_m[:, b % 2, m, t * P:(t + 1) * P],
                                         vr[:, b % 2, m, :], start=(m == 0), stop=(m == 1))
                last.then_inc(u_full, 1)

            def turn_updates(n, b):
                pe.wait_ge(upd_ready, n + 1)
                wait(pe, updT_ready, n)
                for t in range(2):
                    last = pe.transpose(ps[:, 3, t * P:(t + 1) * P], upd[:, b % 2, t, :], ident[:, :])
                last.then_inc(t3_full, 1)

            def gates(n, b):
                pe.wait_ge(updT_ready, n + 1)
                wait(pe, npre_ready, n - 1)
                for t in range(2):
                    bank = ps[:, 4 + 2 * (b % 2) + t, :]
                    pe.matmul(bank, ones_b[:, :], bias[:, :], start=True, stop=False)
                    pe.matmul(bank[:, 0:3 * D], updT[:, b % 2, t * P:(t + 1) * P], w_ih[:, :], start=False, stop=False)
                    last = pe.matmul(bank[:, D:4 * D], snh[:, b % 4, 256 + t * P:256 + (t + 1) * P], w_hh[:, :],
                                     start=False, stop=True)
                last.then_inc(g_full, 1)

            def step(n, k):
                if 0 <= k < BLOCKS:
                    turn_updates(n, k % 8)
                if 0 <= k + 2 < BLOCKS:
                    score_slots(n + 2, (k + 2) % 8)
                if 0 <= k + 1 < BLOCKS:
                    update_slots(n + 1, (k + 1) % 8)
                if 0 <= k + 3 < BLOCKS:
                    turn_slots(n + 3, (k + 3) % 8)
                if 0 <= k < BLOCKS:
                    gates(n, k % 8)

            pe.wait_ge(biases, 1)
            pe.wait_ge(h0_free, 4)
            for k in range(-3, 3):
                step(k, k)
            with pe.Fori(0, ITERS - 1) as it:
                for k in range(3, 11):
                    step(8 * it + k, k)
            for k in range(8 * (ITERS - 1) + 3, BLOCKS):
                step(k, k)

            def turn_x2(q):
                pe.wait_ge(x2_high if q >= 2 else x2_low, q % 2 + 1)
                for k in range(4):
                    last = pe.transpose(ps[:, q, k * P:(k + 1) * P], x2[:, 4 * q + k, :], ident[:, :])
                last.then_inc(x2T_full, 1)

            def logits(t0, t1, bank):
                pe.wait_ge(x2T_free, t1 // 4)
                for t in range(t0, t1):
                    last = pe.matmul(ps[:, bank, t * E:(t + 1) * E], x1T[:, t * P:(t + 1) * P], wg[:, :],
                                     start=True, stop=True)
                last.then_inc(lg_full, 1)

            for q in range(3):
                turn_x2(q)
            pe.wait_ge(npre_ready, BLOCKS - 1)
            logits(0, 12, 4)
            turn_x2(3)
            logits(12, T, 5)
            pe.wait_ge(npre_ready, BLOCKS)
            stay_warm(7, 4)
            pe.wait_ge(hot_ready, 1)
            hot_flat = hot[:, :, :].rearrange("p e q -> p (e q)")
            pe.matmul(ps[:, 6, 0:256], ones_b[:, :], hot_flat, start=True, stop=True)
            pe.matmul(ps[:, 7, 0:256], not_before[:, :], hot_flat, start=True, stop=True).then_inc(rank_full, 1)
            stay_warm(5, 12)
            pe.wait_ge(rows_a, 1)
            pe.wait_ge(rows_b, 1)
            for k in range(4):
                pe.wait_ge(lo_ready, k + 1)
                for q in range(k * QN // 4, (k + 1) * QN // 4):
                    last = pe.matmul(ps[:, 4, 0:2 * NT], hot_lo[:, q, :], rows_hi[:, q, :], start=(q == 0),
                                     stop=(q == QN - 1))
            last.then_inc(rows_full, 1)
            stay_warm(5, 28)

            def weights_table():
                pe.wait_ge(wts_ready, 1)
                for q in range(QN):
                    last = pe.matmul(ps[:, 6, 0:3 * NT], hot_lo[:, q, :], wts_hi[:, q, :], start=(q == 0),
                                     stop=(q == QN - 1))
                last.then_inc(wts_full, 1)

            def turn_expert(e):
                pe.wait_ge(ld_xe[e], 16 * CT)
                wait(pe, xeT_free, e)
                if e == 0:
                    pe.wait_ge(x2T_free, 4)
                for j in range(CT):
                    bank, col = divmod(j * P, 512)
                    last = pe.transpose(ps[:, bank, col:col + P], xe[:, e * CT + j, :], ident[:, :])
                last.then_inc(xeT_full, 1)

            def expand_expert(e):
                r = e % 2
                pe.wait_ge(we_split, e + 1)
                pe.wait_ge(xeT_free, e + 1)
                for f in range(FC):
                    wait(pe, gelu_done, FC * e + f - 1)
                    w = cfc_hi[:, r, f * P:(f + 1) * P], cfc_lo[:, r, f * P:(f + 1) * P]
                    for half in range(2):
                        cols = slice(half * CAP // 2, (half + 1) * CAP // 2)
                        last = exact(ps[:, 2 + 2 * (f % 2) + half, 0:CAP // 2], w, (xeT_hi[:, r, cols], xeT_lo[:, r, cols]))
                    last.then_inc(fc_full, 1)

            def reduce_expert(e):
                r = e % 2
                wait(pe, eo_ready, e)
                if e == 0:
                    pe.wait_ge(wts_kept, 1)
                for j in range(CT):
                    bank, col = divmod(j * P, 512)
                    for f in range(FC):
                        if j == 0:
                            pe.wait_ge(gelu_done, FC * e + f + 1)
                        last = pe.matmul(ps[:, 6 + bank, col:col + P], hT[:, r, f, j * P:(j + 1) * P], cpr[:, r, f, :],
                                         start=(f == 0), stop=(f == FC - 1))
                last.then_inc(pr_full, 1)

            def reduce_last(e):
                r = e % 2
                for j in range(CT):
                    if j == 0:
                        wait(pe, eo_ready, e)
                    for f in range(FC):
                        if j == 0:
                            pe.wait_ge(gelu_done, FC * e + f + 1)
                        last = pe.matmul(ps[:, LAST_BANKS[j], 0:P], hT[:, r, f, j * P:(j + 1) * P], cpr[:, r, f, :],
                                         start=(f == 0), stop=(f == FC - 1))
                    last.then_inc(tile_full, 1)

            turn_expert(0)
            for e in range(E):
                expand_expert(e)
                if e == 0:
                    weights_table()
                if e + 1 < E:
                    turn_expert(e + 1)
                    reduce_expert(e)
            reduce_last(E - 1)

        @block.vector
        def _(dve):
            links = [0]

            def link(ins, base=None):
                links[0] += 1
                ins.then_inc(dve_link, 1)
                dve.wait_ge(dve_link, links[0] if base is None else base + links[0])

            def rsqrt(base, a, y, t, guess=True, steps=3):
                if guess:
                    link(dve.tensor_scalar(t.bitcast(I32), a.bitcast(I32), 1, None, ALU.logical_shift_right), base)
                    link(dve.tensor_scalar(y.bitcast(I32), t.bitcast(I32), -1.0, float(0x5F3759DF), ALU.mult, ALU.add),
                         base)
                for _ in range(steps):
                    link(dve.tensor_tensor(t, y, y, ALU.mult), base)
                    link(dve.scalar_tensor_tensor(t, t, -0.5, a, ALU.mult, ALU.mult), base)
                    link(dve.scalar_tensor_tensor(y, t, 1.5, y, ALU.add, ALU.mult), base)

            def stats(g0, g1, src, eps):
                if src is not None:
                    for g in range(g0, g1):
                        last = dve.bn_stats(st[:, g, :], src[:, g, :])
                    link(last)
                if eps is None:
                    return
                for g in range(g0, g1):
                    last = dve.bn_aggr(mv[:, g, :], st[:, g, :])
                link(last)
                link(dve.tensor_scalar(var[:, g0:g1], mv[:, g0:g1, 1], eps, None, ALU.add))
                rsqrt(None, var[:, g0:g1], rs[:, g0:g1], rt[:, g0:g1])

            def normalise_in(sg):
                wait(dve, b0_full, b0_item(sg - 1, 1))
                for g in range(GL):
                    n = GL * sg + g
                    last = dve.tensor_scalar(xn[:, g, :], xg[:, n, :], mv[:, n, 0:1],
                                             rs[:, n:n + 1] if isinstance(n, int) else rs[:, bass.ds(n, 1)],
                                             ALU.subtract, ALU.mult)
                last.then_inc(xn_ready, 1)

            def split_turned(sg):
                dve.wait_ge(lnT_hi_ready, sg + 1)
                dve.tensor_tensor(lnT_lo[:, :], lnT, lnT_hi[:, :].bitcast(F32), ALU.subtract).then_inc(lnT_split, 1)

            def split_wqkv(i):
                dve.wait_ge(w_hi_ready, i + 1)
                cols = slice(W_PIECES[i] * 512, W_PIECES[i] * 512 + 512)
                dve.tensor_tensor(w_lo[:, cols], wqkv[:, cols], w_hi[:, cols].bitcast(F32), ALU.subtract).then_inc(w_split, 1)

            def key_low(sg, hp):
                dve.wait_ge(b1_full, b1_item(sg, hp) + 1)
                dve.tensor_copy(kz[0:DH, hp, :, 0, :], ps[0:DH, b1_bank(hp), :].rearrange("p (g n) -> p g n", g=GL)
                                ).then_inc(b1_free_dve, 1)

            def value_high(sg, g):
                dve.wait_ge(b1_full, b1_item(sg, HP + g) + 1)
                dve.tensor_copy(v[:, g, 512:1024], ps[:, b1_bank(g), :]).then_inc(b1_free_dve, 1)

            def diagonal(n, g, base):
                dve.wait_ge(s_full0, n + 1)
                src = ps[:, 2:4, :].rearrange("p b (h k) -> p (b h) k", h=4)
                for q in range(4):
                    r = slice(QB * q, QB * q + QB)
                    last = dve.tensor_tensor(sc[r, g % 2, 0:8, :], src[r, :, QB * q:QB * q + QB],
                                             mask[r, :].unsqueeze(1).to_broadcast([QB, 8, QB]), ALU.add)
                last.then_inc(s_free0, 1)

            def mask_high(n, g, base):
                dve.wait_ge(s_free1, n + 1)
                hi = sc[:, g % 2, 8:16, :]
                link(dve.tensor_tensor(hi, hi, mask[:, :].unsqueeze(1).to_broadcast([P, 8, QB]), ALU.add), base)

            def shift(n, g, base):
                link(dve.tensor_reduce(mx[:, :], sc[:, g % 2, :, :], AX.X, ALU.max), base)
                dve.tensor_tensor(sc[:, g % 2, :, :], sc[:, g % 2, :, :],
                                  mx[:, :].unsqueeze(2).to_broadcast([P, H, QB]), ALU.subtract).then_inc(shifted, 1)

            def divide(n, g, base):
                dve.wait_ge(exped, n + 1)
                link(dve.tensor_reduce(sm[:, :], pc[:, g % 2, :, :], AX.X, ALU.add), base)
                link(dve.reciprocal(sm[:, :], sm[:, :]), base)
                link(dve.tensor_tensor(pc[:, g % 2, :, :], pc[:, g % 2, :, :],
                                       sm[:, :].unsqueeze(2).to_broadcast([P, H, QB]), ALU.mult), base)

            def turn_blocks(n, g, reuse):
                if reuse:
                    dve.wait_ge(spread, n - 1)
                dve.transpose(pt[:, g % 2, :, :].rearrange("p h k -> p (h k)"),
                              pc[:, g % 2, :, :].rearrange("p h k -> p (h k)")).then_inc(probs, 1)

            def context_high(n):
                dve.wait_ge(pv1, n + 1)
                dve.tensor_copy(ctxT[:, 4:8, :], ps[:, 7, :].rearrange("p (h n) -> p h n", h=4)).then_inc(ctx1, 1)

            def residual(n):
                dve.wait_ge(o_full, n + 1)
                row = xg[:, n, :]
                dve.tensor_tensor(row, row, ps[:, 7, 0:P], ALU.add).then_inc(o_free, 1)
                dve.wait_ge(o_free, n + 1)
                return dve.bn_stats(st[:, n, :], row)

            def context_scale(part):
                if part < 2:
                    for g in range(part * T // 2, (part + 1) * T // 2):
                        last = dve.bn_aggr(c_mv[:, g, :], c_st[:, g, :])
                    link(last)
                elif part == 2:
                    link(dve.tensor_tensor(c_var[:, :], c_mv[:, :, 0], c_mv[:, :, 0], ALU.mult))
                    link(dve.scalar_tensor_tensor(c_var[:, :], c_var[:, :], RMS_EPS, c_mv[:, :, 1], ALU.add, ALU.add))
                    rsqrt(None, c_var[:, :], c_r[:, :], c_rt[:, :], True, 1)
                else:
                    rsqrt(None, c_var[:, :], c_r[:, :], c_rt[:, :], False, 2)
                    dve.tensor_copy(c_rt[:, :], c_r[:, :]).then_inc(c_rs, 1)

            def supergroup(sg, first, final, base):
                for hp in range(HP):
                    key_low(sg, hp)
                    if first and hp in NEXT_PIECE:
                        split_wqkv(NEXT_PIECE[hp])
                    if first and hp < 6:
                        if hp == 0:
                            dve.wait_ge(ld_x_rest, 16 * (T - GL))
                        for g in (GL + 2 * hp, GL + 2 * hp + 1):
                            last = dve.bn_stats(st[:, g, :], xg[:, g, :])
                        link(last)
                    if not first:
                        if hp == 0:
                            residual(GL * sg - 3)
                        if hp == 2:
                            divide(GL * sg - 1, 3, base)
                        if hp == 3:
                            turn_blocks(GL * sg - 1, 3, True)
                    if final and hp >= 4:
                        context_scale(hp - 4)
                if first:
                    stats(GL, T, None, LN_EPS)
                else:
                    context_high(GL * sg - 2)
                diagonal(GL * sg, 0, base)
                mask_high(GL * sg, 0, base)
                if not first:
                    residual(GL * sg - 2)
                shift(GL * sg, 0, base)
                divide(GL * sg, 0, base)
                turn_blocks(GL * sg, 0, not first)
                if not first:
                    context_high(GL * sg - 1)
                diagonal(GL * sg + 1, 1, base)
                mask_high(GL * sg + 1, 1, base)
                if not first:
                    residual(GL * sg - 1)
                value_high(sg, 0)
                value_high(sg, 1)
                shift(GL * sg + 1, 1, base)
                value_high(sg, 2)
                value_high(sg, 3)
                divide(GL * sg + 1, 1, base)
                turn_blocks(GL * sg + 1, 1, not first)
                if not final:
                    normalise_in(sg + 1)
                context_high(GL * sg)
                if first:
                    dve.wait_ge(ld_ctx, 16)
                if not final:
                    for g in range(GL):
                        dve.bn_stats(c_st[:, GL * sg + g, :], ctx_t[:, GL * sg + g, :])
                diagonal(GL * sg + 2, 2, base)
                mask_high(GL * sg + 2, 2, base)
                residual(GL * sg)
                shift(GL * sg + 2, 2, base)
                divide(GL * sg + 2, 2, base)
                turn_blocks(GL * sg + 2, 2, True)
                if first:
                    for g in range(T - GL, T):
                        dve.bn_stats(c_st[:, g, :], ctx_t[:, g, :])
                if final:
                    dve.wait_ge(ld_in, 32)
                    dve.wait_ge(turned_w, 1)
                    dve.tensor_scalar(w_kq[:, :], ps[:, 0, 0:P], lnv[:, 3:4], None, ALU.mult).then_inc(w_done_dve, 1)
                    dve.tensor_scalar(w_v[:, :], ps[:, 0, P:2 * P], lnv[:, 3:4], None, ALU.mult).then_inc(w_done_dve, 1)
                    dve.tensor_copy(w_ih[:, D:3 * D], ps[:, 0, 2 * P:4 * P]).then_inc(w_done_dve, 1)
                context_high(GL * sg + 1)
                diagonal(GL * sg + 3, 3, base)
                if not final:
                    split_turned(sg + 1)
                mask_high(GL * sg + 3, 3, base)
                shift(GL * sg + 3, 3, base)

            dve.memset(kz[DH:P, :, :, 0, :], 0.0).then_inc(zeroed, 1)
            dve.wait_ge(ld_x, 16 * GL)
            stats(0, GL, xg, LN_EPS)
            normalise_in(0)
            split_wqkv(0)
            split_wqkv(1)
            dve.wait_ge(consts, 5)
            for q in range(4):
                last = dve.tensor_copy(mask[QB * q:QB * q + QB, :], full_mask[QB * q:QB * q + QB, QB * q:QB * q + QB])
            link(last)
            dve.wait_ge(consts, 14)
            dve.tensor_copy(iota_p[:, :], iota_pi[:, :])
            dve.tensor_copy(row_f[:, :], row_i[:, :])
            dve.tensor_copy(iota_e[:, :], iota_i[:, :])
            dve.memset(top[:, 2, :], NEG_INF)
            split_turned(0)
            dve.wait_ge(zeroed, 4)
            supergroup(0, True, False, None)
            done = links[0]
            PER = 5 * GL
            with dve.Fori(1, SG - 1) as sg:
                supergroup(sg, False, False, sg * PER - PER)
                assert links[0] - done == PER, links[0] - done
            links[0] = done + PER * (SG - 2)
            supergroup(SG - 1, False, True, None)
            residual(T - 3)
            divide(T - 1, 3, None)
            turn_blocks(T - 1, 3, True)
            context_high(T - 2)
            residual(T - 2)

            def first_norm(g0, g1):
                stats(g0, g1, None, OUT_EPS)
                for g in range(g0, g1):
                    last = dve.tensor_scalar(xg[:, g, :], xg[:, g, :], mv[:, g, 0:1], rs[:, g:g + 1],
                                             ALU.subtract, ALU.mult)
                    if g % 4 == 3:
                        last.then_inc(x1_ready, 1)

            first_norm(0, T - GL)
            context_high(T - 1)
            for q in range(4):
                dve.wait_ge(v_full, q + 1)
                dve.tensor_copy(vp[:, 4 * q:4 * q + 4, :], ps[:, 2 + q, :].rearrange("p (t d) -> p t d", t=4)
                                ).then_inc(v_free, 1)
                if q == 2:
                    link(residual(T - 1))
                    first_norm(T - GL, T)

            def squares(t, i):
                return dve.tensor_tensor_reduce(sq_out[:, i * D:i * D + D], h[:, t, :], h[:, t, :], 1.0, 0.0,
                                                ALU.mult, ALU.add, sq[:, t:t + 1])

            def slot_scale(t0, t1, base, first=True, last=True):
                if first:
                    link(dve.tensor_scalar(var[:, t0:t1], sq[:, t0:t1], 1.0 / D, RMS_EPS, ALU.mult, ALU.add), base)
                    rsqrt(base, var[:, t0:t1], r_h[:, t0:t1], rt[:, t0:t1], True, 1)
                if last:
                    rsqrt(base, var[:, t0:t1], r_h[:, t0:t1], rt[:, t0:t1], False, 2)

            def normalise_slots(n, b):
                wait(dve, t12_full, n - 1)
                dve.tensor_tensor(sn[:, b % 2, :, :], h[:, 2 * b:2 * b + 2, :],
                                  r_h[:, 2 * b:2 * b + 2].unsqueeze(2).to_broadcast([P, 2, D]), ALU.mult
                                  ).then_inc(sn_ready, 1)

            def maxima(n, b):
                dve.wait_ge(sB_full, n + 1)
                wait(dve, exB, n - 1)
                dve.tensor_reduce(n_mx[:, b % 2, :], ps[:, 1, :].rearrange("p (m k) -> p m k", m=2), AX.X, ALU.max,
                                  negate=True).then_inc(negmax, 1)

            def scale_values(n, b, base):
                dve.wait_ge(exB, n + 1)
                wait(dve, u_full, n - 1)
                link(dve.reciprocal(vr[:, b % 2, :, D:D + 1], den[:, b % 2, :].unsqueeze(2)), base)
                dve.tensor_tensor(vr[:, b % 2, :, 0:D], vp[:, 2 * b:2 * b + 2, :],
                                  vr[:, b % 2, :, D:D + 1].to_broadcast([P, 2, D]), ALU.mult).then_inc(vr_ready, 1)

            def scale_updates(n, b, base):
                dve.wait_ge(u_full, n + 1)
                wait(dve, t3_full, n - 1)
                u = ps[:, 2, :].rearrange("p (t d) -> p t d", t=2)
                link(dve.tensor_scalar(r_sum[:, :], u[:, :, D], SUM_EPS, None, ALU.add), base)
                link(dve.reciprocal(r_sum[:, :], r_sum[:, :]), base)
                dve.tensor_tensor(upd[:, b % 2, :, :], u[:, :, 0:D], r_sum[:, :].unsqueeze(2).to_broadcast([P, 2, D]),
                                  ALU.mult).then_inc(upd_ready, 1)

            def candidate(n, b, base):
                dve.wait_ge(rz_ready, n + 1)
                g = ps[:, 4 + 2 * (b % 2):6 + 2 * (b % 2), :]
                link(dve.scalar_tensor_tensor(tmp, trz[:, b % 2, :, 0:D], 1.0, g[:, :, 3 * D:4 * D], ALU.add, ALU.mult), base)
                dve.scalar_tensor_tensor(new[:, b % 2, :, :], tmp, 0.5, g[:, :, 0:D], ALU.mult, ALU.add
                                         ).then_inc(npre_ready, 1)

            def blend(n, b, base):
                dve.wait_ge(new_ready, n + 1)
                hb = h[:, 2 * b:2 * b + 2, :]
                nb = new[:, b % 2, :, :]
                link(dve.tensor_tensor(tmp2, hb, nb, ALU.subtract), base)
                link(dve.scalar_tensor_tensor(tmp2, trz[:, b % 2, :, D:2 * D], 1.0, tmp2, ALU.add, ALU.mult), base)
                dve.scalar_tensor_tensor(hb, tmp2, 0.5, nb, ALU.mult, ALU.add).then_inc(h_ready, 1)

            def step(n, k, base):
                if 0 <= k - 1:
                    candidate(n - 1, (k - 1) % 8, base)
                if 0 <= k + 2 < BLOCKS:
                    maxima(n + 2, (k + 2) % 8)
                if k == 1:
                    dve.wait_ge(x1n_ready, 4)
                if 0 <= k - 1:
                    blend(n - 1, (k - 1) % 8, base)
                if 0 <= k + 1 < BLOCKS:
                    scale_updates(n + 1, (k + 1) % 8, base)
                if 0 <= k + 2 < BLOCKS:
                    scale_values(n + 2, (k + 2) % 8, base)
                j = (k - 1) % 8
                if 0 <= k - 1 < BLOCKS - 8 and j in (2, 3, 5, 6, 7):
                    group = (0, 6) if j < 5 else (6, 12) if j < 7 else (12, 16)
                    if j in (2, 5, 7):
                        dve.wait_ge(sq_ready, n)
                    slot_scale(*group, base, j in (2, 5, 7), j in (3, 6))
                if j == 0 and 8 <= k - 1 <= BLOCKS - 8:
                    slot_scale(12, 16, base, False, True)
                if 0 <= k + 4 < BLOCKS:
                    normalise_slots(n + 4, (k + 4) % 8)
                if isinstance(n, int) and n >= BLOCKS - 5:
                    second_stats(n)

            def tiles_stats(t0, t1):
                for t in range(t0, t1):
                    last = dve.bn_stats(st[:, t, :], h[:, t, :])
                link(last)

            def second_norm(t0, t1):
                for t in range(t0, t1):
                    last = dve.tensor_scalar(x2[:, t, :], h[:, t, :], mv[:, t, 0:1], rs[:, t:t + 1],
                                             ALU.subtract, ALU.mult)
                last.then_inc(x2_high, 1)

            def second_stats(n):
                b = n - (BLOCKS - 7)
                if b in (2, 3, 4, 5, 6):
                    dve.wait_ge(sum_ready, b + 1)
                    tiles_stats(0 if b == 2 else 2 * b, 2 * b + 2)
                if b in (3, 5):
                    t0, t1 = (0, 8) if b == 3 else (8, 12)
                    for t in range(t0, t1):
                        last = dve.bn_aggr(mv[:, t, :], st[:, t, :])
                    link(last)
                    link(dve.tensor_scalar(var[:, t0:t1], mv[:, t0:t1, 1], OUT_EPS, None, ALU.add))
                    rsqrt(None, var[:, t0:t1], rs[:, t0:t1], rt[:, t0:t1], True, 1)
                if b in (4, 6):
                    t0, t1 = (0, 8) if b == 4 else (8, 12)
                    rsqrt(None, var[:, t0:t1], rs[:, t0:t1], rt[:, t0:t1], False, 2)
                    if b == 4:
                        dve.tensor_copy(rt[:, 0:8], rs[:, 0:8]).then_inc(x2_scale, 1)
                    else:
                        second_norm(8, 12)

            for j in range(4):
                dve.wait_ge(h0_free, j + 1)
                for i in range(4):
                    last = squares(8 * (j % 2) + 2 * i + j // 2, 4 * (j % 2) + i)
                if j % 2 == 1:
                    link(last)
            slot_scale(0, T, None)
            for k in range(-4, 3):
                step(k, k, None)
            done = links[0]
            PER_IT = 8 * (2 + 2 + 1 + 1) + 3 * 12
            with dve.Fori(0, ITERS - 1) as it:
                for k in range(3, 11):
                    step(8 * it + k, k, it * PER_IT)
                assert links[0] - done == PER_IT, links[0] - done
            links[0] = done + PER_IT * (ITERS - 1)
            for k in range(8 * (ITERS - 1) + 3, BLOCKS + 1):
                step(k, k, None)

            def split_weights(pair, r, e):
                dve.wait_ge(ld_we[r], 32 * pair + 32)
                wait(dve, pr_full, e - 1)
                dve.tensor_copy(cfc_hi[:, r, :], cfc[:, r, :]).then_inc(we_hi, 1)
                dve.wait_ge(we_hi, e + 1)
                dve.tensor_tensor(cfc_lo[:, r, :], cfc[:, r, :], cfc_hi[:, r, :].bitcast(F32), ALU.subtract).then_inc(we_split, 1)

            dve.wait_ge(h_ready, BLOCKS)
            link(dve.tensor_tensor(h[:, 14:16, :], h[:, 14:16, :], x1n[:, 14:16, :], ALU.add))
            stats(14, 16, h, None)
            stats(12, 16, None, OUT_EPS)
            second_norm(12, 16)

            def top_two(t0, t1, bank, count):
                dve.wait_ge(lg_full, count)
                link(dve.tensor_copy(lg[:, t0:t1, :], ps[:, bank, t0 * E:t1 * E].rearrange("p (t e) -> p t e", e=E)))
                for t in range(t0, t1):
                    last = dve.max(v8[:, t, :], lg[:, t, :])
                link(last)
                for t in range(t0, t1):
                    last = dve.max_index(i8[:, t, :], v8[:, t, :], lg[:, t, :])
                link(last)

            top_two(0, 12, 4, 1)
            top_two(12, T, 5, 2)
            link(dve.tensor_copy(pick[:, :, :], i8[:, :, 0:TOPK].rearrange("p t k -> p k t")))
            pick_flat = pick[:, :, :].rearrange("p k t -> p (k t)")
            dve.tensor_tensor(hot[:, :, :], pick_flat.unsqueeze(1).to_broadcast([P, E, QN]),
                              iota_e[:, :].unsqueeze(2).to_broadcast([P, E, QN]), ALU.is_equal).then_inc(hot_ready, 1)
            link(dve.tensor_copy(top[:, 0:2, :], v8[:, :, 0:TOPK].rearrange("p t k -> p k t")))
            link(dve.tensor_tensor(top_m[:, :], top[:, 0, :], top[:, 2, :], ALU.max))
            dve.tensor_tensor(top[:, :, :], top[:, :, :], top_m[:, :].unsqueeze(1).to_broadcast([P, 3, T]), ALU.subtract
                              ).then_inc(top_ready, 1)
            dve.wait_ge(rank_full, 1)
            link(dve.tensor_tensor_scan(incl[:, :], seg[:, :, :].rearrange("p e q -> p (e q)"), ps[:, 6, 0:E * QN], 0.0,
                                        ALU.mult, ALU.add))
            link(dve.tensor_tensor(incl[:, :], incl[:, :], ps[:, 7, 0:E * QN], ALU.add))
            link(dve.tensor_tensor(incl[:, :], incl[:, :], hot[:, :, :].rearrange("p e q -> p (e q)"), ALU.mult))
            link(dve.tensor_reduce(slot[:, :], incl[:, :].rearrange("p (e q) -> p q e", e=E), AX.X, ALU.add))
            dve.tensor_scalar(over[:, :], slot[:, :], float(CAP), float(NOWHERE), ALU.is_ge, ALU.mult)
            link(dve.scalar_tensor_tensor(wt[:, :], pick_flat, float(CAP), slot[:, :], ALU.mult, ALU.add))
            link(dve.tensor_tensor(slot_i[:, :], wt[:, :], over[:, :], ALU.add))
            dve.tensor_scalar(slot_hi[:, :], slot_i[:, :], P.bit_length() - 1, None, ALU.logical_shift_right)
            link(dve.tensor_scalar(slot_lo[:, :], slot_i[:, :], P - 1, None, ALU.bitwise_and))
            dve.tensor_copy(hi_f[:, :], slot_hi[:, :])
            link(dve.tensor_copy(lo_f[:, :], slot_lo[:, :]))
            dve.tensor_tensor(tile_hot, hi_f[:, :].unsqueeze(2).to_broadcast([P, QN, NT]),
                              iota_p[:, 0:NT].unsqueeze(1).to_broadcast([P, QN, NT]), ALU.is_equal).then_inc(hi_ready, 1)
            for k in range(4):
                part_k = slice(k * QN // 4, (k + 1) * QN // 4)
                dve.tensor_tensor(hot_lo[:, part_k, :], lo_f[:, part_k].unsqueeze(2).to_broadcast([P, QN // 4, P]),
                                  iota_p[:, :].unsqueeze(1).to_broadcast([P, QN // 4, P]), ALU.is_equal).then_inc(lo_ready, 1)
            dve.wait_ge(rows_full, 1)
            link(dve.tensor_reduce(t_row[:, :], ps[:, 4, 0:2 * NT].rearrange("p (g n) -> p n g", g=2), AX.X, ALU.add))
            link(dve.tensor_scalar(t_tmp[:, :], t_row[:, :], float(N), -float(N), ALU.is_gt, ALU.mult))
            link(dve.scalar_tensor_tensor(t_tmp[:, :], t_row[:, :], -1.0, t_tmp[:, :], ALU.add, ALU.add))
            dve.tensor_scalar(t_src[:, :], t_tmp[:, :], 0.0, None, ALU.max).then_inc(src_ready, 1)
            dve.wait_ge(src_ready, 1)
            link(dve.tensor_scalar(t_tmp[:, :], t_row[:, :], 0.5, float(NOWHERE), ALU.is_lt, ALU.mult))
            dve.scalar_tensor_tensor(t_dst[:, :], t_row[:, :], -1.0, t_tmp[:, :], ALU.add, ALU.add).then_inc(dst_ready, 1)
            split_weights(0, 0, 0)
            dve.tensor_scalar(keep[:, :], slot[:, :], float(CAP), None, ALU.is_lt)
            dve.wait_ge(expt_ready, 1)
            link(dve.scalar_tensor_tensor(top_m[:, :], expt[:, 2, :], float(E - TOPK), expt[:, 0, :], ALU.mult, ALU.add))
            link(dve.tensor_tensor(top_m[:, :], top_m[:, :], expt[:, 1, :], ALU.add))
            link(dve.reciprocal(top_m[:, :], top_m[:, :]))
            link(dve.tensor_tensor(prob[:, :, :], expt[:, 0:2, :], top_m[:, :].unsqueeze(1).to_broadcast([P, TOPK, T]), ALU.mult))
            link(dve.tensor_tensor(wt[:, :], prob[:, :, :].rearrange("p k t -> p (k t)"), keep[:, :], ALU.mult))
            for k in range(3):
                link(dve.tensor_copy(w_cut[:, k, :], wt[:, :]))
                if k < 2:
                    link(dve.tensor_tensor(wt[:, :], wt[:, :], w_cut[:, k, :], ALU.subtract))
                last = dve.tensor_tensor(wts_hi[:, :, k * NT:(k + 1) * NT], tile_hot,
                                         w_cut[:, k, :].unsqueeze(2).to_broadcast([P, QN, NT]), ALU.mult)
            last.then_inc(wts_ready, 1)

            def keep_weights():
                dve.wait_ge(wts_full, 1)
                dve.tensor_reduce(t_wt[:, :], ps[:, 6, 0:3 * NT].rearrange("p (g n) -> p n g", g=3), AX.X, ALU.add
                                  ).then_inc(wts_kept, 1)
                dve.wait_ge(wts_kept, 1)

            def take_batch(e, r):
                dve.wait_ge(xeT_full, e + 1)
                src = ps[:, 0:2, :].rearrange("p b n -> p (b n)")[:, 0:CAP]
                dve.tensor_copy(xeT_hi[:, r, :], src).then_inc(xeT_kept, 1)
                dve.wait_ge(xeT_kept, e + 1)
                dve.tensor_tensor(xeT_lo[:, r, :], src, xeT_hi[:, r, :].bitcast(F32), ALU.subtract).then_inc(xeT_free, 1)

            def weigh_output(pair, e, r, reuse):
                dve.wait_ge(pr_full, e + 1)
                if reuse:
                    dve.wait_ge(returned[r], 16 * CT * pair)
                src = ps[:, 6:8, :].rearrange("p b n -> p (b n)")[:, 0:CAP].rearrange("p (j d) -> p j d", j=CT)
                w = t_wt[:, e * CT:(e + 1) * CT] if isinstance(e, int) else t_wt[:, bass.ds(e * CT, CT)]
                dve.tensor_tensor(eo[:, r, :, :], src, w.unsqueeze(2).to_broadcast([P, CT, D]), ALU.mult
                                  ).then_inc(eo_ready, 1)

            def weigh_last(pair, e, r):
                dve.wait_ge(returned[r], 16 * CT * pair)
                for j in range(CT):
                    c = e * CT + j
                    dve.wait_ge(tile_full, j + 1)
                    dve.tensor_scalar(eo[:, r, j, :], ps[:, LAST_BANKS[j], 0:P], t_wt[:, c:c + 1], None, ALU.mult
                                      ).then_inc(tile_ready, 1)

            def experts(pair, reuse, final):
                for r in range(2):
                    e = 2 * pair + r
                    if final and r == 1:
                        weigh_last(pair, e, r)
                    else:
                        take_batch(e + 1, 1 - r)
                        split_weights(pair + r, 1 - r, e + 1)
                        weigh_output(pair, e, r, reuse)

            take_batch(0, 0)
            keep_weights()
            experts(0, False, False)
            with dve.Fori(1, E // 2 - 1) as pair:
                experts(pair, True, False)
            experts(E // 2 - 1, True, True)
            for q in range(4):
                g0, g1 = 4 * q, 4 * q + 4
                dve.wait_ge(halves_added, q + 1)
                link(dve.tensor_tensor(h[:, g0:g1, :], xg[:, g0:g1, :], x2[:, g0:g1, :], ALU.add))
                for t in range(g0, g1):
                    last = dve.bn_stats(st[:, t, :], h[:, t, :])
            link(last)
            stats(0, T, None, OUT_EPS)
            dve.scalar_tensor_tensor(rt[:, 0:8], mv[:, 0:8, 0], -1.0, rs[:, 0:8], ALU.mult, ALU.mult).then_inc(y_sums, 1)
            for t in range(8, T):
                last = dve.tensor_scalar(h[:, t, :], h[:, t, :], mv[:, t, 0:1], rs[:, t:t + 1], ALU.subtract, ALU.mult)
                if t % 4 == 3:
                    last.then_inc(y_ready, 1)

        @block.scalar
        def _(act):
            def turned(sg):
                act.wait_ge(b0_full, b0_item(sg, 0) + 1)
                act.activation(lnT, ps[:, 0, :], ACT.Identity, bias=lnv[:, 1:2], scale=lnv[:, 0:1]
                               ).then_inc(b0_free, 1)

            def round_turned(sg):
                act.wait_ge(b0_free, b0_item(sg, 1))
                act.activation(lnT_hi[:, :], lnT, ACT.Copy).then_inc(lnT_hi_ready, 1)

            def round_wqkv(i):
                cols = slice(W_PIECES[i] * 512, W_PIECES[i] * 512 + 512)
                act.wait_ge(ld_w[i // 2], 32)
                act.activation(w_hi[:, cols], wqkv[:, cols], ACT.Copy).then_inc(w_hi_ready, 1)

            def query(sg, hp):
                act.wait_ge(b0_full, b0_item(sg, 1 + hp) + 1)
                act.activation(qT[:, hp, :], ps[:, query_bank(hp), :], ACT.Copy).then_inc(b0_free, 1)

            def key_high(sg, hp):
                act.wait_ge(b1_full, b1_item(sg, hp) + 1)
                act.activation(kz[DH:P, hp, :, 1, :], ps[DH:P, b1_bank(hp), :].rearrange("p (g n) -> p g n", g=GL), ACT.Copy
                               ).then_inc(b1_free_act, 1)

            def value_low(sg, g):
                act.wait_ge(b0_full, b0_item(sg, 1 + HP + g) + 1)
                act.activation(v[:, g, 0:512], ps[:, value_bank(g), :], ACT.Copy).then_inc(b0_free, 1)

            def diagonal(n, g, reuse):
                act.wait_ge(s_full1, n + 1)
                if reuse:
                    act.wait_ge(shifted, n - 1)
                src = ps[:, 4:6, :].rearrange("p b (h k) -> p (b h) k", h=4)
                for q in range(4):
                    r = slice(QB * q, QB * q + QB)
                    last = act.activation(sc[r, g % 2, 8:16, :], src[r, :, QB * q:QB * q + QB], ACT.Copy)
                last.then_inc(s_free1, 1)

            def exponent(n, g, reuse):
                act.wait_ge(shifted, n + 1)
                if reuse:
                    act.wait_ge(probs, n - 1)
                act.activation(pc[:, g % 2, :, :], sc[:, g % 2, :, :], ACT.Exp, scale=float(DH) ** -0.5
                               ).then_inc(exped, 1)

            def expand(n, g, reuse, quadrants=range(4)):
                act.wait_ge(probs, n + 1)
                if reuse:
                    act.wait_ge(pv1, n - 1)
                for q in quadrants:
                    r = slice(QB * q, QB * q + QB)
                    last = act.activation(pbd[r, g % 2, :, QB * q:QB * q + QB], pt[r, g % 2, :, :], ACT.Copy)
                if 3 in quadrants:
                    last.then_inc(spread, 1)

            def context_low(n):
                act.wait_ge(pv0, n + 1)
                act.activation(ctxT[:, 0:4, :], ps[:, 6, :].rearrange("p (h n) -> p h n", h=4), ACT.Copy
                               ).then_inc(ctx0, 1)

            def supergroup(sg, first, final):
                for hp in range(HP):
                    query(sg, hp)
                    key_high(sg, hp)
                    if not first:
                        if hp == 1:
                            exponent(GL * sg - 1, 3, True)
                    elif hp in NEXT_PIECE:
                        round_wqkv(NEXT_PIECE[hp])
                if not first:
                    expand(GL * sg - 1, 3, True)
                    context_low(GL * sg - 2)
                diagonal(GL * sg, 0, not first)
                exponent(GL * sg, 0, not first)
                if not first:
                    context_low(GL * sg - 1)
                diagonal(GL * sg + 1, 1, not first)
                value_low(sg, 0)
                expand(GL * sg, 0, not first)
                value_low(sg, 1)
                exponent(GL * sg + 1, 1, not first)
                value_low(sg, 2)
                value_low(sg, 3)
                context_low(GL * sg)
                expand(GL * sg + 1, 1, not first)
                diagonal(GL * sg + 2, 2, True)
                if not final:
                    turned(sg + 1)
                exponent(GL * sg + 2, 2, True)
                if not final:
                    round_turned(sg + 1)
                context_low(GL * sg + 1)
                expand(GL * sg + 2, 2, True)
                if final:
                    act.wait_ge(turned_w, 2)
                    act.activation(w_ih[:, 0:D], ps[:, 1, 0:P], ACT.Copy).then_inc(w_done_act, 1)
                    act.activation(w_hh[:, :], ps[:, 1, P:4 * P], ACT.Copy).then_inc(w_done_act, 1)
                diagonal(GL * sg + 3, 3, True)

            act.dma_start(lnv[:, 2:3], slot_w.rearrange("(p a) -> p a", a=1)).then_inc(ld_in, 16)
            act.dma_start(lnv[:, 3:4], input_w.rearrange("(p a) -> p a", a=1)).then_inc(ld_in, 16)
            act.dma_start(lnv[:, 0:1], ln_scale.rearrange("(p a) -> p a", a=1)).then_inc(ld_vec, 16)
            act.dma_start(lnv[:, 1:2], ln_bias.rearrange("(p a) -> p a", a=1)).then_inc(ld_vec, 16)
            act.wait_ge(ld_in, 32)
            act.activation(lnv[:, 4:5], lnv[:, 2:3], ACT.Copy, scale=float(D) ** -0.5).then_inc(w_done_act, 1)
            act.wait_ge(ld_vec, 32)
            round_wqkv(0)
            round_wqkv(1)
            turned(0)
            round_turned(0)
            act.wait_ge(zeroed, 4)
            supergroup(0, True, False)
            with act.Fori(1, SG - 1) as sg:
                supergroup(sg, False, False)
            supergroup(SG - 1, False, True)
            def keep_context(q):
                act.wait_ge(cT_full, q + 1)
                act.activation(cT[:, 512 * q:512 * q + 512], ps[:, q % 2, :], ACT.Copy).then_inc(cT_free, 1)

            exponent(T - 1, 3, True)
            keep_context(0)
            keep_context(1)
            context_low(T - 2)
            expand(T - 1, 3, True)
            keep_context(2)
            keep_context(3)
            act.wait_ge(w_done_act, 1)
            for q in range(4):
                act.wait_ge(kq_full, q + 1)
                act.activation(kq[:, 512 * q:512 * q + 512], ps[:, 2 + q, :], ACT.Copy, scale=lnv[:, 4:5]
                               ).then_inc(kq_free, 1)
            context_low(T - 1)
            act.wait_ge(v_full, 4)
            for q in range(4):
                act.wait_ge(x1T_full, q + 1)
                for g in range(4):
                    base = (4 * q + g) * 16
                    last = act.activation(x1T[:, :].rearrange("p (s b) -> p s b", s=S)[:, :, base:base + 16],
                                          ps[:, q % 2, g * P:(g + 1) * P].rearrange("p (l s) -> p s l", s=S), ACT.Copy)
                last.then_inc(x1T_free, 1)
                if q % 2 == 1:
                    for j in (q - 1, q):
                        act.wait_ge(h0_full, j + 1)
                        act.activation(quarter(h, j), ps[:, 4 + j, :].rearrange("p (t d) -> p t d", t=4), ACT.Copy
                                       ).then_inc(h0_free, 1)

            def keep_turned(n, b):
                act.wait_ge(t12_full, n + 1)
                act.activation(snh[:, b % 4, :], ps[:, 0, :], ACT.Copy).then_inc(snh_ready, 1)

            def exponents(n, b):
                act.wait_ge(negmax, n + 1)
                wait(act, u_full, n - 1)
                wait(act, vr_ready, n - 1)
                for m in range(2):
                    last = act.activation(e_m[:, b % 2, m, :], ps[:, 1, m * 256:(m + 1) * 256], ACT.Exp,
                                          bias=n_mx[:, b % 2, m:m + 1], accum_out=den[:, b % 2, m:m + 1])
                last.then_inc(exB, 1)

            def keep_updates(n, b):
                act.wait_ge(t3_full, n + 1)
                act.activation(updT[:, b % 2, :], ps[:, 3, 0:256], ACT.Copy).then_inc(updT_ready, 1)

            def half_tanh(n, b):
                act.wait_ge(g_full, n + 1)
                wait(act, h_ready, n - 1)
                act.activation(trz[:, b % 2, :, :], ps[:, 4 + 2 * (b % 2):6 + 2 * (b % 2), D:3 * D], ACT.Tanh, scale=0.5
                               ).then_inc(rz_ready, 1)

            def new_tanh(n, b):
                act.wait_ge(npre_ready, n + 1)
                act.activation(new[:, b % 2, :, :], new[:, b % 2, :, :], ACT.Tanh).then_inc(new_ready, 1)

            def squares(n, b):
                act.wait_ge(h_ready, n + 1)
                for t in range(2):
                    last = act.activation(sq_out[:, t * D:t * D + D], h[:, 2 * b + t, :], ACT.Square,
                                          accum_out=sq[:, 2 * b + t:2 * b + t + 1])
                last.then_inc(sq_ready, 1)

            def step(n, k):
                if 0 <= k < BLOCKS:
                    keep_updates(n, k % 8)
                if 0 <= k - 1:
                    half_tanh(n - 1, (k - 1) % 8)
                if 0 <= k - 1:
                    new_tanh(n - 1, (k - 1) % 8)
                if 0 <= k + 2 < BLOCKS:
                    exponents(n + 2, (k + 2) % 8)
                if 0 <= k + 3 < BLOCKS:
                    keep_turned(n + 3, (k + 3) % 8)
                if 0 <= k - 1 < BLOCKS - 8:
                    squares(n - 1, (k - 1) % 8)

            for k in range(-3, 3):
                step(k, k)
            with act.Fori(0, ITERS - 1) as it:
                for k in range(3, 11):
                    step(8 * it + k, k)
            for k in range(8 * (ITERS - 1) + 3, BLOCKS + 1):
                step(k, k)

            for q in range(4):
                act.wait_ge(x2T_full, q + 1)
                act.activation(x1T[:, 512 * q:512 * q + 512], ps[:, q, :], ACT.Copy).then_inc(x2T_free, 1)
            act.wait_ge(top_ready, 1)
            act.activation(expt[:, :, :], top[:, :, :], ACT.Exp).then_inc(expt_ready, 1)
            act.activation(lnv[:, 5:6], lnv[:, 0:1], ACT.Gelu)
            act.wait_ge(hi_ready, 1)
            act.activation(rows_hi[:, :, NT:2 * NT], tile_hot, ACT.Copy, scale=row_f[:, QN:QN + 1]).then_inc(rows_b, 1)

            def gelu(pair, r, e):
                for f in range(FC):
                    act.wait_ge(fc_full, FC * e + f + 1)
                    wait(act, pr_full, e - 1)
                    b0 = 2 + 2 * (f % 2)
                    act.activation(hT[:, r, f, :].rearrange("p (b n) -> p b n", b=2), ps[:, b0:b0 + 2, 0:CAP // 2], ACT.Gelu
                                   ).then_inc(gelu_done, 1)

            def experts(pair):
                for r in range(2):
                    gelu(pair, r, 2 * pair + r)

            experts(0)
            with act.Fori(1, E // 2) as pair:
                experts(pair)
            act.wait_ge(y_sums, 1)
            for t in range(6):
                last = act.activation(h[:, t, :], h[:, t, :], ACT.Identity, bias=rt[:, t:t + 1], scale=rs[:, t:t + 1])
                if t in (3, 5):
                    last.then_inc(y_act, 1)


_INS = ['x', 'ctx_1024', 'L0_attn_ln_scale', 'L0_attn_ln_bias', 'L0_attn_qkv_kernel', 'L0_attn_out_kernel',
        'L0_xattn_Wq', 'L0_xattn_Wk', 'L0_xattn_Wv', 'L0_xattn_gru_wih', 'L0_xattn_gru_whh', 'L0_xattn_gru_bih',
        'L0_xattn_gru_bhh', 'L0_xattn_slot_norm_w', 'L0_xattn_input_norm_w', 'L0_ffn_w_g', 'L0_ffn_c_fc',
        'L0_ffn_c_proj']


def kernel(**inputs):
    import numpy as np
    import concourse.bacc as bacc
    from concourse.bass_utils import run_bass_kernel_spmd

    nc = bacc.Bacc("TRN2", target_bir_lowering=False, num_devices=1)
    arrays, args = {}, []
    for name in _INS:
        a = np.ascontiguousarray(inputs[name])
        arrays[f"in_{name}"] = a
        args.append(nc.dram_tensor(f"in_{name}", a.shape, mybir.dt.from_np(a.dtype), kind="ExternalInput").ap())
    args.append(nc.dram_tensor("out", (S, B, D), F32, kind="ExternalOutput").ap())
    build(nc, *args)
    r = run_bass_kernel_spmd(nc, [arrays], core_ids=[0])
    return r.results[0]["out"]
```
